# Optimizing a Trainium2 kernel written in Bass

```python
import numpy as np
import jax
import jax.numpy as jnp

def _softmax(x, axis=-1):
    return jax.nn.softmax(x, axis=axis)

def _gelu(x):
    return jax.nn.gelu(x, approximate=True)

def _silu(x):
    return jax.nn.silu(x)

def _sigmoid(x):
    return jax.nn.sigmoid(x)

def _layernorm(x, axis=-1, eps=1e-05):
    m = jnp.mean(x, axis=axis, keepdims=True)
    v = jnp.var(x, axis=axis, keepdims=True)
    return (x - m) / jnp.sqrt(v + eps)

def _scatter_add(tgt, idx, src, axis=0):
    return tgt.at[idx].add(src)

def _segment_sum(src, seg, n):
    return jax.ops.segment_sum(src, seg, n)
kernel_name = 'mk_flamingo_gated_d2_seqx_r4_7e93fa'

def setup_inputs(seed: int=0):
    np.random.seed(seed)
    _w = jnp.asarray

    def _rec_inputs():
        import jax
        import jax.numpy as jnp
        _rk = jax.random.key(seed)
        x = 7.22e-05 + 1 * jax.random.normal(jax.random.fold_in(_rk, 1), (4, 1024, 256), jnp.float32)
        _lenS = 1024 - jax.random.randint(jax.random.fold_in(_rk, 7), (4,), 0, max(1, 1024 // 4) + 1, jnp.int32)
        _lenS2 = 154 - jax.random.randint(jax.random.fold_in(_rk, 8), (4,), 0, max(1, 154 // 4) + 1, jnp.int32)
        _ctx_1024P = jax.random.normal(jax.random.fold_in(_rk, 11), (4, 16, 256), jnp.float32)
        _ctx_1024c = jax.random.dirichlet(jax.random.fold_in(_rk, 511), 0.3 * jnp.ones((16,), jnp.float32), (4, 154))
        _ctx_1024t = jnp.einsum('bsk,bkd->bsd', _ctx_1024c, _ctx_1024P)
        _ctx_1024t = _ctx_1024t * jax.lax.rsqrt(jnp.mean(jnp.square(_ctx_1024t)) + 1e-12) * 0.953939
        ctx_1024 = 4.13588e-05 + 0.999923 * (_ctx_1024t + 0.3 * jax.random.normal(jax.random.fold_in(_rk, 611), (4, 154, 256), jnp.float32))
        _g = jax.random.normal(jax.random.fold_in(_rk, 9001), (2, 2), jnp.float32)
        _g = jnp.sign(_g) * jnp.maximum(jnp.abs(_g), 1.0) + (_g == 0) * 1.0
        g_xattn = _g[0]
        g_ffn = _g[1]
        return (x, ctx_1024, g_xattn, g_ffn)
    x, ctx_1024, g_xattn, g_ffn = _rec_inputs()

    def _L0_xattn_setup():
        import jax, jax.numpy as jnp
        import numpy as np
        B, SQ, SKV, E, H = (4, 512, 512, 256, 16)
        HD = E // H

        def stablemax(x):
            s = jnp.where(x >= 0, x + 1.0, 1.0 / (1.0 - x))
            return s / jnp.sum(s, axis=-1, keepdims=True)
        key = jax.random.key(seed)
        ks = jax.random.split(key, 6)
        scale = 1.0 / np.sqrt(E)
        return {'query': jax.random.normal(ks[0], (B, SQ, E), jnp.float32), 'key_value': jax.random.normal(ks[1], (B, SKV, E), jnp.float32), 'Wq': jax.random.normal(ks[2], (E, E), jnp.float32) * scale, 'bq': jnp.zeros((E,), jnp.float32), 'Wk': jax.random.normal(ks[3], (E, E), jnp.float32) * scale, 'bk': jnp.zeros((E,), jnp.float32), 'Wv': jax.random.normal(ks[4], (E, E), jnp.float32) * scale, 'bv': jnp.zeros((E,), jnp.float32), 'Wo': jax.random.normal(ks[5], (E, E), jnp.float32) * scale, 'bo': jnp.zeros((E,), jnp.float32)}
    _L0_xattn_all = _L0_xattn_setup()
    _L0_xattn_in = {k: v for k, v in _L0_xattn_all.items() if k in ('Wq', 'bq', 'Wk', 'bk', 'Wv', 'bv', 'Wo', 'bo')}
    del _L0_xattn_all

    def _L0_ffn_setup():
        import jax, jax.numpy as jnp
        import numpy as np
        TOP_K = 8
        CAPACITY = 128

        def _silu(x):
            return x * jax.nn.sigmoid(x)
        key = jax.random.key(seed)
        ks = jax.random.split(key, 7)
        B, S, H, E, I, Is = (2, 256, 256, 64, 128, 512)
        s = 0.05
        return {'hidden_states': jax.random.normal(ks[0], (B, S, H), jnp.float32), 'gate_w': jax.random.normal(ks[1], (H, E), jnp.float32) * s, 'shared_gate_w': jax.random.normal(ks[2], (H, 1), jnp.float32) * s, 'shared_gate_up_w': jax.random.normal(ks[3], (H, 2 * Is), jnp.float32) * s, 'shared_down_w': jax.random.normal(ks[4], (Is, H), jnp.float32) * s, 'expert_gate_up_w': jax.random.normal(ks[5], (E, H, 2 * I), jnp.float32) * s, 'expert_down_w': jax.random.normal(ks[6], (E, I, H), jnp.float32) * s}
    _L0_ffn_all = _L0_ffn_setup()
    _L0_ffn_in = {k: v for k, v in _L0_ffn_all.items() if k in ('gate_w', 'shared_gate_w', 'shared_gate_up_w', 'shared_down_w', 'expert_gate_up_w', 'expert_down_w')}
    del _L0_ffn_all

    def _L1_xattn_setup():
        import jax, jax.numpy as jnp
        import numpy as np
        DIMS = 256
        HEADS = 16
        DEPTH = DIMS // HEADS

        def _split_heads(x):
            b, s, _ = x.shape
            return x.reshape(b, s, HEADS, DEPTH).transpose(0, 2, 1, 3)
        key = jax.random.key(seed)
        kq, kk, kv = jax.random.split(key, 3)
        B, S = (2, 512)
        q = jax.random.normal(kq, (B, S, DIMS), dtype=jnp.float32)
        k = jax.random.normal(kk, (B, S, DIMS), dtype=jnp.float32)
        v = jax.random.normal(kv, (B, S, DIMS), dtype=jnp.float32)
        return {'q': q, 'k': k, 'v': v}
    _L1_xattn_all = _L1_xattn_setup()
    _L1_xattn_in = {k: v for k, v in _L1_xattn_all.items() if k in ()}
    del _L1_xattn_all

    def _L1_ffn_setup():
        import jax, jax.numpy as jnp
        import numpy as np
        D_MODEL = 256
        EXPANSION = 4
        D_HIDDEN = D_MODEL * EXPANSION
        NUM_STAGES = int(np.log2(D_HIDDEN))

        def butterfly(y, weights, dim):
            lead = y.shape[:-1]
            for stage in range(weights.shape[0]):
                s = 2 ** stage
                nb = dim // (2 * s)
                yr = y.reshape(*lead, nb, 2, s)
                a = yr[..., 0, :]
                b = yr[..., 1, :]
                w = weights[stage].reshape(nb, s, 2, 2)
                na = w[..., 0, 0] * a + w[..., 0, 1] * b
                nb2 = w[..., 1, 0] * a + w[..., 1, 1] * b
                y = jnp.stack([na, nb2], axis=-2).reshape(*lead, dim)
            return y
        key = jax.random.key(seed)
        ks = jax.random.split(key, 6)
        B, S = (4, 512)
        x = jax.random.normal(ks[0], (B, S, D_MODEL), jnp.float32)
        W_exp = jax.random.normal(ks[1], (D_MODEL, D_HIDDEN), jnp.float32) * 0.02
        b_exp = jnp.zeros((D_HIDDEN,), jnp.float32)
        up_weights = jax.random.normal(ks[2], (NUM_STAGES, D_HIDDEN // 2, 2, 2), jnp.float32) * 0.02
        up_bias = jnp.zeros((D_HIDDEN,), jnp.float32)
        down_weights = jax.random.normal(ks[3], (NUM_STAGES, D_HIDDEN // 2, 2, 2), jnp.float32) * 0.02
        W_con = jax.random.normal(ks[4], (D_HIDDEN, D_MODEL), jnp.float32) * 0.02
        b_con = jnp.zeros((D_MODEL,), jnp.float32)
        down_bias = jnp.zeros((D_MODEL,), jnp.float32)
        return dict(x=x, W_exp=W_exp, b_exp=b_exp, up_weights=up_weights, up_bias=up_bias, down_weights=down_weights, W_con=W_con, b_con=b_con, down_bias=down_bias)
    _L1_ffn_all = _L1_ffn_setup()
    _L1_ffn_in = {k: v for k, v in _L1_ffn_all.items() if k in ('W_exp', 'b_exp', 'up_weights', 'up_bias', 'down_weights', 'W_con', 'b_con', 'down_bias')}
    del _L1_ffn_all
    return {'x': x, 'ctx_1024': ctx_1024, 'g_xattn': g_xattn, 'g_ffn': g_ffn, 'L0_xattn_Wq': _L0_xattn_in['Wq'], 'L0_xattn_bq': _L0_xattn_in['bq'], 'L0_xattn_Wk': _L0_xattn_in['Wk'], 'L0_xattn_bk': _L0_xattn_in['bk'], 'L0_xattn_Wv': _L0_xattn_in['Wv'], 'L0_xattn_bv': _L0_xattn_in['bv'], 'L0_xattn_Wo': _L0_xattn_in['Wo'], 'L0_xattn_bo': _L0_xattn_in['bo'], 'L0_ffn_gate_w': _L0_ffn_in['gate_w'], 'L0_ffn_shared_gate_w': _L0_ffn_in['shared_gate_w'], 'L0_ffn_shared_gate_up_w': _L0_ffn_in['shared_gate_up_w'], 'L0_ffn_shared_down_w': _L0_ffn_in['shared_down_w'], 'L0_ffn_expert_gate_up_w': _L0_ffn_in['expert_gate_up_w'], 'L0_ffn_expert_down_w': _L0_ffn_in['expert_down_w'], 'L1_ffn_W_exp': _L1_ffn_in['W_exp'], 'L1_ffn_b_exp': _L1_ffn_in['b_exp'], 'L1_ffn_up_weights': _L1_ffn_in['up_weights'], 'L1_ffn_up_bias': _L1_ffn_in['up_bias'], 'L1_ffn_down_weights': _L1_ffn_in['down_weights'], 'L1_ffn_W_con': _L1_ffn_in['W_con'], 'L1_ffn_b_con': _L1_ffn_in['b_con'], 'L1_ffn_down_bias': _L1_ffn_in['down_bias']}

def reference(x, ctx_1024, g_xattn, g_ffn, L0_xattn_Wq, L0_xattn_bq, L0_xattn_Wk, L0_xattn_bk, L0_xattn_Wv, L0_xattn_bv, L0_xattn_Wo, L0_xattn_bo, L0_ffn_gate_w, L0_ffn_shared_gate_w, L0_ffn_shared_gate_up_w, L0_ffn_shared_down_w, L0_ffn_expert_gate_up_w, L0_ffn_expert_down_w, L1_ffn_W_exp, L1_ffn_b_exp, L1_ffn_up_weights, L1_ffn_up_bias, L1_ffn_down_weights, L1_ffn_W_con, L1_ffn_b_con, L1_ffn_down_bias):
    import jax
    import jax.numpy as jnp

    def _L0_xattn_ref(query, key_value, Wq, bq, Wk, bk, Wv, bv, Wo, bo):
        import jax, jax.numpy as jnp
        import numpy as np
        B, SQ, SKV, E, H = (4, 512, 512, 256, 16)
        HD = E // H

        def stablemax(x):
            s = jnp.where(x >= 0, x + 1.0, 1.0 / (1.0 - x))
            return s / jnp.sum(s, axis=-1, keepdims=True)
        b = query.shape[0]
        q = query @ Wq.T + bq
        k = key_value @ Wk.T + bk
        v = key_value @ Wv.T + bv
        q = q.reshape(b, -1, H, HD).transpose(0, 2, 1, 3)
        k = k.reshape(b, -1, H, HD).transpose(0, 2, 1, 3)
        v = v.reshape(b, -1, H, HD).transpose(0, 2, 1, 3)
        scores = jnp.einsum('bhqd,bhkd->bhqk', q, k) / np.sqrt(HD).astype(np.float32)
        attn = stablemax(scores)
        context = jnp.einsum('bhqk,bhkd->bhqd', attn, v)
        context = context.transpose(0, 2, 1, 3).reshape(b, -1, E)
        return context @ Wo.T + bo

    def _L0_ffn_ref(hidden_states, gate_w, shared_gate_w, shared_gate_up_w, shared_down_w, expert_gate_up_w, expert_down_w):
        import jax, jax.numpy as jnp
        import numpy as np
        TOP_K = 8
        CAPACITY = 128

        def _silu(x):
            return x * jax.nn.sigmoid(x)
        B, S, H = hidden_states.shape
        x = hidden_states.reshape(-1, H)
        T = x.shape[0]
        E = gate_w.shape[1]
        Is = shared_gate_up_w.shape[1] // 2
        I = expert_gate_up_w.shape[2] // 2
        gu = x @ shared_gate_up_w
        shared = _silu(gu[:, :Is]) * gu[:, Is:] @ shared_down_w
        shared = shared * jax.nn.sigmoid(x @ shared_gate_w)
        logits = x @ gate_w
        probs = jax.nn.softmax(logits.astype(jnp.float32), axis=-1)
        w, idx = jax.lax.top_k(probs, TOP_K)
        w = (w / jnp.sum(w, axis=-1, keepdims=True)).astype(x.dtype)
        e_flat = idx.reshape(-1)
        w_flat = w.reshape(-1)
        A = e_flat.shape[0]
        tok = jnp.arange(A) // TOP_K
        onehot = jax.nn.one_hot(e_flat, E, dtype=jnp.int32)
        pos = jnp.take_along_axis(jnp.cumsum(onehot, axis=0) - 1, e_flat[:, None], axis=1)[:, 0]
        slot = jnp.minimum(pos, CAPACITY)
        buf = jnp.zeros((E, CAPACITY + 1, H), x.dtype).at[e_flat, slot].set(x[tok])
        gu_e = jnp.einsum('ech,ehf->ecf', buf, expert_gate_up_w)
        act = _silu(gu_e[..., :I]) * gu_e[..., I:]
        out_e = jnp.einsum('eci,eih->ech', act, expert_down_w)
        y = out_e[e_flat, slot] * w_flat[:, None]
        y = jnp.where((pos < CAPACITY)[:, None], y, jnp.zeros_like(y))
        y = y.reshape(T, TOP_K, H).sum(axis=1)
        return (y + shared).reshape(B, S, H)

    def _L1_xattn_ref(q, k, v):
        import jax, jax.numpy as jnp
        import numpy as np
        DIMS = 256
        HEADS = 16
        DEPTH = DIMS // HEADS

        def _split_heads(x):
            b, s, _ = x.shape
            return x.reshape(b, s, HEADS, DEPTH).transpose(0, 2, 1, 3)
        b, s, _ = q.shape
        qh = _split_heads(q)
        kh = _split_heads(k)
        vh = _split_heads(v)
        scores = jnp.einsum('bhqd,bhkd->bhqk', qh, kh)
        weights = jax.nn.softmax(scores, axis=-1)
        out = jnp.einsum('bhqk,bhkd->bhqd', weights, vh)
        out = out.transpose(0, 2, 1, 3).reshape(b, s, DIMS)
        return out

    def _L1_ffn_ref(x, W_exp, b_exp, up_weights, up_bias, down_weights, W_con, b_con, down_bias):
        import jax, jax.numpy as jnp
        import numpy as np
        D_MODEL = 256
        EXPANSION = 4
        D_HIDDEN = D_MODEL * EXPANSION
        NUM_STAGES = int(np.log2(D_HIDDEN))

        def butterfly(y, weights, dim):
            lead = y.shape[:-1]
            for stage in range(weights.shape[0]):
                s = 2 ** stage
                nb = dim // (2 * s)
                yr = y.reshape(*lead, nb, 2, s)
                a = yr[..., 0, :]
                b = yr[..., 1, :]
                w = weights[stage].reshape(nb, s, 2, 2)
                na = w[..., 0, 0] * a + w[..., 0, 1] * b
                nb2 = w[..., 1, 0] * a + w[..., 1, 1] * b
                y = jnp.stack([na, nb2], axis=-2).reshape(*lead, dim)
            return y
        h = jnp.einsum('bsd,dh->bsh', x, W_exp) + b_exp
        h = butterfly(h, up_weights, D_HIDDEN)
        h = jax.nn.gelu(h + up_bias, approximate=False)
        h = butterfly(h, down_weights, D_HIDDEN)
        y = jnp.einsum('bsh,hd->bsd', h, W_con) + b_con
        return y + down_bias
    x = x + jnp.tanh(g_xattn[0]) * _L0_xattn_ref(_layernorm(x, axis=-1), ctx_1024, L0_xattn_Wq, L0_xattn_bq, L0_xattn_Wk, L0_xattn_bk, L0_xattn_Wv, L0_xattn_bv, L0_xattn_Wo, L0_xattn_bo)
    x = x + jnp.tanh(g_ffn[0]) * _L0_ffn_ref(_layernorm(x, axis=-1), L0_ffn_gate_w, L0_ffn_shared_gate_w, L0_ffn_shared_gate_up_w, L0_ffn_shared_down_w, L0_ffn_expert_gate_up_w, L0_ffn_expert_down_w)
    x = x + jnp.tanh(g_xattn[1]) * _L1_xattn_ref(_layernorm(x, axis=-1), ctx_1024, ctx_1024)
    x = x + jnp.tanh(g_ffn[1]) * _L1_ffn_ref(_layernorm(x, axis=-1), L1_ffn_W_exp, L1_ffn_b_exp, L1_ffn_up_weights, L1_ffn_up_bias, L1_ffn_down_weights, L1_ffn_W_con, L1_ffn_b_con, L1_ffn_down_bias)
    return x

_drawn_inputs = setup_inputs


def setup_inputs(seed=0):
    import zlib

    import numpy as np

    out = dict(_drawn_inputs(seed))
    spreads = {'g_ffn': (-1.0, 0.6),
     'L0_xattn_bq': (0.0, 0.659),
     'L0_xattn_bk': (0.0, 2.0),
     'L0_xattn_bv': (0.0, 0.1),
     'L0_xattn_bo': (0.0, 0.1),
     'L1_ffn_b_exp': (0.0, 0.1),
     'L1_ffn_up_bias': (0.0, 0.1),
     'L1_ffn_b_con': (0.0, 0.1),
     'L1_ffn_down_bias': (0.0, 0.1)}
    factors = {}
    for name, (base, spread) in spreads.items():
        noise = np.random.default_rng([zlib.crc32(name.encode()), seed]).standard_normal(out[name].shape)
        drawn = base * np.exp(spread * noise) if base else spread * noise
        out[name] = jnp.asarray(drawn.astype(out[name].dtype))
    for name, factor in factors.items():
        out[name] = (out[name] * factor).astype(out[name].dtype)
    return out
```

```python
from collections import deque
from contextlib import ExitStack

import numpy as np

import concourse.bass as bass
from concourse import mybir

F32 = mybir.dt.float32
F32R = mybir.dt.float32r
BF16 = mybir.dt.bfloat16
I32 = mybir.dt.int32
U32 = mybir.dt.uint32
ALU = mybir.AluOpType
ACT = mybir.ActivationFunctionType
AX = mybir.AxisListType

P = 128
BATCH, SEQ, DIM = 4, 1024, 256
KEYS = 154
REST = KEYS - P
HEADS = 16
HD = DIM // HEADS
PAIRS = HEADS // 2
GROUPS = HEADS // 4
TOKENS = BATCH * SEQ
TILES = TOKENS // P
HALF = 512
HT = HALF // P
HALVES = TOKENS // HALF
CD = DIM // P
STACK = 96
NK = HEADS + PAIRS
EXPERTS, TOPK, CAP = 64, 8, 128
INNER, SHARED = 128, 512
HID = 1024
HB = HID // P
STAGES = 10
INSIDE = 7
EPS = 1e-5
ROW = DIM + EXPERTS
SUMS = 2
NA, NB = 8, 16
EG = 16


class Lane:

    def __init__(self, engine, sem):
        self.engine, self.sem, self.count, self.queue, self.passed = engine, sem, 0, [], {}

    def wait(self, *marks):
        for m in marks:
            if isinstance(m, list):
                self.wait(*m)
            elif m is not None:
                sem, value = m
                if self.passed.get(sem.name, 0) < value:
                    self.passed[sem.name] = value
                    self.queue.append((self.engine.wait_ge, (sem, value), {}, None, 0))

    def do(self, operation, *args, signal=True, **named):
        self.count += signal
        self.queue.append((operation, args, named, self.sem if signal else None, 1))
        return (self.sem, self.count) if signal else None

    def run(self):
        for operation, args, named, sem, by in self.queue:
            issued = operation(*args, **named)
            if sem is not None:
                issued.then_inc(sem, by)


class Dmas:

    def __init__(self, lane, sems):
        self.lane, self.sems, self.n = lane, sems, 0
        self.last = [None] * len(sems)

    def start(self, operation, *args, **named):
        k = self.n % len(self.sems)
        self.lane.wait(self.last[k])
        sem, value = self.sems[k], 16 * (self.n // len(self.sems) + 1)
        self.n += 1
        self.lane.queue.append((operation, args, named, sem, 16))
        self.last[k] = (sem, value)
        return self.last[k]

    def copy(self, out, in_):
        return self.start(self.lane.engine.dma_start, out, in_)


class Slot:

    def __init__(self, ap):
        self.ap, self.ready, self.free = ap, [], []


class Ring:
    def __init__(self, aps):
        self.slots, self.n = [Slot(a) for a in aps], 0

    def take(self, *writers):
        s = self.slots[self.n % len(self.slots)]
        self.n += 1
        assert s.free is not None, "its readers are not queued yet"
        for lane in writers:
            lane.wait(s.free)
        s.ready, s.free = [], None
        return s


class Background:

    def __init__(self):
        self.work = deque()

    def add(self, gen):
        self.work.append(gen)
        return gen

    def step(self, n=1):
        for _ in range(n):
            while self.work:
                try:
                    next(self.work[0])
                    break
                except StopIteration:
                    self.work.popleft()

    def finish(self, gen):
        while gen in self.work:
            self.step()

    def drain(self):
        while self.work:
            self.step()


def build(nc, D, out, stop=None):
    ctx = ExitStack()
    with ctx:
        sem = lambda name: ctx.enter_context(nc.semaphore(name))
        T, A, V, G, S = nc.tensor, nc.scalar, nc.vector, nc.gpsimd, nc.sync
        pe, act, dve, pool, sp = (Lane(n, sem(f"ends_{w}")) for n, w in
                                  ((T, "pe"), (A, "act"), (V, "dve"), (G, "pool"), (S, "sp")))
        lanes = [pe, act, dve, pool, sp]
        dma = Dmas(sp, [sem(f"dma_sp{i}") for i in range(24)])
        gdma = Dmas(pool, [sem(f"dma_pool{i}") for i in range(12)])

        def sb(name, shape, dt, scope=ctx):
            return scope.enter_context(nc.sbuf_tensor(name, list(shape), dt))

        psum = ctx.enter_context(nc.psum_tensor("psum", [P, 8, 512], F32))
        bank = [Slot(psum[:, i, :]) for i in range(8)]

        def use(slots):
            r = Ring([])
            r.slots = list(slots)
            return r

        x = sb("x", [P, TILES, DIM], F32)
        ident = sb("ident", [P, P], F32)
        gates = sb("gates", [P, 4], F32)
        tg = sb("tanh_gates", [P, 4], F32)
        b_att = sb("bias_att", [P, DIM], F32)
        half_pow = sb("minus_half", [P, HT], F32)
        stats = Ring([sb(f"stats{i}", [P, HT, 6], F32)[:, :, :] for i in range(2)])
        moments = Ring([sb(f"moments{i}", [P, HT, 2], F32)[:, :, :] for i in range(2)])
        vareps = Ring([sb(f"vareps{i}", [P, HT], F32)[:, :] for i in range(2)])
        rstd = Ring([sb(f"rstd{i}", [P, HT], F32)[:, :] for i in range(2)])

        rows_dram = nc.dram_tensor("rows_scratch", (TOKENS, ROW), F32).ap()
        feats_dram = nc.dram_tensor("feats_scratch", (HALVES, P, CD * HALF), F32).ap()
        sum_dram = [nc.dram_tensor(f"expert_sums{i}", (TOKENS + P, DIM), F32).ap() for i in range(SUMS)]
        list_dram = nc.dram_tensor("list_scratch", (4, P, NB), F32).ap()
        max_dram = nc.dram_tensor("max_scratch", (HALVES, 2, HEADS, HALF), F32).ap()

        x_view = D["x"].rearrange("(i p) f -> p i f", p=P)
        out_view = out.rearrange("(i p) f -> p i f", p=P)
        m_x = []
        for h in range(HALVES):
            m_x.append(dma.copy(x[:, HT * h:HT * h + HT, :], x_view[:, HT * h:HT * h + HT, :]))
            if h == 0:
                m_ident = dma.copy(ident[:, :], D["ident"])
                m_gates = dma.copy(gates[:, :], D["gates"])
        m_batt = dma.copy(b_att[:, :], D["bo"])
        m_hp = pool.do(G.memset, half_pow[:, :], -0.5)

        act.wait(m_gates)
        m_tg = act.do(A.activation, tg[:, :], gates[:, :], ACT.Tanh)
        act.do(A.preload_act_table_set, "natural_log_exp_and_others", signal=False)
        pool.wait(m_tg, m_batt)
        m_batt = pool.do(G.tensor_tensor, b_att[:, :], b_att[:, :],
                                                   tg[:, 0:1].to_broadcast([P, DIM]), ALU.mult)

        x_ready = [[m] for m in m_x]

        def layernorm(h, dst, width_free):
            st, mo, ve, rs = stats.take(dve), moments.take(dve), vareps.take(pool), rstd.take(pool)
            dve.wait(x_ready[h])
            got = []
            for t in range(HT):
                got.append(dve.do(V.bn_stats, st.ap[:, t, :], x[:, HT * h + t, :]))
            for t in range(HT):
                dve.wait(got[t])
                m = dve.do(V.bn_aggr, mo.ap[:, t, :], st.ap[:, t, :])
            st.free = [m]
            yield
            pool.wait(m)
            m = pool.do(G.tensor_scalar, ve.ap, mo.ap[:, :, 1], EPS, 0.0, ALU.add, ALU.add)
            pool.wait(m, m_hp)
            m = pool.do(G.tensor_tensor, rs.ap, ve.ap, half_pow[:, :], ALU.pow)
            ve.free = [m]
            yield
            dve.wait(m)
            width_free.ready = []
            for t in range(HT):
                m = dve.do(V.tensor_scalar, 
                    dst[:, t, :], x[:, HT * h + t, :], mo.ap[:, t, 0:1], rs.ap[:, t:t + 1],
                    ALU.subtract, ALU.mult)
                width_free.ready.append(m)
            mo.free = rs.free = [m]
            yield

        def turn_half(src, ready, misc):
            banks = []
            for c in range(CD):
                b = misc.take(pe)
                for t in range(HT):
                    pe.wait(ready[t] if t < len(ready) else ready[-1])
                    m = pe.do(T.transpose, 
                        b.ap[:, t * P:(t + 1) * P], src[:, t, c * P:(c + 1) * P], ident[:, :],
                        signal=t == HT - 1)
                b.ready = [m]
                banks.append(b)
            return banks

        def send_stack(stage, stack):
            sp.wait(stage.ready)
            stack.ready = []
            hi = stage.ap.bitcast(F32)
            st = stack.ap.bitcast(F32)
            for r in range(4):
                for part, row in ((0, 0), (0, 32), (1, 64)):
                    stack.ready.append(dma.copy(st[row:row + 32, r::4, :],
                                                hi[32 * r:32 * r + 32, part, :, :]))
            stage.free = list(stack.ready)

        def split_keys(raw, stack, rows, scale):
            act.wait(raw.ready)
            m = act.do(A.activation, stack.ap[0:rows, :, :], raw.ap[0:rows, :, :], ACT.Copy,
                                              scale=scale)
            dve.wait(m, raw.ready)
            m2 = dve.do(V.scalar_tensor_tensor, 
                stack.ap[32:64, :, :].rearrange("p a b -> p (a b)"),
                raw.ap[32:64, :, :].rearrange("p a b -> p (a b)"), scale,
                stack.ap[32:64, :, :].rearrange("p a b -> p (a b)").bitcast(F32),
                ALU.mult, ALU.subtract)
            raw.free = [m, m2]
            stack.ready = [m, m2]

        def key_scores(chunk, rows, bank_slot, keys, stack, g):
            b = bank_slot
            pe.wait(keys.ready, stack.ready)
            if chunk < 4:
                head = 4 * g + chunk
                m = pe.do(T.matmul, b.ap, keys.ap[0:rows, head, :],
                                             stack.ap[0:rows, head // 2, :], start=True, stop=True)
            else:
                for s in range(2):
                    pair = 2 * g + s
                    m = pe.do(T.matmul, 
                        b.ap, keys.ap[0:rows, HEADS + pair, :], stack.ap[0:rows, pair, :],
                        start=s == 0, stop=s == 1, signal=s == 1)
            b.ready = [m]

        def weigh_values(g, weights, values, o_bank, turned):
            pe.wait(values.ready, o_bank.free)
            for part in range(2):
                for j in range(4):
                    w = weights[j] if part == 0 else weights[4]
                    pe.wait(w.ready)
                    m = pe.do(T.matmul, 
                        o_bank.ap[32 * j:32 * j + 32, :], values.ap[:, part, 4 * g + j, :], w.ap,
                        start=part == 0, stop=part == 1, tile_position=(0, 32 * j),
                        signal=j == 3)
            for w in weights:
                w.free = [m]
            act.wait(m)
            m2 = act.do(A.activation, turned.ap[:, g, :], o_bank.ap, ACT.Copy)
            o_bank.free = [m2]
            turned.ready = [m2]
            return m

        def normalize_heads(t, turned, misc, sums, dst):
            b = misc.take(pe)
            pe.wait(turned.ready)
            for g in range(GROUPS):
                m = pe.do(T.transpose, b.ap[:, g * P:(g + 1) * P],
                                                     turned.ap[:, g, t * P:(t + 1) * P], ident[:, :],
                          signal=g == GROUPS - 1)
            s = sums.take(dve)
            view = b.ap.rearrange("p (h w) -> p h w", w=32)
            dve.wait(m)
            m2 = dve.do(V.reciprocal, s.ap, view[:, :, HD])
            dve.wait(m2)
            m3 = dve.do(V.tensor_tensor, 
                dst.rearrange("p (h d) -> p h d", d=HD), view[:, :, 0:HD],
                s.ap.unsqueeze(2).to_broadcast([P, HEADS, HD]), ALU.mult)
            b.free = s.free = [m3]
            return m, m3

        sgate = sb("sgate", [P, TILES], F32)
        w_con = sb("w_con_fused", [P, HB, DIM], F32)
        positions = w_con[:, :, :].rearrange("p a n -> p (a n)").bitcast(BF16)
        pos_a, pos_b = (positions[:, i * TILES * EXPERTS:(i + 1) * TILES * EXPERTS].rearrange(
            "p (t n) -> p t n", n=EXPERTS) for i in range(2))

        scope = ExitStack()
        with scope:
            s0 = lambda n, s, d: sb(n, s, d, scope)
            wq, wo, wv = (s0(f"w{n}", [P, CD, DIM], F32) for n in "qov")
            wk_ring = Ring([s0(f"wk_stack{i}", [P, CD, 4, STACK], F32)[:, :, :, :] for i in range(2)])
            bk = s0("bk_stack", [STACK, HEADS], F32)
            bq = s0("bq", [P, CD], F32)
            bv = s0("bv", [P, DIM], F32)
            gate_w = s0("gate_w", [P, CD, EXPERTS + 1], F32)
            ctx_t = s0("ctx_t", [P, CD, 3 * P], F32)
            upper = s0("upper", [P, P], BF16)
            ones = s0("ones", [P, P], BF16)
            zeros = s0("zeros", [P, 1, DIM], F32)
            masks = s0("masks", [P, HT, EXPERTS], BF16)
            before = s0("mask_sums", [P, 2, EXPERTS], BF16)
            k_raw = Slot(s0("k_raw0", [STACK, NK, P], F32)[:, :, :])
            keys_ring = Ring([s0(f"k_stack{i}", [P, NK, P], F32R)[:, :, :] for i in range(2)])
            vals_ring = Ring([s0(f"values{i}", [P, 2, HEADS, 32], F32)[:, :, :, :] for i in range(2)])
            q_stacks = Ring([s0(f"q_stack{i}", [P, PAIRS, HALF], F32R)[:, :, :] for i in range(2)])
            q_stage = Ring([s0("q_stage", [P, 2, CD, HALF], F32R)[:, :, :, :]])
            weights = Ring([s0(f"weights{i}", [P, HALF], F32)[:, :] for i in range(9)])
            turned_ring = Ring([s0(f"turned{i}", [P, GROUPS, HALF], F32)[:, :, :] for i in range(2)])
            normed = Ring([s0("normed", [P, HT, DIM], F32)[:, :, :]])
            rows = Ring([s0("rows", [P, HT, ROW], F32)[:, :, :]])
            feats = Ring([s0(f"feats{i}", [P, CD, HALF], F32)[:, :, :] for i in range(2)])
            att = Ring([s0("att", [P, HT, DIM], F32)[:, :, :]])
            sums = Ring([s0(f"sums{i}", [P, HEADS], F32)[:, :] for i in range(2)])
            probs = Ring([s0(f"probs{i}", [P, HT, EXPERTS], F32)[:, :, :] for i in range(1)])
            small = Ring([s0(f"small{i}", [P, 8, HT], F32)[:, :, :] for i in range(2)])
            top = Ring([s0(f"top{i}", [P, HT, TOPK], F32)[:, :, :] for i in range(2)])
            picked = Ring([s0(f"picked{i}", [P, HT, EXPERTS], F32)[:, :, :] for i in range(1)])
            posf = Ring([s0("pos_f", [P, HT, EXPERTS], F32)[:, :, :]])
            posi = Ring([s0("pos_i", [P, 2, HT, EXPERTS], I32)[:, :, :, :]])

            m_w = {}
            for name, t in (("bk", bk[:, :]),
                            ("wv", wv[:, :, :]), ("bv", bv[:, :]), ("wq", wq[:, :, :]), ("bq", bq[:, :]),
                            ("wo", wo[:, :, :]), ("gate_w", gate_w[:, :, :]), ("upper", upper[:, :]),
                            ):
                m_w[name] = dma.copy(t, D[name])
            m = pool.do(G.memset, zeros[:, :, :], 0.0)
            pool.wait(m)
            m_sums = [gdma.start(G.dma_start, t.rearrange("(p r) f -> p r f", p=P),
                                 zeros[:, :, :].to_broadcast([P, TILES + 1, DIM])) for t in sum_dram]
            m_ones = pool.do(G.memset, ones[:, :], 1.0)
            m_before = pool.do(G.memset, before[:, :, :], 0.0)
            sum_ready = [m_before]
            m_z = pool.do(G.memset, k_raw.ap, 0.0)
            k_raw.free = [m_z]

            def clear_values(ring):
                for v in ring.slots:
                    a = [pool.do(G.memset, v.ap[:, 1, :, :], 0.0),
                         pool.do(G.memset, v.ap[:, 0, :, HD:32], 1.0)]
                    for j in range(4):
                        pool.wait(a)
                        a.append(pool.do(G.memset, 
                            v.ap[32 * j:32 * j + REST, 1, j::4, HD:32], 1.0))
                    pool.wait(a)
                    v.free = a

            clear_values(vals_ring)

            misc = use(bank[6:8])
            s_banks = use(bank[0:5])
            o_bank = bank[5]
            keys_of, vals_of, stack_of, turned_of = {}, {}, {}, {}
            ctx_slot = Slot(ctx_t[:, :, :])

            def prepare_keys(b):
                sp.wait(ctx_slot.free)
                m_ctx = dma.copy(ctx_t[:, :, :], D["ctx_t"][b])
                pe.wait(m_ctx)
                dve.wait(k_raw.free, m_w["bk"])
                k_raw.free = None
                k_raw.ready = []
                for p in range(PAIRS):
                    if p % 2 == 0:
                        wk = wk_ring.take(sp)
                        wk.ready = [dma.copy(wk.ap, D["wk"][p // 2])]
                    pe.wait(wk.ready)
                    bk_slot = misc.take(pe)
                    for a in range(2):
                        for c in range(CD):
                            m = pe.do(T.matmul, 
                                bk_slot.ap[0:STACK, a * KEYS:(a + 1) * KEYS], wk.ap[:, c, 2 * (p % 2) + a, :],
                                ctx_t[:, c, 0:KEYS], start=c == 0, stop=c == CD - 1,
                                signal=a == 1 and c == CD - 1)
                    if p % 2:
                        wk.free = [m]
                    view = bk_slot.ap[0:STACK, 0:2 * KEYS].rearrange("p (a k) -> p a k", a=2)
                    bias = bk[:, 2 * p:2 * p + 2].unsqueeze(2)
                    s = p % 2
                    dve.wait(m)
                    k_raw.ready.append(dve.do(V.tensor_tensor, 
                        k_raw.ap[:, 2 * p:2 * p + 2, :], view[:, :, 0:P],
                        bias.to_broadcast([STACK, 2, P]), ALU.add))
                    k_raw.ready.append(dve.do(V.tensor_tensor, 
                        k_raw.ap[:, HEADS + p, :].rearrange("p (j k) -> p j k", k=32)[:, 2 * s:2 * s + 2, 0:REST],
                        view[:, :, P:KEYS], bias.to_broadcast([STACK, 2, REST]), ALU.add))
                    bk_slot.free = k_raw.ready[-1:]
                    yield
                k_stack = keys_ring.take(act)
                split_keys(k_raw, k_stack, STACK, 0.25)
                keys_of[b] = k_stack
                yield
                v_slot = misc.take(pe)
                values = vals_ring.take(dve)
                pe.wait(m_w["wv"])
                for part in range(2):
                    for c in range(CD):
                        m = pe.do(T.matmul, 
                            v_slot.ap[:, part * DIM:(part + 1) * DIM],
                            ctx_t[:, c, 2 * part * P:(2 * part + 1) * P], wv[:, c, :],
                            start=c == 0, stop=c == CD - 1, signal=part == 1 and c == CD - 1)
                ctx_slot.free = [m]
                dve.wait(m, m_w["bv"])
                values.ready = [dve.do(V.tensor_tensor, 
                    values.ap[:, 0, :, 0:HD], v_slot.ap[:, 0:DIM].rearrange("p (h d) -> p h d", d=HD),
                    bv[:, :].rearrange("p (h d) -> p h d", d=HD), ALU.add)]
                for j in range(4):
                    r = slice(32 * j, 32 * j + REST)
                    values.ready.append(dve.do(V.tensor_tensor, 
                        values.ap[r, 1, j::4, 0:HD],
                        v_slot.ap[r, DIM:2 * DIM].rearrange("p (h d) -> p h d", d=HD)[:, j::4, :],
                        bv[r, :].rearrange("p (h d) -> p h d", d=HD)[:, j::4, :], ALU.add))
                v_slot.free = values.ready[-1:]
                vals_of[b] = values
                yield

            def prepare_queries(h):
                n = normed.take(dve)
                yield from layernorm(h, n.ap, n)
                pool.wait(n.ready[-1], m_batt)
                m = pool.do(G.tensor_tensor, 
                    x[:, HT * h:HT * h + HT, :], x[:, HT * h:HT * h + HT, :],
                    b_att[:, :].unsqueeze(1).to_broadcast([P, HT, DIM]), ALU.add)
                x_ready[h] = [m]
                yield
                pe.wait(m_ident)
                f = feats.take(act)
                for c, b in enumerate(turn_half(n.ap, n.ready, misc)):
                    act.wait(b.ready)
                    m = act.do(A.activation, f.ap[:, c, :], b.ap, ACT.Copy)
                    f.ready.append(m)
                    b.free = [m]
                    n.free = list(b.ready)
                yield
                stage = q_stage.take(act, dve)
                for mo in range(CD):
                    b = misc.take(pe)
                    pe.wait(f.ready, m_w["wq"])
                    for c in range(CD):
                        m = pe.do(T.matmul, 
                            b.ap, wq[:, c, mo * P:(mo + 1) * P], f.ap[:, c, :],
                            start=c == 0, stop=c == CD - 1, signal=c == CD - 1)
                    act.wait(m, m_w["bq"])
                    m1 = act.do(A.activation, 
                        stage.ap[:, 0, mo, :], b.ap, ACT.Identity, bias=bq[:, mo:mo + 1])
                    dve.wait(m1)
                    m2 = dve.do(V.scalar_tensor_tensor, 
                        stage.ap[:, 1, mo, :], b.ap, bq[:, mo:mo + 1],
                        stage.ap[:, 0, mo, :].bitcast(F32), ALU.add, ALU.subtract)
                    b.free = [m2]
                    stage.ready += [m1, m2]
                    yield
                f.free = [m]
                stack = q_stacks.take(sp)
                send_stack(stage, stack)
                stack_of[h] = stack
                yield

            def after_attention(h, turned):
                a = att.take(dve)
                for t in range(HT):
                    m, m3 = normalize_heads(t, turned, misc, sums, a.ap[:, t, :])
                    a.ready.append(m3)
                    yield
                turned.free = [m]
                f = feats.take(act)
                for c, b in enumerate(turn_half(a.ap, a.ready, misc)):
                    act.wait(b.ready)
                    m = act.do(A.activation, f.ap[:, c, :], b.ap, ACT.Copy)
                    f.ready.append(m)
                    b.free = [m]
                    a.free = list(b.ready)
                yield
                x_marks = []
                for two in range(HT // 2):
                    b = misc.take(pe)
                    pe.wait(f.ready, m_w["wo"])
                    for i in range(2):
                        for c in range(CD):
                            t = 2 * two + i
                            m = pe.do(T.matmul, 
                                b.ap[:, i * DIM:(i + 1) * DIM], f.ap[:, c, t * P:(t + 1) * P],
                                wo[:, c, :], start=c == 0, stop=c == CD - 1,
                                signal=i == 1 and c == CD - 1)
                    dve.wait(m, x_ready[h])
                    xs = x[:, HT * h + 2 * two:HT * h + 2 * two + 2, :].rearrange("p i f -> p (i f)")
                    m2 = dve.do(V.scalar_tensor_tensor, 
                        xs, b.ap, tg[:, 0:1], xs, ALU.mult, ALU.add)
                    b.free = [m2]
                    x_marks.append(m2)
                    yield
                f.free = [m]
                x_ready[h] = x_marks
                r = rows.take(dve)
                yield from layernorm(h, r.ap[:, :, 0:DIM], r)
                f = feats.take(act)
                for c, b in enumerate(turn_half(r.ap, r.ready, misc)):
                    act.wait(b.ready)
                    m = act.do(A.activation, f.ap[:, c, :], b.ap, ACT.Copy)
                    f.ready.append(m)
                    b.free = [m]
                    turned_rows = list(b.ready)
                yield
                sp.wait(f.ready)
                m_feats = dma.copy(feats_dram[h].rearrange("p (c n) -> p c n", c=CD), f.ap)
                NL = EXPERTS + 1
                b = misc.take(pe)
                pe.wait(f.ready, m_w["gate_w"])
                for t in range(HT):
                    for c in range(CD):
                        m = pe.do(T.matmul, 
                            b.ap[:, t * NL:(t + 1) * NL], f.ap[:, c, t * P:(t + 1) * P],
                            gate_w[:, c, :], start=c == 0, stop=c == CD - 1,
                            signal=t == HT - 1 and c == CD - 1)
                f.free = [m, m_feats]
                logits = b.ap[:, 0:HT * NL].rearrange("p (t n) -> p t n", n=NL)
                pr, sm, tp, pk = probs.take(dve), small.take(dve), top.take(dve), picked.take(dve)
                dve.wait(m)
                m = dve.do(V.tensor_reduce, sm.ap[:, 0, :], logits[:, :, 0:EXPERTS], AX.X, ALU.max)
                dve.wait(m)
                m = dve.do(V.tensor_tensor, pr.ap, logits[:, :, 0:EXPERTS],
                           sm.ap[:, 0, :].unsqueeze(2).to_broadcast([P, HT, EXPERTS]), ALU.subtract)
                act.wait(m)
                m1 = act.do(A.activation, pr.ap, pr.ap, ACT.Exp)
                m2 = act.do(A.activation, sm.ap[:, 1, :], logits[:, :, EXPERTS], ACT.Exp, scale=-1.0)
                b.free = [m, m2]
                yield
                dve.wait(m1, m2)
                ma = dve.do(V.tensor_reduce, sm.ap[:, 2, :], pr.ap, AX.X, ALU.add)
                mb = dve.do(V.tensor_scalar, sm.ap[:, 3, :], sm.ap[:, 1, :], 1.0, 0.0, ALU.add, ALU.add)
                dve.wait(ma, mb)
                ma = dve.do(V.reciprocal, sm.ap[:, 4:6, :].rearrange("p a t -> p (a t)"),
                                                   sm.ap[:, 2:4, :].rearrange("p a t -> p (a t)"))
                dve.wait(ma)
                m_sg = dve.do(V.tensor_scalar, sgate[:, HT * h:HT * h + HT], sm.ap[:, 5, :],
                                                        tg[:, 1:2], None, ALU.mult)
                m = dve.do(V.tensor_tensor, pr.ap, pr.ap,
                           sm.ap[:, 4, :].unsqueeze(2).to_broadcast([P, HT, EXPERTS]), ALU.mult)
                dve.wait(m)
                ms = [dve.do(V.max, tp.ap[:, t, :], pr.ap[:, t, :]) for t in range(HT)]
                yield
                for t in range(HT):
                    dve.wait(ms[t])
                    m = dve.do(V.match_replace, pk.ap[:, t, :], tp.ap[:, t, :],
                                                              pr.ap[:, t, :], -1.0)
                ma = dve.do(V.tensor_reduce, sm.ap[:, 6, :], tp.ap, AX.X, ALU.add)
                dve.wait(m, ma, mask_free)
                m_mask = dve.do(V.tensor_scalar, masks[:, :, :], pk.ap, 0.0, None, ALU.is_lt)
                ma = dve.do(V.reciprocal, sm.ap[:, 7, :], sm.ap[:, 6, :])
                dve.wait(ma)
                ma = dve.do(V.tensor_scalar, sm.ap[:, 7, :], sm.ap[:, 7, :], tg[:, 1:2], None, ALU.mult)
                dve.wait(ma)
                m = dve.do(V.tensor_tensor, r.ap[:, :, DIM:ROW], pr.ap,
                           sm.ap[:, 7, :].unsqueeze(2).to_broadcast([P, HT, EXPERTS]), ALU.mult)
                pr.free = sm.free = tp.free = pk.free = [m]
                sp.wait(m, r.ready)
                m_rows = dma.copy(rows_dram[HALF * h:HALF * (h + 1), :].rearrange("(t p) n -> p t n", p=P), r.ap)
                r.free = [m_rows] + turned_rows
                yield
                b = misc.take(pe)
                pe.wait(m_mask, m_w["upper"], m_ones)
                for t in range(HT):
                    i = HT * h + t
                    pe.do(T.matmul, b.ap[:, t * EXPERTS:(t + 1) * EXPERTS], upper[:, :],
                                                  masks[:, t, :], start=True, stop=False, signal=False)
                    pe.wait(sum_ready[0])
                    m = pe.do(T.matmul, b.ap[:, t * EXPERTS:(t + 1) * EXPERTS], ones[:, :],
                                                           before[:, i % 2, :], start=False, stop=True)
                    dve.wait(m, sum_ready[0])
                    sum_ready[0] = dve.do(V.tensor_tensor, 
                        before[:, (i + 1) % 2, :], before[:, i % 2, :], masks[:, t, :], ALU.add)
                counts = b.ap[:, 0:HT * EXPERTS].rearrange("p (t n) -> p t n", n=EXPERTS)
                pf, pi = posf.take(dve), posi.take(dve)
                FAR = 4096.0
                dve.wait(m)
                m = dve.do(V.scalar_tensor_tensor, pf.ap, masks[:, :, :], -FAR, counts, ALU.mult, ALU.add)
                mask_free[:] = [m]
                b.free = [m]
                dve.wait(m)
                m = dve.do(V.tensor_scalar, pf.ap, pf.ap, FAR, None, ALU.add)
                dve.wait(m)
                ma = dve.do(V.tensor_copy, pi.ap[:, 0, :, :], pf.ap)
                pf.free = [ma]
                dve.wait(ma)
                mb = dve.do(V.tensor_scalar, pi.ap[:, 1, :, :], pi.ap[:, 0, :, :], 4, None,
                                                      ALU.logical_shift_right)
                dve.wait(mb)
                mc = dve.do(V.tensor_scalar, pi.ap[:, 0, :, :], pi.ap[:, 0, :, :], NB - 1, None,
                                                      ALU.bitwise_and)
                dve.wait(mc)
                sl = slice(HT * h, HT * h + HT)
                md = dve.do(V.tensor_copy, pos_a[:, sl, :], pi.ap[:, 1, :, :])
                me = dve.do(V.tensor_copy, pos_b[:, sl, :], pi.ap[:, 0, :, :])
                pos_ready.extend([md, me])
                pi.free = [me]
                yield

            mask_free, pos_ready = [], []
            fg = Background()
            for g_ in (prepare_keys(0), prepare_queries(0)):
                fg.add(g_)
            fg.drain()
            early, late = Background(), Background()
            later = {}
            tick = [0]

            def at(n, fn):
                later.setdefault(n, []).append(fn)

            def advance():
                for fn in later.pop(tick[0], []):
                    fn()
                tick[0] += 1

            for h in range(HALVES):
                early.drain()
                keys, values, stack = keys_of[h // 2], vals_of[h // 2], stack_of[h]
                turned = turned_ring.take(act)
                if h + 1 < HALVES:
                    if (h + 1) % 2 == 0:
                        early.add(prepare_keys((h + 1) // 2))
                    early.add(prepare_queries(h + 1))
                for g in range(GROUPS):
                    chunks = []
                    for j in range(5):
                        n = tick[0]
                        b = s_banks.take(pe)
                        key_scores(j, STACK, b, keys, stack, g)
                        w = weights.take(act, dve)
                        if j in (1, 3):
                            act.wait(b.ready)
                            m = act.do(A.activation, w.ap, b.ap, ACT.Relu, scale=-1.0)
                        else:
                            dve.wait(b.ready)
                            m = dve.do(V.tensor_scalar, w.ap, b.ap, 0.0, None, ALU.min)

                        def log_it(m=m, w=w, sign=1.0 if j in (1, 3) else -1.0):
                            act.wait(m)
                            w.log = act.do(A.activation, w.ap, w.ap, ACT.Ln, bias=1.0, scale=sign)

                        def exp_it(w=w):
                            act.wait(w.log)
                            w.log = act.do(A.activation, w.ap, w.ap, ACT.Exp, scale=-1.0)

                        def take_max(b=b, w=w):
                            dve.wait(w.log)
                            m2 = dve.do(V.scalar_tensor_tensor, w.ap, b.ap, 1.0, w.ap, ALU.add, ALU.max)
                            w.ready = [m2]
                            b.free = [m2]

                        at(n + 1, log_it)
                        at(n + 2, exp_it)
                        at(n + 3, take_max)
                        chunks.append(w)
                        if j == 4:
                            def weigh(g=g, chunks=chunks, values=values, turned=turned, h=h):
                                m = weigh_values(g, chunks, values, o_bank, turned)
                                if g == GROUPS - 1:
                                    if h % 2 == 1:
                                        values.free = [m]
                                    late.add(after_attention(h, turned))
                            at(n + 4, weigh)
                            if g == GROUPS - 1:
                                stack.free = list(b.ready)
                                if h % 2 == 1:
                                    keys.free = list(b.ready)
                        advance()
                        early.step(1)
                        late.step(1)
                late.drain()
            while later:
                advance()
            late.drain()

        def barrier():
            marks = [(l.sem, l.count) for l in lanes if l.count]
            marks += [m for d in (dma, gdma) for m in d.last if m]
            for l in lanes:
                l.wait(marks)

        if stop == "L0":
            sp.wait([x_ready[h] for h in range(HALVES)])

        barrier()

        w_up = sb("w_up_fused", [P, CD, HID], F32)
        hid_bias = sb("hidden_bias", [P, HB], F32)
        b_out = sb("bias_out", [P, DIM], F32)

        scope = ExitStack()
        with scope:
            s1 = lambda n, s, d: sb(n, s, d, scope)
            a_iota = s1("a_iota", [P, 4, NA, EG], BF16)
            b_iota = s1("b_iota", [P, NB, EXPERTS], BF16)
            lane_no = s1("lane_no", [P, 1], F32)
            spare_row = s1("spare_row", [P, 1], F32)
            diag = s1("diag", [P, NB, EG], F32)
            hot_a = Ring([s1(f"hot_a{i}", [P, 3, 4, NA, EG], BF16)[:, :, :, :, :] for i in range(2)])
            hot_b = Ring([s1(f"hot_b{i}", [P, NB, EXPERTS], BF16)[:, :, :] for i in range(2)])
            lists = s1("lists", [P, 4, NB, EG], F32)
            lists_b = s1("lists_b", [P, 4, NB], F32)
            by_expert = s1("by_expert", [EXPERTS, P], F32)
            tokens = s1("tokens", [P, EXPERTS], U32)
            sum_rows = s1("sum_rows", [P, EXPERTS], U32)
            listed = s1("listed", [P, 3, EXPERTS], F32)
            w_ring = Ring([s1(f"expert_w{i}", [P, 3, DIM], F32)[:, :, :] for i in range(8)])
            got_ring = Ring([s1(f"got{i}", [P, ROW], F32)[:, :] for i in range(6)])
            got_t = Ring([s1(f"got_t{i}", [P, CD, P], F32)[:, :, :] for i in range(3)])
            silu_ring = Ring([s1(f"silu{i}", [P, P], F32)[:, :] for i in range(2)])
            inner_ring = Ring([s1(f"inner{i}", [P, P], F32)[:, :] for i in range(3)])
            made_ring = Ring([s1(f"made{i}", [P, DIM], F32)[:, :] for i in range(4)])
            w_sgu = s1("w_shared_up", [P, CD, 2 * SHARED], F32)
            w_sd = s1("w_shared_down", [P, SHARED // P, DIM], F32)
            feats = Ring([s1(f"feats_m{i}", [P, CD, HALF], F32)[:, :, :] for i in range(2)])
            s_silu = Ring([s1(f"shared_silu{i}", [P, HALF], F32)[:, :] for i in range(2)])
            s_inner = Ring([s1(f"shared_inner{i}", [P, SHARED // P, HALF], F32)[:, :, :] for i in range(2)])
            bf_u = s1("butterfly_u", [P, HB, DIM + 1], F32)
            bf_v = s1("butterfly_v", [P, HB, DIM + 1], F32)
            swaps = s1("swaps", [P, INSIDE, P], F32)
            taps = s1("taps", [P, 4, STAGES, HB], F32)
            up_bias = s1("up_bias", [P, HB], F32)
            down_bias = s1("down_bias", [P, DIM], F32)
            stage_m = Ring([s1(f"stage_m{i}", [P, P], F32)[:, :] for i in range(4)])
            part_ring = Ring([s1(f"stage_p{i}", [P, P], F32)[:, :] for i in range(2)])

            m_c = {n: dma.copy(t, D[n]) for n, t in (
                ("a_iota", a_iota[:, :, :, :]), ("b_iota", b_iota[:, :, :]), ("lane_no", lane_no[:, :]),
                ("spare_row", spare_row[:, :]),
                ("diag", diag[:, :, :]), ("w_sgu", w_sgu[:, :, :]), ("w_sd", w_sd[:, :, :]),
                ("w_exp", bf_u[:, :, :]), ("swaps", swaps[:, :, :]), ("taps", taps[:, :, :, :]),
                ("up_bias", up_bias[:, :]), ("b_con", b_out[:, :]), ("down_bias", down_bias[:, :]))}
            experts_w = {}

            def load_expert(e_):
                w = w_ring.take(sp)
                w.ready = [dma.copy(w.ap, D["expert_w"][e_])]
                experts_w[e_] = w

            for e_ in range(3):
                load_expert(e_)

            hot_banks = bank[0:4]
            for i in range(TILES):
                ha, hb = hot_a.take(dve), hot_b.take(dve)
                dve.wait(m_c["a_iota"], m_c["b_iota"], m_c["lane_no"], pos_ready)
                m = dve.do(V.tensor_tensor, ha.ap[:, 0, :, :, :], a_iota[:, :, :, :],
                           pos_a[:, i, :].rearrange("p (g e) -> p g e", e=EG).unsqueeze(2).to_broadcast(
                               [P, 4, NA, EG]), ALU.is_equal)
                mb = dve.do(V.tensor_tensor, hb.ap, b_iota[:, :, :],
                            pos_b[:, i, :].unsqueeze(1).to_broadcast([P, NB, EXPERTS]), ALU.is_equal)
                dve.wait(m)
                m1 = dve.do(V.tensor_scalar, ha.ap[:, 1, :, :, :], ha.ap[:, 0, :, :, :], lane_no[:, 0:1], None, ALU.mult)
                m2 = dve.do(V.tensor_scalar, ha.ap[:, 2, :, :, :], ha.ap[:, 0, :, :, :], float(P * i), None, ALU.mult)
                pe.wait(mb, m2)
                for g in range(4):
                    eg = slice(EG * g, EG * g + EG)
                    if i == 0:
                        pe.wait(hot_banks[g].free)
                    for part in (1, 2):
                        m = pe.do(T.matmul, hot_banks[g].ap[:, 0:NB * EG], ha.ap[:, part, g, :, :],
                                  hb.ap[:, :, eg], start=i == 0 and part == 1,
                                  stop=i == TILES - 1 and part == 2, signal=g == 3 and part == 2)
                ha.free = hb.free = [m]
            dve.wait(m, m_c["diag"], m_c["spare_row"])
            parts = []
            for g in range(4):
                parts.append(dve.do(V.tensor_tensor, lists[:, g, :, :],
                                    hot_banks[g].ap[:, 0:NB * EG].rearrange("p (b e) -> p b e", e=EG),
                                    diag[:, :, :], ALU.mult))
                hot_banks[g].free = [parts[-1]]
            dve.wait(parts)
            m = dve.do(V.tensor_reduce, lists_b[:, :, :], lists[:, :, :, :], AX.X, ALU.add)
            sp.wait(m)
            m = dma.copy(list_dram.rearrange("g p b -> p g b"), lists_b[:, :, :])
            sp.wait(m)
            ms = [dma.copy(by_expert[EG * g:EG * g + EG, :].rearrange("e (a b) -> e a b", a=NA),
                           list_dram[g].rearrange("(a e) b -> e a b", a=NA)) for g in range(4)]
            tok_bank = bank[7]
            pe.wait(ms, tok_bank.free)
            m = pe.do(T.transpose, tok_bank.ap[:, 0:EXPERTS], by_expert[:, :], ident[0:EXPERTS, 0:EXPERTS])
            dve.wait(m)
            m1 = dve.do(V.tensor_scalar, listed[:, 0, :], tok_bank.ap[:, 0:EXPERTS], -1.0, 0.0, ALU.add, ALU.max)
            m2 = dve.do(V.tensor_scalar, listed[:, 1, :], tok_bank.ap[:, 0:EXPERTS], 0.5, None, ALU.is_lt)
            dve.wait(m1, m2)
            m_tokens = [dve.do(V.tensor_copy, tokens[:, :], listed[:, 0, :])]
            m = dve.do(V.scalar_tensor_tensor, listed[:, 2, :], listed[:, 1, :], spare_row[:, 0:1],
                       listed[:, 0, :], ALU.mult, ALU.add)
            dve.wait(m)
            m_tokens.append(dve.do(V.tensor_copy, sum_rows[:, :], listed[:, 2, :]))
            tok_bank.free = [m2]

            back = Background()
            s_ring = use(bank[6:8])

            def shared_expert(h):
                f = feats.take(sp)
                f.ready = [dma.copy(f.ap, feats_dram[h].rearrange("p (c n) -> p c n", c=CD))]
                inner = s_inner.take(dve)
                yield
                for k in range(SHARED // P):
                    got = []
                    for part in range(2):
                        b = s_ring.take(pe)
                        pe.wait(f.ready, m_c["w_sgu"])
                        for c in range(CD):
                            m = pe.do(T.matmul, b.ap,
                                      w_sgu[:, c, part * SHARED + k * P:part * SHARED + (k + 1) * P],
                                      f.ap[:, c, :], start=c == 0, stop=c == CD - 1, signal=c == CD - 1)
                        got.append((b, m))
                    (bg, mg), (bu, mu) = got
                    sl = s_silu.take(act)
                    act.wait(mg)
                    m1 = act.do(A.activation, sl.ap, bg.ap, ACT.Silu)
                    bg.free = [m1]
                    dve.wait(m1, mu)
                    m2 = dve.do(V.tensor_tensor, inner.ap[:, k, :], sl.ap, bu.ap, ALU.mult)
                    bu.free = sl.free = [m2]
                    inner.ready.append(m2)
                    yield
                f.free = [mu]
                marks = []
                for two in range(HT // 2):
                    b = s_ring.take(pe)
                    pe.wait(inner.ready, m_c["w_sd"])
                    for i in range(2):
                        t = 2 * two + i
                        for k in range(SHARED // P):
                            m = pe.do(T.matmul, b.ap[:, i * DIM:(i + 1) * DIM],
                                      inner.ap[:, k, t * P:(t + 1) * P], w_sd[:, k, :],
                                      start=k == 0, stop=k == SHARED // P - 1,
                                      signal=i == 1 and k == SHARED // P - 1)
                    dve.wait(m, x_ready[h])
                    for i in range(2):
                        t = HT * h + 2 * two + i
                        marks.append(dve.do(V.scalar_tensor_tensor, x[:, t, :], b.ap[:, i * DIM:(i + 1) * DIM],
                                            sgate[:, t:t + 1], x[:, t, :], ALU.mult, ALU.add))
                    b.free = [marks[-1]]
                    yield
                inner.free = [m]
                x_ready[h] = marks

            f_ring = use(bank[5:6])

            def inside(buf, width, ready, which, s, k):
                mm, pp = stage_m.take(pool, dve), part_ring.take(pool)
                pool.wait(m_ident, m_c["taps"], m_c["swaps"])
                own, other = taps[:, 2 * which, s, k:k + 1], taps[:, 2 * which + 1, s, k:k + 1]
                ma = pool.do(G.tensor_scalar, pp.ap, ident[:, :], own, 0.0, ALU.mult, ALU.add)
                dve.wait(ma, m_c["taps"], m_c["swaps"])
                mb = dve.do(V.scalar_tensor_tensor, mm.ap, swaps[:, s, :], other, pp.ap, ALU.mult, ALU.add)
                pp.free = [mb]
                b = f_ring.take(pe)
                pe.wait(mb, ready[k])
                mc = pe.do(T.matmul, b.ap[:, 0:width], mm.ap, buf[:, k, 0:width], start=True, stop=True)
                mm.free = [mc]
                act.wait(mc)
                md = act.do(A.activation, buf[:, k, 0:width], b.ap[:, 0:width], ACT.Copy)
                b.free = [md]
                ready[k] = [md]

            def across(src, dst, width, ready, which, s):
                new = []
                pool.wait(ready)
                for k in range(HB):
                    o = k ^ (1 << (s - INSIDE))
                    own = taps[:, 2 * which, s, k:k + 1]
                    other = taps[:, 2 * which + 1, s, (o if which else k):(o if which else k) + 1]
                    ma = pool.do(G.tensor_scalar, dst[:, k, 0:width], src[:, k, 0:width], own, 0.0,
                                 ALU.mult, ALU.add)
                    dve.wait(ma)
                    mb = dve.do(V.scalar_tensor_tensor, dst[:, k, 0:width], src[:, o, 0:width], other,
                                dst[:, k, 0:width], ALU.mult, ALU.add)
                    new.append([mb])
                ready[:] = new

            def fuse():
                ready = [[m_c["w_exp"]] for _ in range(HB)]
                for s in range(INSIDE):
                    for k in range(HB):
                        inside(bf_u, DIM + 1, ready, 0, s, k)
                        if k % 2:
                            yield
                bufs = [bf_u, bf_v]
                for s in range(INSIDE, STAGES):
                    across(bufs[0], bufs[1], DIM + 1, ready, 0, s)
                    bufs.reverse()
                    yield
                last = bufs[0]
                marks = []
                for c in range(CD):
                    for q in range(HB // 4):
                        b = f_ring.take(pe)
                        for i in range(4):
                            pe.wait(ready[4 * q + i])
                            m = pe.do(T.transpose, b.ap[:, i * P:(i + 1) * P],
                                      last[:, 4 * q + i, c * P:(c + 1) * P], ident[:, :], signal=i == 3)
                        act.wait(m)
                        m2 = act.do(A.activation, w_up[:, c, 4 * q * P:4 * (q + 1) * P], b.ap, ACT.Copy)
                        b.free = [m2]
                        marks.append(m)
                        yield
                dve.wait(ready, m_c["up_bias"])
                m = dve.do(V.tensor_tensor, hid_bias[:, :], last[:, :, DIM], up_bias[:, :], ALU.add)
                sp.wait(marks, m)
                m = dma.copy(bf_u[:, :, 0:DIM], D["w_con"])
                ready = [[m] for _ in range(HB)]
                bufs = [bf_u, w_con]
                for s in reversed(range(INSIDE, STAGES)):
                    across(bufs[0], bufs[1], DIM, ready, 1, s)
                    bufs.reverse()
                    yield
                for s in reversed(range(INSIDE)):
                    for k in range(HB):
                        inside(w_con, DIM, ready, 1, s, k)
                        if k % 2:
                            yield
                dve.wait(m_c["b_con"], m_c["down_bias"])
                m = dve.do(V.tensor_tensor, b_out[:, :], b_out[:, :], down_bias[:, :], ALU.add)
                dve.wait(m)
                dve.do(V.tensor_scalar, b_out[:, :], b_out[:, :], tg[:, 3:4], None, ALU.mult)
                yield

            for h in range(HALVES):
                back.add(shared_expert(h))
            fusing = Background()
            fusing.add(fuse())

            t_banks, h_banks, d_banks = use(bank[0:2]), use(bank[2:3]), use(bank[3:5])
            flow = {}

            def gather(e_):
                got = got_ring.take(pool)
                pool.wait(m_tokens)
                got.ready = [gdma.start(G.indirect_dma_start, got.ap, None, rows_dram,
                                        bass.IndirectOffsetOnAxis(ap=tokens[:, e_:e_ + 1], axis=0),
                                        bounds_check=TOKENS - 1, oob_is_err=False)]
                flow[e_] = {"got": got}

            def turn(e_):
                d = flow[e_]
                b = t_banks.take(pe)
                pe.wait(d["got"].ready)
                for c in range(CD):
                    m = pe.do(T.transpose, b.ap[:, c * P:(c + 1) * P], d["got"].ap[:, c * P:(c + 1) * P],
                              ident[:, :], signal=c == CD - 1)
                d["turned"] = m
                d["t"] = t = got_t.take(act)
                act.wait(m)
                m = act.do(A.activation, t.ap.rearrange("p c n -> p (c n)"), b.ap[:, 0:CD * P], ACT.Copy)
                b.free = t.ready = [m]

            def gate_up(e_):
                d = flow[e_]
                b, w, t = h_banks.take(pe), experts_w[e_], d["t"]
                pe.wait(t.ready, w.ready)
                for part in range(2):
                    for c in range(CD):
                        m = pe.do(T.matmul, b.ap[:, part * P:(part + 1) * P],
                                  w.ap[:, c, part * INNER:(part + 1) * INNER], t.ap[:, c, :],
                                  start=c == 0, stop=c == CD - 1, signal=part == 1 and c == CD - 1)
                t.free = [m]
                sl, inner = silu_ring.take(act), inner_ring.take(dve)
                act.wait(m)
                m1 = act.do(A.activation, sl.ap, b.ap[:, 0:P], ACT.Silu)
                dve.wait(m1)
                m2 = dve.do(V.tensor_tensor, inner.ap, sl.ap, b.ap[:, P:2 * P], ALU.mult)
                b.free = sl.free = inner.ready = [m2]
                d["inner"] = inner

            def down(e_):
                d = flow.pop(e_)
                b, w, inner, got = d_banks.take(pe), experts_w.pop(e_), d["inner"], d["got"]
                pe.wait(inner.ready)
                m = pe.do(T.matmul, b.ap[:, 0:DIM], inner.ap, w.ap[:, 2, :], start=True, stop=True)
                inner.free = w.free = [m]
                made = made_ring.take(dve)
                dve.wait(m, got.ready)
                m = dve.do(V.tensor_scalar, made.ap, b.ap[:, 0:DIM], got.ap[:, DIM + e_:DIM + e_ + 1],
                           None, ALU.mult)
                b.free = [m]
                got.free = [m, d["turned"]]
                pool.wait(m, m_sums[e_ % SUMS])
                m_sums[e_ % SUMS] = gdma.start(
                    G.indirect_dma_start, sum_dram[e_ % SUMS],
                    bass.IndirectOffsetOnAxis(ap=sum_rows[:, e_:e_ + 1], axis=0), made.ap, None,
                    bounds_check=TOKENS + P - 1, oob_is_err=True, compute_op=ALU.add)
                made.free = [m_sums[e_ % SUMS]]

            LAGS = ((gather, 0), (turn, 3), (gate_up, 4), (down, 5))
            for n in range(EXPERTS + LAGS[-1][1]):
                for work, lag in reversed(LAGS):
                    if 0 <= n - lag < EXPERTS:
                        work(n - lag)
                if n + 3 < EXPERTS:
                    load_expert(n + 3)
                back.step()
                fusing.step(2)
            back.drain()
            fusing.drain()
        barrier()

        ROWS1 = STACK + 4
        scope = ExitStack()
        with scope:
            s2 = lambda n, s, d: sb(n, s, d, scope)
            k_raw = Slot(s2("k1_raw", [ROWS1, NK, P], F32)[:, :, :])
            keys_ring = Ring([s2(f"k1_stack{i}", [P, NK, P], F32R)[:, :, :] for i in range(2)])
            vals_ring = Ring([s2(f"values1_{i}", [P, 2, HEADS, 32], F32)[:, :, :, :] for i in range(2)])
            q_stacks = Ring([s2(f"q1_stack{i}", [P, PAIRS, HALF], F32R)[:, :, :] for i in range(3)])
            q_stage = Ring([s2("q1_stage", [P, 2, CD, HALF], F32R)[:, :, :, :]])
            weights = Ring([s2(f"weights1_{i}", [P, HALF], F32)[:, :] for i in range(8)])
            turned_ring = Ring([s2("turned1_0", [P, GROUPS, HALF], F32)[:, :, :]])
            normed = Ring([s2("normed1", [P, HT, DIM], F32)[:, :, :]])
            att = Ring([s2("att1", [P, HT, DIM], F32)[:, :, :]])
            sums = Ring([s2(f"sums1_{i}", [P, HEADS], F32)[:, :] for i in range(2)])
            fetched = Ring([s2(f"fetched{i}", [P, SUMS, HT, DIM], F32)[:, :, :, :] for i in range(2)])
            peaks = Ring([s2(f"peaks{i}", [P, HT, HEADS], F32)[:, :, :] for i in range(2)])
            peak_t = Ring([s2(f"peak_t{i}", [HEADS, 2, HALF], F32R)[:, :, :] for i in range(2)])
            clear_values(vals_ring)
            s_banks, misc, o_bank = use(bank[0:3]), use(bank[6:8]), bank[5]
            peak_banks = use(bank[3:5])
            keys_of, vals_of, stack_of, fetched_of = {}, {}, {}, {}

            def fetch_experts(h):
                f = fetched.take(sp)
                sp.wait(m_sums)
                f.ready = [dma.copy(f.ap[:, i, :, :], sum_dram[i][HALF * h:HALF * (h + 1), :].rearrange(
                    "(t p) f -> p t f", p=P)) for i in range(SUMS)]
                fetched_of[h] = f

            def add_experts(h):
                f = fetched_of.pop(h)
                xs = x[:, HT * h:HT * (h + 1), :]
                for i in range(SUMS):
                    pool.wait(f.ready[i], x_ready[h])
                    x_ready[h] = [pool.do(G.tensor_tensor, xs, xs, f.ap[:, i, :, :], ALU.add)]
                    yield
                f.free = x_ready[h]

            def prepare_keys1(b):
                sp.wait(k_raw.free)
                k_raw.ready, k_raw.free = [dma.copy(k_raw.ap, D["k1"][b])], None
                k_stack = keys_ring.take(act)
                split_keys(k_raw, k_stack, ROWS1, 1.0)
                keys_of[b] = k_stack
                values = vals_ring.take(sp)
                src = D["ctx"][b]
                values.ready = [dma.copy(values.ap[:, 0, :, 0:HD], src[0:P].rearrange("k (h d) -> k h d", d=HD))]
                rest = src[P:KEYS].rearrange("k (g j d) -> k g j d", j=4, d=HD)
                for j in range(4):
                    values.ready.append(dma.copy(values.ap[32 * j:32 * j + REST, 1, j::4, 0:HD], rest[:, :, j, :]))
                vals_of[b] = values
                yield

            def prepare_queries1(h):
                n = normed.take(dve)
                yield from layernorm(h, n.ap, n)
                stage = q_stage.take(act, dve)
                for c, b in enumerate(turn_half(n.ap, n.ready, misc)):
                    act.wait(b.ready)
                    m1 = act.do(A.activation, stage.ap[:, 0, c, :], b.ap, ACT.Copy)
                    dve.wait(m1)
                    m2 = dve.do(V.tensor_tensor, stage.ap[:, 1, c, :], b.ap,
                                stage.ap[:, 0, c, :].bitcast(F32), ALU.subtract)
                    b.free = [m2]
                    stage.ready += [m1, m2]
                    n.free = list(b.ready)
                yield
                stack = q_stacks.take(sp)
                send_stack(stage, stack)
                stack_of[h] = stack
                yield

            def find_peaks(h):
                stack, keys = stack_of[h], keys_of[h // 2]
                peak = peaks.take(dve)
                for t in range(HT):
                    for two in range(PAIRS // 2):
                        pe.wait(keys.ready, stack.ready)
                        got = []
                        for i in range(2):
                            p = 2 * two + i
                            b = peak_banks.take(pe)
                            q = stack.ap[0:STACK, p, t * P:(t + 1) * P]
                            view = b.ap[:, 0:2 * KEYS].rearrange("p (a k) -> p a k", a=2)
                            pe.do(T.matmul, view[:, :, 0:P], q, keys.ap[0:STACK, 2 * p:2 * p + 2, :],
                                  start=True, stop=True, signal=False)
                            rest = keys.ap[0:STACK, HEADS + p, :].rearrange("p (j k) -> p j k", k=32)
                            got.append((p, b, view, pe.do(
                                T.matmul, view[:, :, P:KEYS], q, rest[:, 2 * i:2 * i + 2, 0:REST],
                                start=True, stop=True)))
                        for p, b, view, m in got:
                            dve.wait(m)
                            m = dve.do(V.tensor_reduce, peak.ap[:, t, 2 * p:2 * p + 2], view, AX.X, ALU.max)
                            b.free = [m]
                        yield
                b = misc.take(pe)
                pe.wait(m)
                for t in range(HT):
                    m = pe.do(T.transpose, b.ap[0:HEADS, t * P:(t + 1) * P], peak.ap[:, t, :], ident[:, :],
                              signal=t == HT - 1)
                peak.free = [m]
                pt = peak_t.take(act, dve)
                act.wait(m)
                m1 = act.do(A.activation, pt.ap[:, 0, :], b.ap[0:HEADS, :], ACT.Copy, scale=-1.0)
                dve.wait(m1)
                m2 = dve.do(V.scalar_tensor_tensor, pt.ap[:, 1, :], b.ap[0:HEADS, :], -1.0,
                            pt.ap[:, 0, :].bitcast(F32), ALU.mult, ALU.subtract)
                b.free = [m2]
                sp.wait(m2)
                m = dma.copy(max_dram[h].rearrange("r h n -> h r n"), pt.ap.bitcast(F32))
                pt.free = [m]
                sp.wait(m)
                for r in range(2):
                    row = STACK + 2 * r
                    stack.ready.append(dma.copy(stack.ap[row:row + 2, :, :].bitcast(F32),
                                                max_dram[h, r].rearrange("(p a) n -> a p n", a=2)))
                yield

            def after_attention1(h, turned):
                a = att.take(dve)
                for t in range(HT):
                    m, m3 = normalize_heads(t, turned, misc, sums, a.ap[:, t, :])
                    a.ready.append(m3)
                    yield
                turned.free = [m]
                marks = []
                for t in range(HT):
                    xs = x[:, HT * h + t, :]
                    dve.wait(a.ready[t], x_ready[h])
                    marks.append(dve.do(V.scalar_tensor_tensor, xs, a.ap[:, t, :], tg[:, 2:3], xs,
                                        ALU.mult, ALU.add))
                a.free = marks[-1:]
                x_ready[h] = marks
                yield

            early, peaking, late = Background(), Background(), Background()
            for b in range(2):
                early.add(prepare_keys1(b))
                fetch_experts(b)
            for h in range(2):
                early.add(add_experts(h))
                early.add(prepare_queries1(h))
            early.drain()
            peaking.add(find_peaks(0))
            peaking.drain()
            later, tick = {}, [0]
            for h in range(HALVES):
                early.drain()
                peaking.drain()
                keys, values, stack = keys_of[h // 2], vals_of[h // 2], stack_of[h]
                turned_slot = {}
                if h + 1 < HALVES:
                    peaking.add(find_peaks(h + 1))
                if h + 2 < HALVES:
                    fetch_experts(h + 2)
                    early.add(add_experts(h + 2))
                    early.add(prepare_queries1(h + 2))
                if h % 2 == 0 and 2 <= h < HALVES - 2:
                    early.add(prepare_keys1(h // 2 + 1))
                for g in range(GROUPS):
                    chunks = []
                    for j in range(5):
                        for fn in later.pop(tick[0], []):
                            fn()
                        n = tick[0]
                        tick[0] += 1
                        b = s_banks.take(pe)
                        key_scores(j, ROWS1, b, keys, stack, g)
                        w = weights.take(act)
                        act.wait(b.ready)
                        w.ready = [act.do(A.activation, w.ap, b.ap, ACT.Exp)]
                        b.free = list(w.ready)
                        chunks.append(w)
                        if j == 4:
                            def weigh(g=g, chunks=chunks, values=values, h=h, slot=turned_slot):
                                if g == 0:
                                    slot["t"] = turned_ring.take(act)
                                m = weigh_values(g, chunks, values, o_bank, slot["t"])
                                if g == GROUPS - 1:
                                    if h % 2 == 1:
                                        values.free = [m]
                                    late.add(after_attention1(h, slot["t"]))
                            later.setdefault(n + 2, []).append(weigh)
                            if g == GROUPS - 1:
                                stack.free = list(b.ready)
                                if h % 2 == 1:
                                    keys.free = list(b.ready)
                        early.step()
                        peaking.step()
                        late.step()
            for n in sorted(later):
                for fn in later[n]:
                    fn()
            late.drain()
        barrier()

        scope = ExitStack()
        with scope:
            s3 = lambda n, s, d: sb(n, s, d, scope)
            normed = Ring([s3(f"normed2_{i}", [P, HT, DIM], F32)[:, :, :] for i in range(2)])
            feats = Ring([s3(f"feats3_{i}", [P, CD, HALF], F32)[:, :, :] for i in range(2)])
            hidden = Ring([s3(f"hidden{i}", [P, HB, HALF], F32)[:, :, :] for i in range(2)])
            up_banks, down_banks, misc = use(bank[0:4]), use(bank[4:6]), use(bank[6:8])
            feats_of = {}

            def prepare_ffn(h):
                n = normed.take(dve)
                yield from layernorm(h, n.ap, n)
                pool.wait(n.ready[-1])
                x_ready[h] = [pool.do(G.tensor_tensor, x[:, HT * h:HT * h + HT, :],
                                      x[:, HT * h:HT * h + HT, :],
                                      b_out[:, :].unsqueeze(1).to_broadcast([P, HT, DIM]), ALU.add)]
                f = feats.take(act)
                for c, b in enumerate(turn_half(n.ap, n.ready, misc)):
                    act.wait(b.ready)
                    m = act.do(A.activation, f.ap[:, c, :], b.ap, ACT.Copy)
                    f.ready.append(m)
                    b.free = [m]
                    n.free = list(b.ready)
                feats_of[h] = f
                yield

            early = Background()
            early.add(prepare_ffn(0))
            early.drain()
            for h in range(HALVES):
                f = feats_of[h]
                hid = hidden.take(act)
                if h + 1 < HALVES:
                    early.add(prepare_ffn(h + 1))
                for k in range(HB):
                    b = up_banks.take(pe)
                    pe.wait(f.ready)
                    for c in range(CD):
                        m = pe.do(T.matmul, b.ap, w_up[:, c, k * P:(k + 1) * P], f.ap[:, c, :],
                                  start=c == 0, stop=c == CD - 1, signal=c == CD - 1)
                    act.wait(m)
                    m2 = act.do(A.activation, hid.ap[:, k, :], b.ap, ACT.Gelu, bias=hid_bias[:, k:k + 1])
                    hid.ready.append(m2)
                    b.free = [m2]
                    early.step()
                f.free = [m]
                early.drain()
                for two in range(HT // 2):
                    b = down_banks.take(pe)
                    for i in range(2):
                        t = 2 * two + i
                        for k in range(HB):
                            pe.wait(hid.ready[k])
                            m = pe.do(T.matmul, b.ap[:, i * DIM:(i + 1) * DIM],
                                      hid.ap[:, k, t * P:(t + 1) * P], w_con[:, k, :],
                                      start=k == 0, stop=k == HB - 1, signal=i == 1 and k == HB - 1)
                    dve.wait(m, x_ready[h])
                    tiles = slice(HT * h + 2 * two, HT * h + 2 * two + 2)
                    xs = x[:, tiles, :].rearrange("p i f -> p (i f)")
                    m2 = dve.do(V.scalar_tensor_tensor, xs, b.ap, tg[:, 3:4], xs, ALU.mult, ALU.add)
                    b.free = [m2]
                    sp.wait(m2)
                    dma.copy(out_view[:, tiles, :], x[:, tiles, :])
                hid.free = [m]

        barrier()
        block = ctx.enter_context(nc.Block())

        @block.tensor
        def _(_):
            pe.run()

        @block.scalar
        def _(_):
            act.run()

        @block.vector
        def _(_):
            dve.run()

        @block.gpsimd
        def _(_):
            pool.run()

        @block.sync
        def _(_):
            sp.run()


def constants():
    bf = mybir.dt.np(BF16)
    rows, cols = np.arange(P)[:, None], np.arange(P)[None, :]
    return {
        "ident": np.eye(P, dtype=np.float32),
        "upper": (rows < cols).astype(bf),
        "a_iota": np.broadcast_to(np.arange(NA)[:, None], (P, 4, NA, EG)).astype(bf),
        "b_iota": np.broadcast_to(np.arange(NB)[:, None], (P, NB, EXPERTS)).astype(bf),
        "lane_no": np.arange(1, P + 1, dtype=np.float32)[:, None].copy(),
        "spare_row": np.arange(TOKENS, TOKENS + P, dtype=np.float32)[:, None].copy(),
        "diag": np.broadcast_to((np.arange(P)[:, None] % EG == np.arange(EG)[None, :])[:, None, :],
                                (P, NB, EG)).astype(np.float32),
        "swaps": np.stack([rows ^ (1 << s) == cols for s in range(INSIDE)], 1).astype(np.float32),
    }


def feature_rows(w):
    return np.ascontiguousarray(w.reshape(-1, P, w.shape[1]).transpose(1, 0, 2))


def on_all(v):
    return np.ascontiguousarray(np.broadcast_to(v, (P, v.shape[0])))


def stacked(by_head, rows_aug):
    n = by_head.shape[1]
    s = np.zeros((STACK + rows_aug, HEADS, n), by_head.dtype)
    for h in range(HEADS):
        for block in range(3):
            r = 32 * block + HD * (h % 2)
            s[r:r + HD, h] = by_head[HD * h:HD * (h + 1)]
    return s


def key_stacks(keys):
    s = stacked(keys.T, 4)
    for h in range(HEADS):
        s[STACK + h % 2, h] = s[STACK + 2 + h % 2, h] = 1.0
    out = np.zeros((STACK + 4, NK, P), keys.dtype)
    out[:, :HEADS] = s[:, :, :P]
    for h in range(HEADS):
        out[:, HEADS + h // 2, 32 * (h % 4):32 * (h % 4) + REST] = s[:, h, P:]
    return out


def tap_rows(w):
    own, other = np.empty((STAGES, HID), w.dtype), np.empty((STAGES, HID), w.dtype)
    for s in range(STAGES):
        st = 1 << s
        v = w[s].reshape(HID // (2 * st), st, 2, 2)
        o, p = own[s].reshape(-1, 2, st), other[s].reshape(-1, 2, st)
        for r in range(2):
            o[:, r], p[:, r] = v[:, :, r, r], v[:, :, r, 1 - r]
    return own, other


def laid_out(i):
    ctx = i["ctx_1024"]
    d = constants()
    d["x"] = i["x"].reshape(TOKENS, DIM)
    d["gates"] = np.ascontiguousarray(np.broadcast_to(
        np.stack([i["g_xattn"][0], i["g_ffn"][0], i["g_xattn"][1], i["g_ffn"][1]]), (P, 4)))
    for n in "qvo":
        d[f"w{n}"] = feature_rows(i[f"L0_xattn_W{n}"].T)
    d["wk"] = stacked(i["L0_xattn_Wk"], 0).reshape(STACK, GROUPS, 4, CD, P).transpose(1, 4, 3, 2, 0)
    d["bk"] = np.ascontiguousarray(stacked(i["L0_xattn_bk"][:, None], 0)[:, :, 0])
    d["bq"] = np.ascontiguousarray(i["L0_xattn_bq"].reshape(CD, P).T)
    d["bv"], d["bo"] = on_all(i["L0_xattn_bv"]), on_all(i["L0_xattn_bo"])
    d["gate_w"] = feature_rows(np.concatenate([i["L0_ffn_gate_w"], i["L0_ffn_shared_gate_w"]], 1))
    keys = np.zeros((BATCH, DIM, 3 * P), ctx.dtype)
    keys[:, :, :KEYS] = ctx.transpose(0, 2, 1)
    for j in range(4):
        keys[:, :, 2 * P + 32 * j:2 * P + 32 * j + REST] = ctx[:, P:].transpose(0, 2, 1)
    d["ctx_t"] = np.stack([feature_rows(k) for k in keys])
    d["ctx"] = ctx
    d["k1"] = np.stack([key_stacks(ctx[b]) for b in range(BATCH)])
    gu, dn = i["L0_ffn_expert_gate_up_w"], i["L0_ffn_expert_down_w"]
    d["expert_w"] = np.ascontiguousarray(np.concatenate(
        [gu.reshape(EXPERTS, CD, P, 2 * INNER).transpose(0, 2, 1, 3), dn[:, :, None, :]], 2))
    d["w_sgu"] = feature_rows(i["L0_ffn_shared_gate_up_w"])
    d["w_sd"] = feature_rows(i["L0_ffn_shared_down_w"])
    d["w_exp"] = feature_rows(np.concatenate([i["L1_ffn_W_exp"].T, i["L1_ffn_b_exp"][:, None]], 1))
    d["w_con"] = feature_rows(i["L1_ffn_W_con"])
    taps = np.empty((4, STAGES, HID), i["L1_ffn_up_weights"].dtype)
    taps[0], taps[1] = tap_rows(i["L1_ffn_up_weights"])
    taps[2], taps[3] = tap_rows(i["L1_ffn_down_weights"])
    at = np.arange(HID)
    for s in range(INSIDE):
        taps[1, s] = taps[1, s][at ^ (1 << s)]
    d["taps"] = np.ascontiguousarray(taps.reshape(4, STAGES, HB, P).transpose(3, 0, 1, 2))
    d["up_bias"] = np.ascontiguousarray(i["L1_ffn_up_bias"].reshape(HB, P).T)
    d["b_con"], d["down_bias"] = on_all(i["L1_ffn_b_con"]), on_all(i["L1_ffn_down_bias"])
    return d


def kernel(**inputs):
    import concourse.bacc as bacc
    from concourse.bass_utils import run_bass_kernel_spmd

    nc = bacc.Bacc("TRN2", target_bir_lowering=False, num_devices=1)
    host = {n: np.asarray(a) for n, a in inputs.items()}
    arrays, aps = {}, {}
    for name, a in laid_out(host).items():
        arrays[f"in_{name}"] = np.ascontiguousarray(a)
        aps[name] = nc.dram_tensor(f"in_{name}", a.shape, mybir.dt.from_np(a.dtype), kind="ExternalInput").ap()
    out = nc.dram_tensor("out", (TOKENS, DIM), F32, kind="ExternalOutput").ap()
    build(nc, aps, out)
    result = run_bass_kernel_spmd(nc, [arrays], core_ids=[0])
    return result.results[0]["out"].reshape(BATCH, SEQ, DIM)
```

```python
from collections import deque
from contextlib import ExitStack

import numpy as np

import concourse.bass as bass
from concourse import mybir

F32 = mybir.dt.float32
F32R = mybir.dt.float32r
BF16 = mybir.dt.bfloat16
I32 = mybir.dt.int32
U32 = mybir.dt.uint32
ALU = mybir.AluOpType
ACT = mybir.ActivationFunctionType
AX = mybir.AxisListType

P = 128
BATCH, SEQ, DIM = 4, 1024, 256
KEYS = 154
REST = KEYS - P
HEADS = 16
HD = DIM // HEADS
PAIRS = HEADS // 2
GROUPS = HEADS // 4
TOKENS = BATCH * SEQ
TILES = TOKENS // P
HALF = 512
HT = HALF // P
HALVES = TOKENS // HALF
CD = DIM // P
STACK = 96
NK = HEADS + PAIRS
EXPERTS, TOPK, CAP = 64, 8, 128
INNER, SHARED = 128, 512
HID = 1024
HB = HID // P
STAGES = 10
INSIDE = 7
EPS = 1e-5
ROW = DIM + EXPERTS
SUMS = 2
PEAK_STEPS = (2, 1)
ON_ACT = (0, 1, 3, 4)
NA, NB = 8, 16
EG = 16


class Lane:

    def __init__(self, engine, sem):
        self.engine, self.sem, self.count, self.queue, self.passed = engine, sem, 0, [], {}

    def wait(self, *marks):
        for m in marks:
            if isinstance(m, list):
                self.wait(*m)
            elif m is not None:
                sem, value = m
                if self.passed.get(sem.name, 0) < value:
                    self.passed[sem.name] = value
                    self.queue.append((self.engine.wait_ge, (sem, value), {}, None, 0))

    def do(self, operation, *args, signal=True, **named):
        self.count += signal
        self.queue.append((operation, args, named, self.sem if signal else None, 1))
        return (self.sem, self.count) if signal else None

    def run(self):
        for operation, args, named, sem, by in self.queue:
            issued = operation(*args, **named)
            if sem is not None:
                issued.then_inc(sem, by)


class Dmas:

    def __init__(self, lane, sems):
        self.lane, self.sems, self.n = lane, sems, 0
        self.last = [None] * len(sems)

    def start(self, operation, *args, **named):
        k = self.n % len(self.sems)
        self.lane.wait(self.last[k])
        sem, value = self.sems[k], 16 * (self.n // len(self.sems) + 1)
        self.n += 1
        self.lane.queue.append((operation, args, named, sem, 16))
        self.last[k] = (sem, value)
        return self.last[k]

    def copy(self, out, in_):
        return self.start(self.lane.engine.dma_start, out, in_)


class Slot:

    def __init__(self, ap):
        self.ap, self.ready, self.free = ap, [], []


class Ring:
    def __init__(self, aps):
        self.slots, self.n = [Slot(a) for a in aps], 0

    def take(self, *writers):
        s = self.slots[self.n % len(self.slots)]
        self.n += 1
        assert s.free is not None, "its readers are not queued yet"
        for lane in writers:
            lane.wait(s.free)
        s.ready, s.free = [], None
        return s


class Background:

    def __init__(self):
        self.work = deque()

    def add(self, gen):
        self.work.append(gen)
        return gen

    def step(self, n=1):
        for _ in range(n):
            while self.work:
                try:
                    next(self.work[0])
                    break
                except StopIteration:
                    self.work.popleft()

    def finish(self, gen):
        while gen in self.work:
            self.step()

    def drain(self):
        while self.work:
            self.step()


def build(nc, D, out, stop=None):
    ctx = ExitStack()
    with ctx:
        sem = lambda name: ctx.enter_context(nc.semaphore(name))
        T, A, V, G, S = nc.tensor, nc.scalar, nc.vector, nc.gpsimd, nc.sync
        pe, act, dve, pool, sp = (Lane(n, sem(f"ends_{w}")) for n, w in
                                  ((T, "pe"), (A, "act"), (V, "dve"), (G, "pool"), (S, "sp")))
        lanes = [pe, act, dve, pool, sp]
        dma = Dmas(sp, [sem(f"dma_sp{i}") for i in range(24)])
        gdma = Dmas(pool, [sem(f"dma_pool{i}") for i in range(12)])

        def sb(name, shape, dt, scope=ctx):
            return scope.enter_context(nc.sbuf_tensor(name, list(shape), dt))

        psum = ctx.enter_context(nc.psum_tensor("psum", [P, 8, 512], F32))
        bank = [Slot(psum[:, i, :]) for i in range(8)]

        def use(slots):
            r = Ring([])
            r.slots = list(slots)
            return r

        x = sb("x", [P, TILES, DIM], F32)
        ident = sb("ident", [P, P], F32)
        gates = sb("gates", [P, 4], F32)
        tg = sb("tanh_gates", [P, 4], F32)
        b_att = sb("bias_att", [P, DIM], F32)
        half_pow = sb("minus_half", [P, HT], F32)
        stats = Ring([sb(f"stats{i}", [P, HT, 6], F32)[:, :, :] for i in range(2)])
        moments = Ring([sb(f"moments{i}", [P, HT, 2], F32)[:, :, :] for i in range(2)])
        vareps = Ring([sb(f"vareps{i}", [P, HT], F32)[:, :] for i in range(2)])
        rstd = Ring([sb(f"rstd{i}", [P, HT], F32)[:, :] for i in range(2)])

        rows_dram = nc.dram_tensor("rows_scratch", (TOKENS, ROW), F32).ap()
        feats_dram = nc.dram_tensor("feats_scratch", (HALVES, P, CD * HALF), F32).ap()
        sum_dram = [nc.dram_tensor(f"expert_sums{i}", (TOKENS + P, DIM), F32).ap() for i in range(SUMS)]
        list_dram = nc.dram_tensor("list_scratch", (4, P, NB), F32).ap()
        max_dram = nc.dram_tensor("max_scratch", (HALVES, 2, HEADS, HALF), F32).ap()

        x_view = D["x"].rearrange("(i p) f -> p i f", p=P)
        out_view = out.rearrange("(i p) f -> p i f", p=P)
        m_x = []
        for h in range(HALVES):
            m_x.append(dma.copy(x[:, HT * h:HT * h + HT, :], x_view[:, HT * h:HT * h + HT, :]))
            if h == 0:
                m_ident = dma.copy(ident[:, :], D["ident"])
                m_gates = dma.copy(gates[:, :], D["gates"])
        m_batt = dma.copy(b_att[:, :], D["bo"])
        m_hp = pool.do(G.memset, half_pow[:, :], -0.5)

        act.wait(m_gates)
        m_tg = act.do(A.activation, tg[:, :], gates[:, :], ACT.Tanh)
        act.do(A.preload_act_table_set, "natural_log_exp_and_others", signal=False)
        pool.wait(m_tg, m_batt)
        m_batt = pool.do(G.tensor_tensor, b_att[:, :], b_att[:, :],
                                                   tg[:, 0:1].to_broadcast([P, DIM]), ALU.mult)

        x_ready = [[m] for m in m_x]

        def layernorm(h, dst, width_free):
            st, mo, ve, rs = stats.take(dve), moments.take(dve), vareps.take(pool), rstd.take(pool)
            dve.wait(x_ready[h])
            got = []
            for t in range(HT):
                got.append(dve.do(V.bn_stats, st.ap[:, t, :], x[:, HT * h + t, :]))
            for t in range(HT):
                dve.wait(got[t])
                m = dve.do(V.bn_aggr, mo.ap[:, t, :], st.ap[:, t, :])
            st.free = [m]
            yield
            pool.wait(m)
            m = pool.do(G.tensor_scalar, ve.ap, mo.ap[:, :, 1], EPS, 0.0, ALU.add, ALU.add)
            pool.wait(m, m_hp)
            m = pool.do(G.tensor_tensor, rs.ap, ve.ap, half_pow[:, :], ALU.pow)
            ve.free = [m]
            yield
            dve.wait(m)
            width_free.ready = []
            for t in range(HT):
                m = dve.do(V.tensor_scalar, 
                    dst[:, t, :], x[:, HT * h + t, :], mo.ap[:, t, 0:1], rs.ap[:, t:t + 1],
                    ALU.subtract, ALU.mult)
                width_free.ready.append(m)
            mo.free = rs.free = [m]
            yield

        def turn_half(src, ready, misc):
            banks = []
            for c in range(CD):
                b = misc.take(pe)
                for t in range(HT):
                    pe.wait(ready[t] if t < len(ready) else ready[-1])
                    m = pe.do(T.transpose, 
                        b.ap[:, t * P:(t + 1) * P], src[:, t, c * P:(c + 1) * P], ident[:, :],
                        signal=t == HT - 1)
                b.ready = [m]
                banks.append(b)
            return banks

        def send_stack(stage, stack):
            sp.wait(stage.ready)
            stack.ready = []
            hi = stage.ap.bitcast(F32)
            st = stack.ap.bitcast(F32)
            for r in range(4):
                for part, row in ((0, 0), (0, 32), (1, 64)):
                    stack.ready.append(dma.copy(st[row:row + 32, r::4, :],
                                                hi[32 * r:32 * r + 32, part, :, :]))
            stage.free = list(stack.ready)

        def split_keys(raw, stack, rows, scale):
            marks = []
            for n in range(0, NK, NK // 4):
                part = slice(n, n + NK // 4)
                act.wait(raw.ready)
                m = act.do(A.activation, stack.ap[0:rows, part, :], raw.ap[0:rows, part, :], ACT.Copy,
                           scale=scale)
                dve.wait(m)
                marks += [m, dve.do(V.scalar_tensor_tensor, stack.ap[32:64, part, :],
                                    raw.ap[32:64, part, :], scale,
                                    stack.ap[32:64, part, :].bitcast(F32), ALU.mult, ALU.subtract)]
                yield
            raw.free = stack.ready = marks

        def key_scores(chunk, rows, bank_slot, keys, stack, g):
            b = bank_slot
            pe.wait(keys.ready, stack.ready)
            if chunk < 4:
                head = 4 * g + chunk
                m = pe.do(T.matmul, b.ap, keys.ap[0:rows, head, :],
                                             stack.ap[0:rows, head // 2, :], start=True, stop=True)
            else:
                for s in range(2):
                    pair = 2 * g + s
                    m = pe.do(T.matmul, 
                        b.ap, keys.ap[0:rows, HEADS + pair, :], stack.ap[0:rows, pair, :],
                        start=s == 0, stop=s == 1, signal=s == 1)
            b.ready = [m]

        def weigh_values(g, weights, values, o_bank, turned):
            pe.wait(values.ready, o_bank.free)
            for part in range(2):
                for j in range(4):
                    w = weights[j] if part == 0 else weights[4]
                    pe.wait(w.ready)
                    m = pe.do(T.matmul, 
                        o_bank.ap[32 * j:32 * j + 32, :], values.ap[:, part, 4 * g + j, :], w.ap,
                        start=part == 0, stop=part == 1, tile_position=(0, 32 * j),
                        signal=j == 3)
            for w in weights:
                w.free = [m]
            act.wait(m)
            m2 = act.do(A.activation, turned.ap[:, g, :], o_bank.ap, ACT.Copy)
            o_bank.free = [m2]
            turned.ready = [m2]
            return m

        def normalize_heads(t, turned, misc, sums, dst):
            b = misc.take(pe)
            pe.wait(turned.ready)
            for g in range(GROUPS):
                m = pe.do(T.transpose, b.ap[:, g * P:(g + 1) * P],
                                                     turned.ap[:, g, t * P:(t + 1) * P], ident[:, :],
                          signal=g == GROUPS - 1)
            s = sums.take(dve)
            view = b.ap.rearrange("p (h w) -> p h w", w=32)
            dve.wait(m)
            m2 = dve.do(V.reciprocal, s.ap, view[:, :, HD])
            dve.wait(m2)
            m3 = dve.do(V.tensor_tensor, 
                dst.rearrange("p (h d) -> p h d", d=HD), view[:, :, 0:HD],
                s.ap.unsqueeze(2).to_broadcast([P, HEADS, HD]), ALU.mult)
            b.free = s.free = [m3]
            return m, m3

        sgate = sb("sgate", [P, TILES], F32)
        w_con = sb("w_con_fused", [P, HB, DIM], F32)
        positions = w_con[:, :, :].rearrange("p a n -> p (a n)").bitcast(BF16)
        pos_a, pos_b = (positions[:, i * TILES * EXPERTS:(i + 1) * TILES * EXPERTS].rearrange(
            "p (t n) -> p t n", n=EXPERTS) for i in range(2))

        scope = ExitStack()
        with scope:
            s0 = lambda n, s, d: sb(n, s, d, scope)
            wq, wo, wv = (s0(f"w{n}", [P, CD, DIM], F32) for n in "qov")
            wk_ring = Ring([s0(f"wk_stack{i}", [P, CD, 4, STACK], F32)[:, :, :, :] for i in range(2)])
            bk = s0("bk_stack", [STACK, HEADS], F32)
            bq = s0("bq", [P, CD], F32)
            bv = s0("bv", [P, DIM], F32)
            gate_w = s0("gate_w", [P, CD, EXPERTS + 1], F32)
            ctx_t = s0("ctx_t", [P, CD, 3 * P], F32)
            upper = s0("upper", [P, P], BF16)
            ones = s0("ones", [P, P], BF16)
            zeros = s0("zeros", [P, 1, DIM], F32)
            masks = s0("masks", [P, HT, EXPERTS], BF16)
            before = s0("mask_sums", [P, 2, EXPERTS], BF16)
            k_raw = Slot(s0("k_raw0", [STACK, NK, P], F32)[:, :, :])
            keys_ring = Ring([s0(f"k_stack{i}", [P, NK, P], F32R)[:, :, :] for i in range(2)])
            vals_ring = Ring([s0(f"values{i}", [P, 2, HEADS, 32], F32)[:, :, :, :] for i in range(2)])
            q_stacks = Ring([s0(f"q_stack{i}", [P, PAIRS, HALF], F32R)[:, :, :] for i in range(2)])
            q_stage = Ring([s0("q_stage", [P, 2, CD, HALF], F32R)[:, :, :, :]])
            weights = Ring([s0(f"weights{i}", [P, HALF], F32)[:, :] for i in range(9)])
            turned_ring = Ring([s0(f"turned{i}", [P, GROUPS, HALF], F32)[:, :, :] for i in range(2)])
            normed = Ring([s0("normed", [P, HT, DIM], F32)[:, :, :]])
            rows = Ring([s0("rows", [P, HT, ROW], F32)[:, :, :]])
            feats = Ring([s0(f"feats{i}", [P, CD, HALF], F32)[:, :, :] for i in range(2)])
            att = Ring([s0("att", [P, HT, DIM], F32)[:, :, :]])
            sums = Ring([s0(f"sums{i}", [P, HEADS], F32)[:, :] for i in range(2)])
            probs = Ring([s0(f"probs{i}", [P, HT, EXPERTS], F32)[:, :, :] for i in range(1)])
            small = Ring([s0(f"small{i}", [P, 8, HT], F32)[:, :, :] for i in range(2)])
            top = Ring([s0(f"top{i}", [P, HT, TOPK], F32)[:, :, :] for i in range(2)])
            picked = Ring([s0(f"picked{i}", [P, HT, EXPERTS], F32)[:, :, :] for i in range(1)])
            posf = Ring([s0("pos_f", [P, HT, EXPERTS], F32)[:, :, :]])
            posi = Ring([s0("pos_i", [P, 2, HT, EXPERTS], I32)[:, :, :, :]])

            m_w = {}
            for name, t in (("bk", bk[:, :]),
                            ("wv", wv[:, :, :]), ("bv", bv[:, :]), ("wq", wq[:, :, :]), ("bq", bq[:, :]),
                            ("wo", wo[:, :, :]), ("gate_w", gate_w[:, :, :]), ("upper", upper[:, :]),
                            ):
                m_w[name] = dma.copy(t, D[name])
            m = pool.do(G.memset, zeros[:, :, :], 0.0)
            pool.wait(m)
            m_sums = [gdma.start(G.dma_start, t.rearrange("(p r) f -> p r f", p=P),
                                 zeros[:, :, :].to_broadcast([P, TILES + 1, DIM])) for t in sum_dram]
            m_ones = pool.do(G.memset, ones[:, :], 1.0)
            m_before = pool.do(G.memset, before[:, :, :], 0.0)
            sum_ready = [m_before]
            m_z = pool.do(G.memset, k_raw.ap, 0.0)
            k_raw.free = [m_z]

            def clear_values(ring):
                for v in ring.slots:
                    a = [pool.do(G.memset, v.ap[:, 1, :, :], 0.0),
                         pool.do(G.memset, v.ap[:, 0, :, HD:32], 1.0)]
                    for j in range(4):
                        pool.wait(a)
                        a.append(pool.do(G.memset, 
                            v.ap[32 * j:32 * j + REST, 1, j::4, HD:32], 1.0))
                    pool.wait(a)
                    v.free = a

            clear_values(vals_ring)

            misc = use(bank[6:8])
            s_banks = use(bank[0:5])
            o_bank = bank[5]
            keys_of, vals_of, stack_of, turned_of = {}, {}, {}, {}
            ctx_slot = Slot(ctx_t[:, :, :])

            def prepare_keys(b, ahead=4):
                sp.wait(ctx_slot.free)
                m_ctx = dma.copy(ctx_t[:, :, :], D["ctx_t"][b])
                coming = deque()

                def load_wk(n):
                    wk = wk_ring.take(sp)
                    wk.ready = [dma.copy(wk.ap, D["wk"][n])]
                    coming.append(wk)

                load_wk(0)
                load_wk(1)
                for _ in range(ahead):
                    yield
                pe.wait(m_ctx)
                dve.wait(k_raw.free, m_w["bk"])
                k_raw.free = None
                k_raw.ready = []
                for p in range(PAIRS):
                    if p % 2 == 0:
                        wk = coming.popleft()
                    pe.wait(wk.ready)
                    bk_slot = misc.take(pe)
                    for a in range(2):
                        for c in range(CD):
                            m = pe.do(T.matmul, 
                                bk_slot.ap[0:STACK, a * KEYS:(a + 1) * KEYS], wk.ap[:, c, 2 * (p % 2) + a, :],
                                ctx_t[:, c, 0:KEYS], start=c == 0, stop=c == CD - 1,
                                signal=a == 1 and c == CD - 1)
                    if p % 2:
                        wk.free = [m]
                        if p // 2 + 2 < PAIRS // 2:
                            load_wk(p // 2 + 2)
                    view = bk_slot.ap[0:STACK, 0:2 * KEYS].rearrange("p (a k) -> p a k", a=2)
                    bias = bk[:, 2 * p:2 * p + 2].unsqueeze(2)
                    s = p % 2
                    dve.wait(m)
                    k_raw.ready.append(dve.do(V.tensor_tensor, 
                        k_raw.ap[:, 2 * p:2 * p + 2, :], view[:, :, 0:P],
                        bias.to_broadcast([STACK, 2, P]), ALU.add))
                    k_raw.ready.append(dve.do(V.tensor_tensor, 
                        k_raw.ap[:, HEADS + p, :].rearrange("p (j k) -> p j k", k=32)[:, 2 * s:2 * s + 2, 0:REST],
                        view[:, :, P:KEYS], bias.to_broadcast([STACK, 2, REST]), ALU.add))
                    bk_slot.free = k_raw.ready[-1:]
                    yield
                k_stack = keys_ring.take(act, dve)
                yield from split_keys(k_raw, k_stack, STACK, 0.25)
                keys_of[b] = k_stack
                yield
                v_slot = misc.take(pe)
                values = vals_ring.take(dve)
                pe.wait(m_w["wv"])
                for part in range(2):
                    for c in range(CD):
                        m = pe.do(T.matmul, 
                            v_slot.ap[:, part * DIM:(part + 1) * DIM],
                            ctx_t[:, c, 2 * part * P:(2 * part + 1) * P], wv[:, c, :],
                            start=c == 0, stop=c == CD - 1, signal=part == 1 and c == CD - 1)
                ctx_slot.free = [m]
                dve.wait(m, m_w["bv"])
                values.ready = [dve.do(V.tensor_tensor, 
                    values.ap[:, 0, :, 0:HD], v_slot.ap[:, 0:DIM].rearrange("p (h d) -> p h d", d=HD),
                    bv[:, :].rearrange("p (h d) -> p h d", d=HD), ALU.add)]
                for j in range(4):
                    r = slice(32 * j, 32 * j + REST)
                    values.ready.append(dve.do(V.tensor_tensor, 
                        values.ap[r, 1, j::4, 0:HD],
                        v_slot.ap[r, DIM:2 * DIM].rearrange("p (h d) -> p h d", d=HD)[:, j::4, :],
                        bv[r, :].rearrange("p (h d) -> p h d", d=HD)[:, j::4, :], ALU.add))
                v_slot.free = values.ready[-1:]
                vals_of[b] = values
                yield

            def prepare_queries(h):
                n = normed.take(dve)
                yield from layernorm(h, n.ap, n)
                pool.wait(n.ready[-1], m_batt)
                m = pool.do(G.tensor_tensor, 
                    x[:, HT * h:HT * h + HT, :], x[:, HT * h:HT * h + HT, :],
                    b_att[:, :].unsqueeze(1).to_broadcast([P, HT, DIM]), ALU.add)
                x_ready[h] = [m]
                yield
                pe.wait(m_ident)
                f = feats.take(act)
                for c, b in enumerate(turn_half(n.ap, n.ready, misc)):
                    act.wait(b.ready)
                    m = act.do(A.activation, f.ap[:, c, :], b.ap, ACT.Copy)
                    f.ready.append(m)
                    b.free = [m]
                    n.free = list(b.ready)
                yield
                stage = q_stage.take(act, dve)
                for mo in range(CD):
                    b = misc.take(pe)
                    pe.wait(f.ready, m_w["wq"])
                    for c in range(CD):
                        m = pe.do(T.matmul, 
                            b.ap, wq[:, c, mo * P:(mo + 1) * P], f.ap[:, c, :],
                            start=c == 0, stop=c == CD - 1, signal=c == CD - 1)
                    act.wait(m, m_w["bq"])
                    m1 = act.do(A.activation, 
                        stage.ap[:, 0, mo, :], b.ap, ACT.Identity, bias=bq[:, mo:mo + 1])
                    dve.wait(m1)
                    m2 = dve.do(V.scalar_tensor_tensor, 
                        stage.ap[:, 1, mo, :], b.ap, bq[:, mo:mo + 1],
                        stage.ap[:, 0, mo, :].bitcast(F32), ALU.add, ALU.subtract)
                    b.free = [m2]
                    stage.ready += [m1, m2]
                    yield
                f.free = [m]
                stack = q_stacks.take(sp)
                send_stack(stage, stack)
                stack_of[h] = stack
                yield

            def after_attention(h, turned):
                a = att.take(dve)
                for t in range(HT):
                    m, m3 = normalize_heads(t, turned, misc, sums, a.ap[:, t, :])
                    a.ready.append(m3)
                    yield
                turned.free = [m]
                f = feats.take(act)
                for c, b in enumerate(turn_half(a.ap, a.ready, misc)):
                    act.wait(b.ready)
                    m = act.do(A.activation, f.ap[:, c, :], b.ap, ACT.Copy)
                    f.ready.append(m)
                    b.free = [m]
                    a.free = list(b.ready)
                yield
                x_marks = []
                for two in range(HT // 2):
                    b = misc.take(pe)
                    pe.wait(f.ready, m_w["wo"])
                    for i in range(2):
                        for c in range(CD):
                            t = 2 * two + i
                            m = pe.do(T.matmul, 
                                b.ap[:, i * DIM:(i + 1) * DIM], f.ap[:, c, t * P:(t + 1) * P],
                                wo[:, c, :], start=c == 0, stop=c == CD - 1,
                                signal=i == 1 and c == CD - 1)
                    dve.wait(m, x_ready[h])
                    xs = x[:, HT * h + 2 * two:HT * h + 2 * two + 2, :].rearrange("p i f -> p (i f)")
                    m2 = dve.do(V.scalar_tensor_tensor, 
                        xs, b.ap, tg[:, 0:1], xs, ALU.mult, ALU.add)
                    b.free = [m2]
                    x_marks.append(m2)
                    yield
                f.free = [m]
                x_ready[h] = x_marks
                r = rows.take(dve)
                yield from layernorm(h, r.ap[:, :, 0:DIM], r)
                f = feats.take(act)
                for c, b in enumerate(turn_half(r.ap, r.ready, misc)):
                    act.wait(b.ready)
                    m = act.do(A.activation, f.ap[:, c, :], b.ap, ACT.Copy)
                    f.ready.append(m)
                    b.free = [m]
                    turned_rows = list(b.ready)
                yield
                sp.wait(f.ready)
                m_feats = dma.copy(feats_dram[h].rearrange("p (c n) -> p c n", c=CD), f.ap)
                NL = EXPERTS + 1
                b = misc.take(pe)
                pe.wait(f.ready, m_w["gate_w"])
                for t in range(HT):
                    for c in range(CD):
                        m = pe.do(T.matmul, 
                            b.ap[:, t * NL:(t + 1) * NL], f.ap[:, c, t * P:(t + 1) * P],
                            gate_w[:, c, :], start=c == 0, stop=c == CD - 1,
                            signal=t == HT - 1 and c == CD - 1)
                f.free = [m, m_feats]
                logits = b.ap[:, 0:HT * NL].rearrange("p (t n) -> p t n", n=NL)
                pr, sm, tp, pk = probs.take(dve), small.take(dve), top.take(dve), picked.take(dve)
                dve.wait(m)
                m = dve.do(V.tensor_reduce, sm.ap[:, 0, :], logits[:, :, 0:EXPERTS], AX.X, ALU.max)
                dve.wait(m)
                m = dve.do(V.tensor_tensor, pr.ap, logits[:, :, 0:EXPERTS],
                           sm.ap[:, 0, :].unsqueeze(2).to_broadcast([P, HT, EXPERTS]), ALU.subtract)
                act.wait(m)
                m1 = act.do(A.activation, pr.ap, pr.ap, ACT.Exp)
                m2 = act.do(A.activation, sm.ap[:, 1, :], logits[:, :, EXPERTS], ACT.Exp, scale=-1.0)
                b.free = [m, m2]
                yield
                dve.wait(m1, m2)
                ma = dve.do(V.tensor_reduce, sm.ap[:, 2, :], pr.ap, AX.X, ALU.add)
                mb = dve.do(V.tensor_scalar, sm.ap[:, 3, :], sm.ap[:, 1, :], 1.0, 0.0, ALU.add, ALU.add)
                dve.wait(ma, mb)
                ma = dve.do(V.reciprocal, sm.ap[:, 4:6, :].rearrange("p a t -> p (a t)"),
                                                   sm.ap[:, 2:4, :].rearrange("p a t -> p (a t)"))
                dve.wait(ma)
                m_sg = dve.do(V.tensor_scalar, sgate[:, HT * h:HT * h + HT], sm.ap[:, 5, :],
                                                        tg[:, 1:2], None, ALU.mult)
                m = dve.do(V.tensor_tensor, pr.ap, pr.ap,
                           sm.ap[:, 4, :].unsqueeze(2).to_broadcast([P, HT, EXPERTS]), ALU.mult)
                dve.wait(m)
                ms = [dve.do(V.max, tp.ap[:, t, :], pr.ap[:, t, :]) for t in range(HT)]
                yield
                for t in range(HT):
                    dve.wait(ms[t])
                    m = dve.do(V.match_replace, pk.ap[:, t, :], tp.ap[:, t, :],
                                                              pr.ap[:, t, :], -1.0)
                ma = dve.do(V.tensor_reduce, sm.ap[:, 6, :], tp.ap, AX.X, ALU.add)
                dve.wait(m, ma, mask_free)
                m_mask = dve.do(V.tensor_scalar, masks[:, :, :], pk.ap, 0.0, None, ALU.is_lt)
                ma = dve.do(V.reciprocal, sm.ap[:, 7, :], sm.ap[:, 6, :])
                dve.wait(ma)
                ma = dve.do(V.tensor_scalar, sm.ap[:, 7, :], sm.ap[:, 7, :], tg[:, 1:2], None, ALU.mult)
                dve.wait(ma)
                m = dve.do(V.tensor_tensor, r.ap[:, :, DIM:ROW], pr.ap,
                           sm.ap[:, 7, :].unsqueeze(2).to_broadcast([P, HT, EXPERTS]), ALU.mult)
                pr.free = sm.free = tp.free = pk.free = [m]
                sp.wait(m, r.ready)
                m_rows = dma.copy(rows_dram[HALF * h:HALF * (h + 1), :].rearrange("(t p) n -> p t n", p=P), r.ap)
                r.free = [m_rows] + turned_rows
                yield
                yield
                yield
                b = misc.take(pe)
                pe.wait(m_mask, m_w["upper"], m_ones)
                pe.wait(sum_ready)
                old, new = before[:, h % 2, :], before[:, (h + 1) % 2, :]
                for t in range(HT):
                    earlier = [old] + [masks[:, u, :] for u in range(t)]
                    here = b.ap[:, t * EXPERTS:(t + 1) * EXPERTS]
                    pe.do(T.matmul, here, upper[:, :], masks[:, t, :], start=True, stop=False,
                          signal=False)
                    for n, mask in enumerate(earlier):
                        m = pe.do(T.matmul, here, ones[:, :], mask, start=False, stop=n == t,
                                  signal=n == t and t == HT - 1)
                for t in range(HT):
                    dve.wait(sum_ready)
                    sum_ready[:] = [dve.do(V.tensor_tensor, new, old if t == 0 else new,
                                           masks[:, t, :], ALU.add)]
                counts = b.ap[:, 0:HT * EXPERTS].rearrange("p (t n) -> p t n", n=EXPERTS)
                pf, pi = posf.take(dve), posi.take(dve)
                FAR = 4096.0
                dve.wait(m)
                m = dve.do(V.scalar_tensor_tensor, pf.ap, masks[:, :, :], -FAR, counts, ALU.mult, ALU.add)
                mask_free[:] = [m]
                b.free = [m]
                dve.wait(m)
                m = dve.do(V.tensor_scalar, pf.ap, pf.ap, FAR, None, ALU.add)
                dve.wait(m)
                ma = dve.do(V.tensor_copy, pi.ap[:, 0, :, :], pf.ap)
                pf.free = [ma]
                dve.wait(ma)
                mb = dve.do(V.tensor_scalar, pi.ap[:, 1, :, :], pi.ap[:, 0, :, :], 4, None,
                                                      ALU.logical_shift_right)
                dve.wait(mb)
                mc = dve.do(V.tensor_scalar, pi.ap[:, 0, :, :], pi.ap[:, 0, :, :], NB - 1, None,
                                                      ALU.bitwise_and)
                dve.wait(mc)
                sl = slice(HT * h, HT * h + HT)
                md = dve.do(V.tensor_copy, pos_a[:, sl, :], pi.ap[:, 1, :, :])
                me = dve.do(V.tensor_copy, pos_b[:, sl, :], pi.ap[:, 0, :, :])
                pos_ready.extend([md, me])
                pi.free = [me]
                yield

            mask_free, pos_ready = [], []
            fg = Background()
            for g_ in (prepare_keys(0), prepare_queries(0)):
                fg.add(g_)
            fg.drain()
            early, late = Background(), Background()
            later = {}
            units = [(h, g, j) for h in range(HALVES) for g in range(GROUPS) for j in range(5)]
            chunks_of, needed = {}, {}

            def start_scores(n):
                h, g, j = units[n]
                if (g, j) == (0, 0):
                    for work in needed.pop(h, []):
                        early.finish(work)
                    late.drain()
                    turned_of[h] = turned_ring.take(act)
                    if h + 1 < HALVES:
                        needed.setdefault(h + 1, []).append(early.add(prepare_queries(h + 1)))
                    if h % 2 == 0 and h + 2 < HALVES:
                        needed[h + 2] = [early.add(prepare_keys(h // 2 + 1))]
                stack, keys = stack_of[h], keys_of[h // 2]
                b = s_banks.take(pe)
                key_scores(j, STACK, b, keys, stack, g)
                if (g, j) == (GROUPS - 1, 4):
                    stack.free = list(b.ready)
                    if h % 2 == 1:
                        keys.free = list(b.ready)
                return b

            def finish_weights(n, b, w):
                dve.wait(w.log)
                w.ready = [dve.do(V.scalar_tensor_tensor, w.ap, b.ap, 1.0, w.ap, ALU.add, ALU.max)]
                b.free = w.ready

            def weigh(n):
                h, g, _ = units[n]
                m = weigh_values(g, chunks_of.pop((h, g)), vals_of[h // 2], o_bank, turned_of[h])
                if g == GROUPS - 1:
                    if h % 2 == 1:
                        vals_of[h // 2].free = [m]
                    late.add(after_attention(h, turned_of[h]))

            b = start_scores(0)
            logs, maxes = deque(), deque()
            for n in range(len(units) + 4):
                live = None
                if logs:
                    live, m, w, sign = logs.popleft()
                    act.wait(m)
                    m_log = act.do(A.activation, w.ap, w.ap, ACT.Ln, bias=1.0, scale=sign)
                if n < len(units):
                    h, g, j = units[n]
                    w_new = weights.take(act, dve)
                    chunks_of.setdefault((h, g), []).append(w_new)
                    if j in ON_ACT:
                        act.wait(b.ready)
                        m = act.do(A.activation, w_new.ap, b.ap, ACT.Relu, scale=-1.0)
                    else:
                        dve.wait(b.ready)
                        m = dve.do(V.tensor_scalar, w_new.ap, b.ap, 0.0, None, ALU.min)
                    logs.append((b, m, w_new, 1.0 if j in ON_ACT else -1.0))
                    if j == 4:
                        later[n + 3] = n
                if live:
                    act.wait(m_log)
                    w.log = act.do(A.activation, w.ap, w.ap, ACT.Exp, scale=-1.0)
                    maxes.append((n + 1, live, w))
                if maxes and maxes[0][0] <= n:
                    finish_weights(*maxes.popleft())
                if n + 1 < len(units):
                    b = start_scores(n + 1)
                if n in later:
                    weigh(later.pop(n))
                early.step()
                late.step()
            late.drain()

        def barrier():
            marks = [(l.sem, l.count) for l in lanes if l.count]
            marks += [m for d in (dma, gdma) for m in d.last if m]
            for l in lanes:
                l.wait(marks)

        if stop == "L0":
            sp.wait([x_ready[h] for h in range(HALVES)])

        barrier()

        w_up = sb("w_up_fused", [P, CD, HID], F32)
        hid_bias = sb("hidden_bias", [P, HB], F32)
        b_out = sb("bias_out", [P, DIM], F32)

        scope = ExitStack()
        with scope:
            s1 = lambda n, s, d: sb(n, s, d, scope)
            a_iota = s1("a_iota", [P, 4, NA, EG], BF16)
            b_iota = s1("b_iota", [P, NB, EXPERTS], BF16)
            lane_no = s1("lane_no", [P, 1], F32)
            spare_row = s1("spare_row", [P, 1], F32)
            diag = s1("diag", [P, NB, EG], F32)
            hot_a = Ring([s1(f"hot_a{i}", [P, 3, 4, NA, EG], BF16)[:, :, :, :, :] for i in range(3)])
            hot_b = Ring([s1(f"hot_b{i}", [P, NB, EXPERTS], BF16)[:, :, :] for i in range(3)])
            lists = s1("lists", [P, 4, NB, EG], F32)
            lists_b = s1("lists_b", [P, 4, NB], F32)
            by_expert = s1("by_expert", [EXPERTS, P], F32)
            tokens = s1("tokens", [P, EXPERTS], U32)
            sum_rows = s1("sum_rows", [P, EXPERTS], U32)
            listed = s1("listed", [P, 3, EXPERTS], F32)
            w_ring = Ring([s1(f"expert_w{i}", [P, 3, DIM], F32)[:, :, :] for i in range(8)])
            got_ring = Ring([s1(f"got{i}", [P, ROW], F32)[:, :] for i in range(6)])
            got_t = Ring([s1(f"got_t{i}", [P, CD, P], F32)[:, :, :] for i in range(3)])
            silu_ring = Ring([s1(f"silu{i}", [P, P], F32)[:, :] for i in range(2)])
            inner_ring = Ring([s1(f"inner{i}", [P, P], F32)[:, :] for i in range(3)])
            made_ring = Ring([s1(f"made{i}", [P, DIM], F32)[:, :] for i in range(4)])
            w_sgu = s1("w_shared_up", [P, CD, 2 * SHARED], F32)
            w_sd = s1("w_shared_down", [P, SHARED // P, DIM], F32)
            feats = Ring([s1(f"feats_m{i}", [P, CD, HALF], F32)[:, :, :] for i in range(2)])
            s_silu = Ring([s1(f"shared_silu{i}", [P, HALF], F32)[:, :] for i in range(2)])
            s_inner = Ring([s1(f"shared_inner{i}", [P, SHARED // P, HALF], F32)[:, :, :] for i in range(2)])
            bf_u = s1("butterfly_u", [P, HB, DIM + 1], F32)
            bf_v = s1("butterfly_v", [P, HB, DIM + 1], F32)
            swaps = s1("swaps", [P, INSIDE, P], F32)
            taps = s1("taps", [P, 4, STAGES, HB], F32)
            up_bias = s1("up_bias", [P, HB], F32)
            down_bias = s1("down_bias", [P, DIM], F32)
            stage_m = Ring([s1(f"stage_m{i}", [P, P], F32)[:, :] for i in range(4)])
            part_ring = Ring([s1(f"stage_p{i}", [P, P], F32)[:, :] for i in range(2)])

            m_c = {n: dma.copy(t, D[n]) for n, t in (
                ("a_iota", a_iota[:, :, :, :]), ("b_iota", b_iota[:, :, :]), ("lane_no", lane_no[:, :]),
                ("spare_row", spare_row[:, :]),
                ("diag", diag[:, :, :]), ("w_sgu", w_sgu[:, :, :]), ("w_sd", w_sd[:, :, :]),
                ("w_exp", bf_u[:, :, :]), ("swaps", swaps[:, :, :]), ("taps", taps[:, :, :, :]),
                ("up_bias", up_bias[:, :]), ("b_con", b_out[:, :]), ("down_bias", down_bias[:, :]))}
            experts_w = {}

            def load_expert(e_):
                w = w_ring.take(sp)
                w.ready = [dma.copy(w.ap, D["expert_w"][e_])]
                experts_w[e_] = w

            for e_ in range(3):
                load_expert(e_)

            back = Background()
            s_ring = use(bank[6:8])

            def shared_expert(h):
                f = feats.take(sp)
                f.ready = [dma.copy(f.ap, feats_dram[h].rearrange("p (c n) -> p c n", c=CD))]
                inner = s_inner.take(dve)
                yield
                for k in range(SHARED // P):
                    got = []
                    for part in range(2):
                        b = s_ring.take(pe)
                        pe.wait(f.ready, m_c["w_sgu"])
                        for c in range(CD):
                            m = pe.do(T.matmul, b.ap,
                                      w_sgu[:, c, part * SHARED + k * P:part * SHARED + (k + 1) * P],
                                      f.ap[:, c, :], start=c == 0, stop=c == CD - 1, signal=c == CD - 1)
                        got.append((b, m))
                    (bg, mg), (bu, mu) = got
                    sl = s_silu.take(act)
                    act.wait(mg)
                    m1 = act.do(A.activation, sl.ap, bg.ap, ACT.Silu)
                    bg.free = [m1]
                    dve.wait(m1, mu)
                    m2 = dve.do(V.tensor_tensor, inner.ap[:, k, :], sl.ap, bu.ap, ALU.mult)
                    bu.free = sl.free = [m2]
                    inner.ready.append(m2)
                    yield
                f.free = [mu]
                marks = []
                for two in range(HT // 2):
                    b = s_ring.take(pe)
                    pe.wait(inner.ready, m_c["w_sd"])
                    for i in range(2):
                        t = 2 * two + i
                        for k in range(SHARED // P):
                            m = pe.do(T.matmul, b.ap[:, i * DIM:(i + 1) * DIM],
                                      inner.ap[:, k, t * P:(t + 1) * P], w_sd[:, k, :],
                                      start=k == 0, stop=k == SHARED // P - 1,
                                      signal=i == 1 and k == SHARED // P - 1)
                    dve.wait(m, x_ready[h])
                    for i in range(2):
                        t = HT * h + 2 * two + i
                        marks.append(dve.do(V.scalar_tensor_tensor, x[:, t, :], b.ap[:, i * DIM:(i + 1) * DIM],
                                            sgate[:, t:t + 1], x[:, t, :], ALU.mult, ALU.add))
                    b.free = [marks[-1]]
                    yield
                inner.free = [m]
                x_ready[h] = marks

            f_ring = use(bank[4:6])

            def stage_matrix(which, s, k):
                mm, pp = stage_m.take(dve), part_ring.take(act)
                own, other = taps[:, 2 * which, s, k:k + 1], taps[:, 2 * which + 1, s, k:k + 1]
                act.wait(m_ident, m_c["taps"])
                ma = act.do(A.activation, pp.ap, ident[:, :], ACT.Copy, scale=own)
                dve.wait(ma, m_c["taps"], m_c["swaps"])
                mb = dve.do(V.scalar_tensor_tensor, mm.ap, swaps[:, s, :], other, pp.ap, ALU.mult, ALU.add)
                pp.free = [mb]
                mm.ready = [mb]
                return mm

            def inside(buf, width, ready, which, stages):
                order = [(s, k) for s in stages for k in range(HB)]
                made = deque(stage_matrix(which, s, k) for s, k in order[:2])
                for n, (s, k) in enumerate(order):
                    if n + 2 < len(order):
                        made.append(stage_matrix(which, *order[n + 2]))
                    mm = made.popleft()
                    b = f_ring.take(pe)
                    pe.wait(mm.ready, ready[k])
                    mc = pe.do(T.matmul, b.ap[:, 0:width], mm.ap, buf[:, k, 0:width], start=True, stop=True)
                    mm.free = [mc]
                    act.wait(mc)
                    md = act.do(A.activation, buf[:, k, 0:width], b.ap[:, 0:width], ACT.Copy)
                    b.free = ready[k] = [md]
                    yield

            def across(src, dst, width, ready, which, s):
                new = []
                act.wait(ready)
                for k in range(HB):
                    o = k ^ (1 << (s - INSIDE))
                    own = taps[:, 2 * which, s, k:k + 1]
                    other = taps[:, 2 * which + 1, s, (o if which else k):(o if which else k) + 1]
                    ma = act.do(A.activation, dst[:, k, 0:width], src[:, k, 0:width], ACT.Copy, scale=own)
                    dve.wait(ma)
                    mb = dve.do(V.scalar_tensor_tensor, dst[:, k, 0:width], src[:, o, 0:width], other,
                                dst[:, k, 0:width], ALU.mult, ALU.add)
                    new.append([mb])
                ready[:] = new

            def fuse():
                ready = [[m_c["w_exp"]] for _ in range(HB)]
                yield from inside(bf_u, DIM + 1, ready, 0, range(INSIDE))
                bufs = [bf_u, bf_v]
                for s in range(INSIDE, STAGES):
                    across(bufs[0], bufs[1], DIM + 1, ready, 0, s)
                    bufs.reverse()
                    yield
                last = bufs[0]
                marks = []
                for c in range(CD):
                    for q in range(HB // 4):
                        b = f_ring.take(pe)
                        for i in range(4):
                            pe.wait(ready[4 * q + i])
                            m = pe.do(T.transpose, b.ap[:, i * P:(i + 1) * P],
                                      last[:, 4 * q + i, c * P:(c + 1) * P], ident[:, :], signal=i == 3)
                        act.wait(m)
                        m2 = act.do(A.activation, w_up[:, c, 4 * q * P:4 * (q + 1) * P], b.ap, ACT.Copy)
                        b.free = [m2]
                        marks.append(m)
                        yield
                dve.wait(ready, m_c["up_bias"])
                m = dve.do(V.tensor_tensor, hid_bias[:, :], last[:, :, DIM], up_bias[:, :], ALU.add)
                sp.wait(marks, m)
                m = dma.copy(bf_u[:, :, 0:DIM], D["w_con"])
                ready = [[m] for _ in range(HB)]
                bufs = [bf_u, w_con]
                for s in reversed(range(INSIDE, STAGES)):
                    across(bufs[0], bufs[1], DIM, ready, 1, s)
                    bufs.reverse()
                    yield
                yield from inside(w_con, DIM, ready, 1, range(INSIDE - 1, -1, -1))
                dve.wait(m_c["b_con"], m_c["down_bias"])
                m = dve.do(V.tensor_tensor, b_out[:, :], b_out[:, :], down_bias[:, :], ALU.add)
                dve.wait(m)
                dve.do(V.tensor_scalar, b_out[:, :], b_out[:, :], tg[:, 3:4], None, ALU.mult)
                yield

            for h in range(HALVES):
                back.add(shared_expert(h))
            fusing = Background()
            fusing.add(fuse())

            hot_banks = bank[0:4]

            def one_hots(i):
                ha, hb = hot_a.take(dve, act), hot_b.take(dve)
                dve.wait(m_c["a_iota"], m_c["b_iota"], pos_ready)
                m = dve.do(V.tensor_tensor, ha.ap[:, 0, :, :, :], a_iota[:, :, :, :],
                           pos_a[:, i, :].rearrange("p (g e) -> p g e", e=EG).unsqueeze(2).to_broadcast(
                               [P, 4, NA, EG]), ALU.is_equal)
                mb = dve.do(V.tensor_tensor, hb.ap, b_iota[:, :, :],
                            pos_b[:, i, :].unsqueeze(1).to_broadcast([P, NB, EXPERTS]), ALU.is_equal)
                act.wait(m, m_c["lane_no"])
                act.do(A.activation, ha.ap[:, 1, :, :, :], ha.ap[:, 0, :, :, :], ACT.Copy,
                       scale=lane_no[:, 0:1])
                ma = act.do(A.activation, ha.ap[:, 2, :, :, :], ha.ap[:, 0, :, :, :], ACT.Copy,
                            scale=float(P * i))
                ha.ready, hb.ready = [ma], [mb]
                return ha, hb

            hots = deque([one_hots(0)])
            for i in range(TILES):
                if i + 1 < TILES:
                    hots.append(one_hots(i + 1))
                ha, hb = hots.popleft()
                pe.wait(ha.ready, hb.ready)
                for g in range(4):
                    eg = slice(EG * g, EG * g + EG)
                    if i == 0:
                        pe.wait(hot_banks[g].free)
                    for part in (1, 2):
                        m = pe.do(T.matmul, hot_banks[g].ap[:, 0:NB * EG], ha.ap[:, part, g, :, :],
                                  hb.ap[:, :, eg], start=i == 0 and part == 1,
                                  stop=i == TILES - 1 and part == 2, signal=g == 3 and part == 2)
                ha.free = hb.free = [m]
                m_hot = m
                if i % 2:
                    back.step()
            dve.wait(m_hot, m_c["diag"], m_c["spare_row"])
            parts = []
            for g in range(4):
                parts.append(dve.do(V.tensor_tensor, lists[:, g, :, :],
                                    hot_banks[g].ap[:, 0:NB * EG].rearrange("p (b e) -> p b e", e=EG),
                                    diag[:, :, :], ALU.mult))
                hot_banks[g].free = [parts[-1]]
            dve.wait(parts)
            m = dve.do(V.tensor_reduce, lists_b[:, :, :], lists[:, :, :, :], AX.X, ALU.add)
            sp.wait(m)
            m = dma.copy(list_dram.rearrange("g p b -> p g b"), lists_b[:, :, :])
            sp.wait(m)
            ms = [dma.copy(by_expert[EG * g:EG * g + EG, :].rearrange("e (a b) -> e a b", a=NA),
                           list_dram[g].rearrange("(a e) b -> e a b", a=NA)) for g in range(4)]
            tok_bank = bank[4]
            back.step(3)
            pe.wait(ms, tok_bank.free)
            m = pe.do(T.transpose, tok_bank.ap[:, 0:EXPERTS], by_expert[:, :], ident[0:EXPERTS, 0:EXPERTS])
            dve.wait(m)
            m1 = dve.do(V.tensor_scalar, listed[:, 0, :], tok_bank.ap[:, 0:EXPERTS], -1.0, 0.0, ALU.add, ALU.max)
            m2 = dve.do(V.tensor_scalar, listed[:, 1, :], tok_bank.ap[:, 0:EXPERTS], 0.5, None, ALU.is_lt)
            dve.wait(m1, m2)
            m_tokens = [dve.do(V.tensor_copy, tokens[:, :], listed[:, 0, :])]
            m = dve.do(V.scalar_tensor_tensor, listed[:, 2, :], listed[:, 1, :], spare_row[:, 0:1],
                       listed[:, 0, :], ALU.mult, ALU.add)
            dve.wait(m)
            m_tokens.append(dve.do(V.tensor_copy, sum_rows[:, :], listed[:, 2, :]))
            tok_bank.free = [m2]

            t_banks, h_banks, d_banks = use(bank[0:2]), use(bank[2:3]), use(bank[3:4])
            flow = {}

            def gather(e_):
                got = got_ring.take(pool)
                pool.wait(m_tokens)
                got.ready = [gdma.start(G.indirect_dma_start, got.ap, None, rows_dram,
                                        bass.IndirectOffsetOnAxis(ap=tokens[:, e_:e_ + 1], axis=0),
                                        bounds_check=TOKENS - 1, oob_is_err=False)]
                flow[e_] = {"got": got}

            def turn(e_):
                d = flow[e_]
                b = t_banks.take(pe)
                pe.wait(d["got"].ready)
                for c in range(CD):
                    m = pe.do(T.transpose, b.ap[:, c * P:(c + 1) * P], d["got"].ap[:, c * P:(c + 1) * P],
                              ident[:, :], signal=c == CD - 1)
                d["turned"] = m
                d["t"] = t = got_t.take(act)
                act.wait(m)
                m = act.do(A.activation, t.ap.rearrange("p c n -> p (c n)"), b.ap[:, 0:CD * P], ACT.Copy)
                b.free = t.ready = [m]

            def gate_up(e_):
                d = flow[e_]
                b, w, t = h_banks.take(pe), experts_w[e_], d["t"]
                pe.wait(t.ready, w.ready)
                for part in range(2):
                    for c in range(CD):
                        m = pe.do(T.matmul, b.ap[:, part * P:(part + 1) * P],
                                  w.ap[:, c, part * INNER:(part + 1) * INNER], t.ap[:, c, :],
                                  start=c == 0, stop=c == CD - 1, signal=part == 1 and c == CD - 1)
                t.free = [m]
                sl, inner = silu_ring.take(act), inner_ring.take(dve)
                act.wait(m)
                m1 = act.do(A.activation, sl.ap, b.ap[:, 0:P], ACT.Silu)
                dve.wait(m1)
                m2 = dve.do(V.tensor_tensor, inner.ap, sl.ap, b.ap[:, P:2 * P], ALU.mult)
                b.free = sl.free = inner.ready = [m2]
                d["inner"] = inner

            def down(e_):
                d = flow.pop(e_)
                b, w, inner, got = d_banks.take(pe), experts_w.pop(e_), d["inner"], d["got"]
                pe.wait(inner.ready)
                m = pe.do(T.matmul, b.ap[:, 0:DIM], inner.ap, w.ap[:, 2, :], start=True, stop=True)
                inner.free = w.free = [m]
                made = made_ring.take(dve)
                dve.wait(m, got.ready)
                m = dve.do(V.tensor_scalar, made.ap, b.ap[:, 0:DIM], got.ap[:, DIM + e_:DIM + e_ + 1],
                           None, ALU.mult)
                b.free = [m]
                got.free = [m, d["turned"]]
                pool.wait(m, m_sums[e_ % SUMS])
                m_sums[e_ % SUMS] = gdma.start(
                    G.indirect_dma_start, sum_dram[e_ % SUMS],
                    bass.IndirectOffsetOnAxis(ap=sum_rows[:, e_:e_ + 1], axis=0), made.ap, None,
                    bounds_check=TOKENS + P - 1, oob_is_err=True, compute_op=ALU.add)
                made.free = [m_sums[e_ % SUMS]]

            LAGS = ((gather, 0), (turn, 3), (gate_up, 4), (down, 5))
            for n in range(EXPERTS + LAGS[-1][1]):
                for (work, lag), other in zip(reversed(LAGS), (fusing, back, fusing, None)):
                    if 0 <= n - lag < EXPERTS:
                        work(n - lag)
                    if other:
                        other.step()
                if n + 3 < EXPERTS:
                    load_expert(n + 3)
            back.drain()
            fusing.drain()
        barrier()

        ROWS1 = STACK + 4
        scope = ExitStack()
        with scope:
            s2 = lambda n, s, d: sb(n, s, d, scope)
            k_raw = Slot(s2("k1_raw", [ROWS1, NK, P], F32)[:, :, :])
            keys_ring = Ring([s2(f"k1_stack{i}", [P, NK, P], F32R)[:, :, :] for i in range(2)])
            vals_ring = Ring([s2(f"values1_{i}", [P, 2, HEADS, 32], F32)[:, :, :, :] for i in range(2)])
            q_stacks = Ring([s2(f"q1_stack{i}", [P, PAIRS, HALF], F32R)[:, :, :] for i in range(3)])
            q_stage = Ring([s2("q1_stage", [P, 2, CD, HALF], F32R)[:, :, :, :]])
            weights = Ring([s2(f"weights1_{i}", [P, HALF], F32)[:, :] for i in range(8)])
            turned_ring = Ring([s2("turned1_0", [P, GROUPS, HALF], F32)[:, :, :]])
            normed = Ring([s2("normed1", [P, HT, DIM], F32)[:, :, :]])
            att = Ring([s2("att1", [P, HT, DIM], F32)[:, :, :]])
            sums = Ring([s2(f"sums1_{i}", [P, HEADS], F32)[:, :] for i in range(2)])
            fetched = Ring([s2(f"fetched{i}", [P, SUMS, HT, DIM], F32)[:, :, :, :] for i in range(2)])
            peaks = Ring([s2(f"peaks{i}", [P, HT, HEADS], F32)[:, :, :] for i in range(2)])
            peak_t = Ring([s2(f"peak_t{i}", [HEADS, 2, HALF], F32R)[:, :, :] for i in range(2)])
            clear_values(vals_ring)
            s_banks, misc, o_bank = use(bank[0:3]), use(bank[6:8]), bank[5]
            peak_banks = use(bank[3:5])
            keys_of, vals_of, stack_of, fetched_of = {}, {}, {}, {}

            def fetch_experts(h):
                f = fetched.take(sp)
                sp.wait(m_sums)
                f.ready = [dma.copy(f.ap[:, i, :, :], sum_dram[i][HALF * h:HALF * (h + 1), :].rearrange(
                    "(t p) f -> p t f", p=P)) for i in range(SUMS)]
                fetched_of[h] = f

            def add_experts(h):
                f = fetched_of.pop(h)
                xs = x[:, HT * h:HT * (h + 1), :]
                for i in range(SUMS):
                    pool.wait(f.ready[i], x_ready[h])
                    x_ready[h] = [pool.do(G.tensor_tensor, xs, xs, f.ap[:, i, :, :], ALU.add)]
                    yield
                f.free = x_ready[h]

            def prepare_keys1(b):
                sp.wait(k_raw.free)
                k_raw.ready, k_raw.free = [dma.copy(k_raw.ap, D["k1"][b])], None
                values = vals_ring.take(sp)
                src = D["ctx"][b]
                values.ready = [dma.copy(values.ap[:, 0, :, 0:HD], src[0:P].rearrange("k (h d) -> k h d", d=HD))]
                rest = src[P:KEYS].rearrange("k (g j d) -> k g j d", j=4, d=HD)
                for j in range(4):
                    values.ready.append(dma.copy(values.ap[32 * j:32 * j + REST, 1, j::4, 0:HD], rest[:, :, j, :]))
                vals_of[b] = values
                for _ in range(3):
                    yield
                k_stack = keys_ring.take(act, dve)
                yield from split_keys(k_raw, k_stack, ROWS1, 1.0)
                keys_of[b] = k_stack

            def prepare_queries1(h):
                n = normed.take(dve)
                yield from layernorm(h, n.ap, n)
                stage = q_stage.take(act, dve)
                for c, b in enumerate(turn_half(n.ap, n.ready, misc)):
                    act.wait(b.ready)
                    m1 = act.do(A.activation, stage.ap[:, 0, c, :], b.ap, ACT.Copy)
                    dve.wait(m1)
                    m2 = dve.do(V.tensor_tensor, stage.ap[:, 1, c, :], b.ap,
                                stage.ap[:, 0, c, :].bitcast(F32), ALU.subtract)
                    b.free = [m2]
                    stage.ready += [m1, m2]
                    n.free = list(b.ready)
                yield
                stack = q_stacks.take(sp)
                send_stack(stage, stack)
                stack_of[h] = stack
                yield

            def find_peaks(h):
                stack, keys = stack_of[h], keys_of[h // 2]
                peak = peaks.take(dve)
                for t in range(HT):
                    for two in range(PAIRS // 2):
                        pe.wait(keys.ready, stack.ready)
                        got = []
                        for i in range(2):
                            p = 2 * two + i
                            b = peak_banks.take(pe)
                            q = stack.ap[0:STACK, p, t * P:(t + 1) * P]
                            view = b.ap[:, 0:2 * KEYS].rearrange("p (a k) -> p a k", a=2)
                            pe.do(T.matmul, view[:, :, 0:P], q, keys.ap[0:STACK, 2 * p:2 * p + 2, :],
                                  start=True, stop=True, signal=False)
                            rest = keys.ap[0:STACK, HEADS + p, :].rearrange("p (j k) -> p j k", k=32)
                            got.append((p, b, view, pe.do(
                                T.matmul, view[:, :, P:KEYS], q, rest[:, 2 * i:2 * i + 2, 0:REST],
                                start=True, stop=True)))
                        for p, b, view, m in got:
                            dve.wait(m)
                            m = dve.do(V.tensor_reduce, peak.ap[:, t, 2 * p:2 * p + 2], view, AX.X, ALU.max)
                            b.free = [m]
                        yield
                b = misc.take(pe)
                pe.wait(m)
                for t in range(HT):
                    m = pe.do(T.transpose, b.ap[0:HEADS, t * P:(t + 1) * P], peak.ap[:, t, :], ident[:, :],
                              signal=t == HT - 1)
                peak.free = [m]
                pt = peak_t.take(act, dve)
                act.wait(m)
                m1 = act.do(A.activation, pt.ap[:, 0, :], b.ap[0:HEADS, :], ACT.Copy, scale=-1.0)
                dve.wait(m1)
                m2 = dve.do(V.scalar_tensor_tensor, pt.ap[:, 1, :], b.ap[0:HEADS, :], -1.0,
                            pt.ap[:, 0, :].bitcast(F32), ALU.mult, ALU.subtract)
                b.free = [m2]
                sp.wait(m2)
                m = dma.copy(max_dram[h].rearrange("r h n -> h r n"), pt.ap.bitcast(F32))
                pt.free = [m]
                sp.wait(m)
                for r in range(2):
                    row = STACK + 2 * r
                    stack.ready.append(dma.copy(stack.ap[row:row + 2, :, :].bitcast(F32),
                                                max_dram[h, r].rearrange("(p a) n -> a p n", a=2)))
                yield

            def after_attention1(h, turned):
                a = att.take(dve)
                for t in range(HT):
                    m, m3 = normalize_heads(t, turned, misc, sums, a.ap[:, t, :])
                    a.ready.append(m3)
                    yield
                turned.free = [m]
                marks = []
                for t in range(HT):
                    xs = x[:, HT * h + t, :]
                    dve.wait(a.ready[t], x_ready[h])
                    marks.append(dve.do(V.scalar_tensor_tensor, xs, a.ap[:, t, :], tg[:, 2:3], xs,
                                        ALU.mult, ALU.add))
                a.free = marks[-1:]
                x_ready[h] = marks
                yield

            early, peaking, late = Background(), Background(), Background()
            for b in range(2):
                early.add(prepare_keys1(b))
                fetch_experts(b)
            for h in range(2):
                early.add(add_experts(h))
                early.add(prepare_queries1(h))
            early.drain()
            peaking.add(find_peaks(0))
            peaking.drain()
            turned_of, chunks_of, later, needed = {}, {}, {}, {}

            def start_scores(n):
                h, g, j = units[n]
                if (g, j) == (0, 0):
                    peaking.drain()
                    for work in needed.pop(h, []):
                        early.finish(work)
                    if h + 1 < HALVES:
                        peaking.add(find_peaks(h + 1))
                    if h + 2 < HALVES:
                        fetch_experts(h + 2)
                        early.add(add_experts(h + 2))
                        needed[h + 1] = [early.add(prepare_queries1(h + 2))]
                    if h % 2 == 0 and 2 <= h < HALVES - 2:
                        needed[h + 1].append(early.add(prepare_keys1(h // 2 + 1)))
                stack, keys = stack_of[h], keys_of[h // 2]
                b = s_banks.take(pe)
                key_scores(j, ROWS1, b, keys, stack, g)
                if (g, j) == (GROUPS - 1, 4):
                    stack.free = list(b.ready)
                    if h % 2 == 1:
                        keys.free = list(b.ready)
                return b

            def weigh(n):
                h, g, _ = units[n]
                if g == 0:
                    turned_of[h] = turned_ring.take(act)
                m = weigh_values(g, chunks_of.pop((h, g)), vals_of[h // 2], o_bank, turned_of[h])
                if g == GROUPS - 1:
                    if h % 2 == 1:
                        vals_of[h // 2].free = [m]
                    late.add(after_attention1(h, turned_of[h]))

            b = start_scores(0)
            for n in range(len(units) + 2):
                if n < len(units):
                    h, g, j = units[n]
                    w = weights.take(act)
                    act.wait(b.ready)
                    w.ready = [act.do(A.activation, w.ap, b.ap, ACT.Exp)]
                    b.free = list(w.ready)
                    chunks_of.setdefault((h, g), []).append(w)
                    if j == 4:
                        later[n + 1] = n
                if n + 1 < len(units):
                    b = start_scores(n + 1)
                if n in later:
                    weigh(later.pop(n))
                early.step()
                peaking.step(PEAK_STEPS[n % len(PEAK_STEPS)])
                late.step()
            late.drain()
        barrier()

        scope = ExitStack()
        with scope:
            s3 = lambda n, s, d: sb(n, s, d, scope)
            normed = Ring([s3(f"normed2_{i}", [P, HT, DIM], F32)[:, :, :] for i in range(2)])
            feats = Ring([s3(f"feats3_{i}", [P, CD, HALF], F32)[:, :, :] for i in range(2)])
            hidden = Ring([s3(f"hidden{i}", [P, HB, HALF], F32)[:, :, :] for i in range(2)])
            up_banks, down_banks, misc = use(bank[0:4]), use(bank[4:6]), use(bank[6:8])
            feats_of = {}

            def prepare_ffn(h):
                n = normed.take(dve)
                yield from layernorm(h, n.ap, n)
                pool.wait(n.ready[-1])
                x_ready[h] = [pool.do(G.tensor_tensor, x[:, HT * h:HT * h + HT, :],
                                      x[:, HT * h:HT * h + HT, :],
                                      b_out[:, :].unsqueeze(1).to_broadcast([P, HT, DIM]), ALU.add)]
                f = feats.take(act)
                for c, b in enumerate(turn_half(n.ap, n.ready, misc)):
                    act.wait(b.ready)
                    m = act.do(A.activation, f.ap[:, c, :], b.ap, ACT.Copy)
                    f.ready.append(m)
                    b.free = [m]
                    n.free = list(b.ready)
                feats_of[h] = f
                yield

            early = Background()
            early.add(prepare_ffn(0))
            early.drain()
            for h in range(HALVES):
                f = feats_of[h]
                hid = hidden.take(act)
                if h + 1 < HALVES:
                    early.add(prepare_ffn(h + 1))
                for k in range(HB):
                    b = up_banks.take(pe)
                    pe.wait(f.ready)
                    for c in range(CD):
                        m = pe.do(T.matmul, b.ap, w_up[:, c, k * P:(k + 1) * P], f.ap[:, c, :],
                                  start=c == 0, stop=c == CD - 1, signal=c == CD - 1)
                    act.wait(m)
                    m2 = act.do(A.activation, hid.ap[:, k, :], b.ap, ACT.Gelu, bias=hid_bias[:, k:k + 1])
                    hid.ready.append(m2)
                    b.free = [m2]
                    early.step()
                f.free = [m]
                early.drain()
                for two in range(HT // 2):
                    b = down_banks.take(pe)
                    for i in range(2):
                        t = 2 * two + i
                        for k in range(HB):
                            pe.wait(hid.ready[k])
                            m = pe.do(T.matmul, b.ap[:, i * DIM:(i + 1) * DIM],
                                      hid.ap[:, k, t * P:(t + 1) * P], w_con[:, k, :],
                                      start=k == 0, stop=k == HB - 1, signal=i == 1 and k == HB - 1)
                    dve.wait(m, x_ready[h])
                    tiles = slice(HT * h + 2 * two, HT * h + 2 * two + 2)
                    xs = x[:, tiles, :].rearrange("p i f -> p (i f)")
                    m2 = dve.do(V.scalar_tensor_tensor, xs, b.ap, tg[:, 3:4], xs, ALU.mult, ALU.add)
                    b.free = [m2]
                    sp.wait(m2)
                    dma.copy(out_view[:, tiles, :], x[:, tiles, :])
                hid.free = [m]

        barrier()
        block = ctx.enter_context(nc.Block())

        @block.tensor
        def _(_):
            pe.run()

        @block.scalar
        def _(_):
            act.run()

        @block.vector
        def _(_):
            dve.run()

        @block.gpsimd
        def _(_):
            pool.run()

        @block.sync
        def _(_):
            sp.run()


def constants():
    bf = mybir.dt.np(BF16)
    rows, cols = np.arange(P)[:, None], np.arange(P)[None, :]
    return {
        "ident": np.eye(P, dtype=np.float32),
        "upper": (rows < cols).astype(bf),
        "a_iota": np.broadcast_to(np.arange(NA)[:, None], (P, 4, NA, EG)).astype(bf),
        "b_iota": np.broadcast_to(np.arange(NB)[:, None], (P, NB, EXPERTS)).astype(bf),
        "lane_no": np.arange(1, P + 1, dtype=np.float32)[:, None].copy(),
        "spare_row": np.arange(TOKENS, TOKENS + P, dtype=np.float32)[:, None].copy(),
        "diag": np.broadcast_to((np.arange(P)[:, None] % EG == np.arange(EG)[None, :])[:, None, :],
                                (P, NB, EG)).astype(np.float32),
        "swaps": np.stack([rows ^ (1 << s) == cols for s in range(INSIDE)], 1).astype(np.float32),
    }


def feature_rows(w):
    return np.ascontiguousarray(w.reshape(-1, P, w.shape[1]).transpose(1, 0, 2))


def on_all(v):
    return np.ascontiguousarray(np.broadcast_to(v, (P, v.shape[0])))


def stacked(by_head, rows_aug):
    n = by_head.shape[1]
    s = np.zeros((STACK + rows_aug, HEADS, n), by_head.dtype)
    for h in range(HEADS):
        for block in range(3):
            r = 32 * block + HD * (h % 2)
            s[r:r + HD, h] = by_head[HD * h:HD * (h + 1)]
    return s


def key_stacks(keys):
    s = stacked(keys.T, 4)
    for h in range(HEADS):
        s[STACK + h % 2, h] = s[STACK + 2 + h % 2, h] = 1.0
    out = np.zeros((STACK + 4, NK, P), keys.dtype)
    out[:, :HEADS] = s[:, :, :P]
    for h in range(HEADS):
        out[:, HEADS + h // 2, 32 * (h % 4):32 * (h % 4) + REST] = s[:, h, P:]
    return out


def tap_rows(w):
    own, other = np.empty((STAGES, HID), w.dtype), np.empty((STAGES, HID), w.dtype)
    for s in range(STAGES):
        st = 1 << s
        v = w[s].reshape(HID // (2 * st), st, 2, 2)
        o, p = own[s].reshape(-1, 2, st), other[s].reshape(-1, 2, st)
        for r in range(2):
            o[:, r], p[:, r] = v[:, :, r, r], v[:, :, r, 1 - r]
    return own, other


def laid_out(i):
    ctx = i["ctx_1024"]
    d = constants()
    d["x"] = i["x"].reshape(TOKENS, DIM)
    d["gates"] = np.ascontiguousarray(np.broadcast_to(
        np.stack([i["g_xattn"][0], i["g_ffn"][0], i["g_xattn"][1], i["g_ffn"][1]]), (P, 4)))
    for n in "qvo":
        d[f"w{n}"] = feature_rows(i[f"L0_xattn_W{n}"].T)
    d["wk"] = stacked(i["L0_xattn_Wk"], 0).reshape(STACK, GROUPS, 4, CD, P).transpose(1, 4, 3, 2, 0)
    d["bk"] = np.ascontiguousarray(stacked(i["L0_xattn_bk"][:, None], 0)[:, :, 0])
    d["bq"] = np.ascontiguousarray(i["L0_xattn_bq"].reshape(CD, P).T)
    d["bv"], d["bo"] = on_all(i["L0_xattn_bv"]), on_all(i["L0_xattn_bo"])
    d["gate_w"] = feature_rows(np.concatenate([i["L0_ffn_gate_w"], i["L0_ffn_shared_gate_w"]], 1))
    keys = np.zeros((BATCH, DIM, 3 * P), ctx.dtype)
    keys[:, :, :KEYS] = ctx.transpose(0, 2, 1)
    for j in range(4):
        keys[:, :, 2 * P + 32 * j:2 * P + 32 * j + REST] = ctx[:, P:].transpose(0, 2, 1)
    d["ctx_t"] = np.stack([feature_rows(k) for k in keys])
    d["ctx"] = ctx
    d["k1"] = np.stack([key_stacks(ctx[b]) for b in range(BATCH)])
    gu, dn = i["L0_ffn_expert_gate_up_w"], i["L0_ffn_expert_down_w"]
    d["expert_w"] = np.ascontiguousarray(np.concatenate(
        [gu.reshape(EXPERTS, CD, P, 2 * INNER).transpose(0, 2, 1, 3), dn[:, :, None, :]], 2))
    d["w_sgu"] = feature_rows(i["L0_ffn_shared_gate_up_w"])
    d["w_sd"] = feature_rows(i["L0_ffn_shared_down_w"])
    d["w_exp"] = feature_rows(np.concatenate([i["L1_ffn_W_exp"].T, i["L1_ffn_b_exp"][:, None]], 1))
    d["w_con"] = feature_rows(i["L1_ffn_W_con"])
    taps = np.empty((4, STAGES, HID), i["L1_ffn_up_weights"].dtype)
    taps[0], taps[1] = tap_rows(i["L1_ffn_up_weights"])
    taps[2], taps[3] = tap_rows(i["L1_ffn_down_weights"])
    at = np.arange(HID)
    for s in range(INSIDE):
        taps[1, s] = taps[1, s][at ^ (1 << s)]
    d["taps"] = np.ascontiguousarray(taps.reshape(4, STAGES, HB, P).transpose(3, 0, 1, 2))
    d["up_bias"] = np.ascontiguousarray(i["L1_ffn_up_bias"].reshape(HB, P).T)
    d["b_con"], d["down_bias"] = on_all(i["L1_ffn_b_con"]), on_all(i["L1_ffn_down_bias"])
    return d


def kernel(**inputs):
    import concourse.bacc as bacc
    from concourse.bass_utils import run_bass_kernel_spmd

    nc = bacc.Bacc("TRN2", target_bir_lowering=False, num_devices=1)
    host = {n: np.asarray(a) for n, a in inputs.items()}
    arrays, aps = {}, {}
    for name, a in laid_out(host).items():
        arrays[f"in_{name}"] = np.ascontiguousarray(a)
        aps[name] = nc.dram_tensor(f"in_{name}", a.shape, mybir.dt.from_np(a.dtype), kind="ExternalInput").ap()
    out = nc.dram_tensor("out", (TOKENS, DIM), F32, kind="ExternalOutput").ap()
    build(nc, aps, out)
    result = run_bass_kernel_spmd(nc, [arrays], core_ids=[0])
    return result.results[0]["out"].reshape(BATCH, SEQ, DIM)
```

```python
from collections import deque
from contextlib import ExitStack

import numpy as np

import concourse.bass as bass
from concourse import mybir

F32 = mybir.dt.float32
F32R = mybir.dt.float32r
BF16 = mybir.dt.bfloat16
I32 = mybir.dt.int32
U32 = mybir.dt.uint32
ALU = mybir.AluOpType
ACT = mybir.ActivationFunctionType
AX = mybir.AxisListType

P = 128
BATCH, SEQ, DIM = 4, 1024, 256
KEYS = 154
REST = KEYS - P
HEADS = 16
HD = DIM // HEADS
PAIRS = HEADS // 2
GROUPS = HEADS // 4
TOKENS = BATCH * SEQ
TILES = TOKENS // P
HALF = 512
HT = HALF // P
HALVES = TOKENS // HALF
CD = DIM // P
STACK = 96
NK = HEADS + PAIRS
EXPERTS, TOPK, CAP = 64, 8, 128
INNER, SHARED = 128, 512
HID = 1024
HB = HID // P
STAGES = 10
INSIDE = 7
EPS = 1e-5
ROW = DIM + EXPERTS
SUMS = 2
PEAK_STEPS = (2, 1)
ON_ACT = (0, 1, 3, 4)
NB = 16
NA = CAP // NB
EG = P // NA


class Lane:

    def __init__(self, engine, sem):
        self.engine, self.sem, self.count, self.queue, self.passed = engine, sem, 0, [], {}

    def wait(self, *marks):
        for m in marks:
            if isinstance(m, list):
                self.wait(*m)
            elif m is not None:
                sem, value = m
                if self.passed.get(sem.name, 0) < value:
                    self.passed[sem.name] = value
                    self.queue.append((self.engine.wait_ge, (sem, value), {}, None, 0))

    def do(self, operation, *args, signal=True, **named):
        self.count += signal
        self.queue.append((operation, args, named, self.sem if signal else None, 1))
        return (self.sem, self.count) if signal else None

    def run(self):
        for operation, args, named, sem, by in self.queue:
            issued = operation(*args, **named)
            if sem is not None:
                issued.then_inc(sem, by)


class Dmas:

    def __init__(self, lane, sems):
        self.lane, self.sems, self.n = lane, sems, 0
        self.last = [None] * len(sems)

    def start(self, operation, *args, **named):
        k = self.n % len(self.sems)
        self.lane.wait(self.last[k])
        sem, value = self.sems[k], 16 * (self.n // len(self.sems) + 1)
        self.n += 1
        self.lane.queue.append((operation, args, named, sem, 16))
        self.last[k] = (sem, value)
        return self.last[k]

    def copy(self, out, in_):
        return self.start(self.lane.engine.dma_start, out, in_)


class Slot:

    def __init__(self, ap):
        self.ap, self.ready, self.free = ap, [], []


class Ring:
    def __init__(self, aps):
        self.slots, self.n = [Slot(a) for a in aps], 0

    def take(self, *writers):
        s = self.slots[self.n % len(self.slots)]
        self.n += 1
        assert s.free is not None, "its readers are not queued yet"
        for lane in writers:
            lane.wait(s.free)
        s.ready, s.free = [], None
        return s


class Background:

    def __init__(self):
        self.work = deque()

    def add(self, gen):
        self.work.append(gen)
        return gen

    def step(self, n=1):
        for _ in range(n):
            while self.work:
                try:
                    next(self.work[0])
                    break
                except StopIteration:
                    self.work.popleft()

    def finish(self, gen):
        while gen in self.work:
            self.step()

    def drain(self):
        while self.work:
            self.step()


def build(nc, D, out):
    ctx = ExitStack()
    with ctx:
        sem = lambda name: ctx.enter_context(nc.semaphore(name))
        T, A, V, G, S = nc.tensor, nc.scalar, nc.vector, nc.gpsimd, nc.sync
        pe, act, dve, pool, sp = (Lane(n, sem(f"ends_{w}")) for n, w in
                                  ((T, "pe"), (A, "act"), (V, "dve"), (G, "pool"), (S, "sp")))
        lanes = [pe, act, dve, pool, sp]
        dma = Dmas(sp, [sem(f"dma_sp{i}") for i in range(24)])
        gdma = Dmas(pool, [sem(f"dma_pool{i}") for i in range(12)])

        def sb(name, shape, dt, scope=ctx):
            return scope.enter_context(nc.sbuf_tensor(name, list(shape), dt))

        psum = ctx.enter_context(nc.psum_tensor("psum", [P, 8, 512], F32))
        bank = [Slot(psum[:, i, :]) for i in range(8)]

        def use(slots):
            r = Ring([])
            r.slots = list(slots)
            return r

        x = sb("x", [P, TILES, DIM], F32)
        ident = sb("ident", [P, P], F32)
        gates = sb("gates", [P, 4], F32)
        tg = sb("tanh_gates", [P, 4], F32)
        b_att = sb("bias_att", [P, DIM], F32)
        half_pow = sb("minus_half", [P, HT], F32)
        stats = Ring([sb(f"stats{i}", [P, HT, 6], F32)[:, :, :] for i in range(2)])
        moments = Ring([sb(f"moments{i}", [P, HT, 2], F32)[:, :, :] for i in range(2)])
        vareps = Ring([sb(f"vareps{i}", [P, HT], F32)[:, :] for i in range(2)])
        rstd = Ring([sb(f"rstd{i}", [P, HT], F32)[:, :] for i in range(2)])

        rows_dram = nc.dram_tensor("rows_scratch", (TOKENS, ROW), F32).ap()
        feats_dram = nc.dram_tensor("feats_scratch", (HALVES, P, CD * HALF), F32).ap()
        sum_dram = [nc.dram_tensor(f"expert_sums{i}", (TOKENS + P, DIM), F32).ap() for i in range(SUMS)]
        list_dram = nc.dram_tensor("list_scratch", (4, P, NB), F32).ap()
        max_dram = nc.dram_tensor("max_scratch", (HALVES, 2, HEADS, HALF), F32).ap()

        x_view = D["x"].rearrange("(i p) f -> p i f", p=P)
        out_view = out.rearrange("(i p) f -> p i f", p=P)
        m_x = []

        def load_x(h):
            m_x.append([dma.copy(x[:, HT * h:HT * h + HT, :], x_view[:, HT * h:HT * h + HT, :])])

        load_x(0)
        m_ident = dma.copy(ident[:, :], D["ident"])
        m_gates = dma.copy(gates[:, :], D["gates"])
        m_hp = pool.do(G.memset, half_pow[:, :], -0.5)

        act.wait(m_gates)
        m_tg = act.do(A.activation, tg[:, :], gates[:, :], ACT.Tanh)
        act.do(A.preload_act_table_set, "natural_log_exp_and_others", signal=False)
        x_ready = m_x

        def layernorm(h, dst, holder):
            st, mo, ve, rs = stats.take(dve), moments.take(dve), vareps.take(pool), rstd.take(pool)
            dve.wait(x_ready[h])
            got = []
            for t in range(HT):
                got.append(dve.do(V.bn_stats, st.ap[:, t, :], x[:, HT * h + t, :]))
            for t in range(HT):
                dve.wait(got[t])
                m = dve.do(V.bn_aggr, mo.ap[:, t, :], st.ap[:, t, :])
            st.free = [m]
            yield
            pool.wait(m)
            m = pool.do(G.tensor_scalar, ve.ap, mo.ap[:, :, 1], EPS, 0.0, ALU.add, ALU.add)
            pool.wait(m, m_hp)
            m = pool.do(G.tensor_tensor, rs.ap, ve.ap, half_pow[:, :], ALU.pow)
            ve.free = [m]
            yield
            dve.wait(m)
            holder.ready = []
            for t in range(HT):
                m = dve.do(V.tensor_scalar,
                    dst[:, t, :], x[:, HT * h + t, :], mo.ap[:, t, 0:1], rs.ap[:, t:t + 1],
                    ALU.subtract, ALU.mult)
                holder.ready.append(m)
            mo.free = rs.free = [m]
            yield

        def turn_half(src, ready, misc):
            banks = []
            for c in range(CD):
                b = misc.take(pe)
                for t in range(HT):
                    pe.wait(ready[t] if t < len(ready) else ready[-1])
                    m = pe.do(T.transpose,
                        b.ap[:, t * P:(t + 1) * P], src[:, t, c * P:(c + 1) * P], ident[:, :],
                        signal=t == HT - 1)
                b.ready = [m]
                banks.append(b)
            return banks

        PRODUCTS = ((0, 0), (1, 0), (0, 1))

        def split_parts(parts, whole, ready):
            act.wait(ready)
            m1 = act.do(A.activation, parts[:, 0], whole, ACT.Copy)
            dve.wait(m1, ready)
            return [m1, dve.do(V.tensor_tensor, parts[:, 1], whole, parts[:, 0].bitcast(F32), ALU.subtract)]

        def send_stack(stage, stack):
            sp.wait(stage.ready)
            stack.ready = []
            hi = stage.ap.bitcast(F32)
            st = stack.ap.bitcast(F32)
            for r in range(4):
                for part, row in ((0, 0), (0, 32), (1, 64)):
                    stack.ready.append(dma.copy(st[row:row + 32, r::4, :],
                                                hi[32 * r:32 * r + 32, part, :, :]))
            stage.free = list(stack.ready)

        def split_keys(raw, stack, rows, scale):
            marks = []
            for n in range(0, NK, NK // 4):
                part = slice(n, n + NK // 4)
                act.wait(raw.ready)
                m = act.do(A.activation, stack.ap[0:rows, part, :], raw.ap[0:rows, part, :], ACT.Copy,
                           scale=scale)
                dve.wait(m)
                marks += [m, dve.do(V.scalar_tensor_tensor, stack.ap[32:64, part, :],
                                    raw.ap[32:64, part, :], scale,
                                    stack.ap[32:64, part, :].bitcast(F32), ALU.mult, ALU.subtract)]
                yield
            raw.free = stack.ready = marks

        def key_scores(chunk, rows, bank_slot, keys, stack, g):
            b = bank_slot
            pe.wait(keys.ready, stack.ready)
            if chunk < 4:
                head = 4 * g + chunk
                m = pe.do(T.matmul, b.ap, keys.ap[0:rows, head, :],
                                             stack.ap[0:rows, head // 2, :], start=True, stop=True)
            else:
                for s in range(2):
                    pair = 2 * g + s
                    m = pe.do(T.matmul,
                        b.ap, keys.ap[0:rows, HEADS + pair, :], stack.ap[0:rows, pair, :],
                        start=s == 0, stop=s == 1, signal=s == 1)
            b.ready = [m]

        def weigh_values(g, part, weights, values, o_bank):
            pe.wait(values.ready, o_bank.free if part == 0 else None)
            for j in range(4):
                w = weights[j] if part == 0 else weights[4]
                pe.wait(w.ready)
                m = pe.do(T.matmul, o_bank.ap[32 * j:32 * j + 32, :], values.ap[:, part, 4 * g + j, :],
                          w.ap, start=part == 0, stop=part == 1, tile_position=(0, 32 * j),
                          signal=j == 3)
            for w in weights[0:4] if part == 0 else weights[4:5]:
                w.free = [m]
            return m

        def keep_weighted(g, m, o_bank, turned):
            act.wait(m)
            m2 = act.do(A.activation, turned.ap[:, g, :], o_bank.ap, ACT.Copy)
            o_bank.free = [m2]
            turned.ready = [m2]

        def normalize_heads(t, turned, misc, sums, dst):
            b = misc.take(pe)
            pe.wait(turned.ready)
            for g in range(GROUPS):
                m = pe.do(T.transpose, b.ap[:, g * P:(g + 1) * P],
                                                     turned.ap[:, g, t * P:(t + 1) * P], ident[:, :],
                          signal=g == GROUPS - 1)
            s = sums.take(dve)
            view = b.ap.rearrange("p (h w) -> p h w", w=32)
            dve.wait(m)
            m2 = dve.do(V.reciprocal, s.ap, view[:, :, HD])
            dve.wait(m2)
            m3 = dve.do(V.tensor_tensor,
                dst.rearrange("p (h d) -> p h d", d=HD), view[:, :, 0:HD],
                s.ap.unsqueeze(2).to_broadcast([P, HEADS, HD]), ALU.mult)
            b.free = s.free = [m3]
            return m, m3

        sgate = sb("sgate", [P, TILES], F32)
        w_con = sb("w_con_fused", [P, HB, DIM], F32)
        positions = w_con[:, :, :].rearrange("p a n -> p (a n)").bitcast(BF16)
        pos_a, pos_b = (positions[:, i * TILES * EXPERTS:(i + 1) * TILES * EXPERTS].rearrange(
            "p (t n) -> p t n", n=EXPERTS) for i in range(2))

        scope = ExitStack()
        with scope:
            s0 = lambda n, s, d: sb(n, s, d, scope)
            wq, wo, wv = (s0(f"w{n}", [P, CD, DIM], F32) for n in "qov")
            wk_ring = Ring([s0(f"wk_stack{i}", [P, CD, 4, STACK], F32)[:, :, :, :] for i in range(2)])
            bk = s0("bk_stack", [STACK, HEADS], F32)
            bq = s0("bq", [P, CD], F32)
            bv = s0("bv", [P, DIM], F32)
            gate_w = s0("gate_w", [P, CD, EXPERTS + 1], F32)
            ctx_t = s0("ctx_t", [P, CD, 3 * P], F32)
            upper = s0("upper", [P, P], BF16)
            ones = s0("ones", [P, P], BF16)
            zeros = s0("zeros", [P, 1, DIM], F32)
            masks = s0("masks", [P, HT, EXPERTS], BF16)
            before = s0("mask_sums", [P, 2, EXPERTS], BF16)
            k_raw = Slot(s0("k_raw0", [STACK, NK, P], F32)[:, :, :])
            keys_ring = Ring([s0(f"k_stack{i}", [P, NK, P], F32R)[:, :, :] for i in range(2)])
            vals_ring = Ring([s0(f"values{i}", [P, 2, HEADS, 32], F32)[:, :, :, :] for i in range(2)])
            q_stacks = Ring([s0(f"q_stack{i}", [P, PAIRS, HALF], F32R)[:, :, :] for i in range(2)])
            q_stage = Ring([s0("q_stage", [P, 2, CD, HALF], F32R)[:, :, :, :]])
            weights = Ring([s0(f"weights{i}", [P, HALF], F32)[:, :] for i in range(9)])
            turned_ring = Ring([s0(f"turned{i}", [P, GROUPS, HALF], F32)[:, :, :] for i in range(2)])
            normed = Ring([s0("normed", [P, HT, DIM], F32)[:, :, :]])
            rows = Ring([s0("rows", [P, HT, ROW], F32)[:, :, :]])
            feats = Ring([s0(f"feats{i}", [P, CD, HALF], F32)[:, :, :] for i in range(2)])
            att = Ring([s0("att", [P, HT, DIM], F32)[:, :, :]])
            sums = Ring([s0(f"sums{i}", [P, HEADS], F32)[:, :] for i in range(2)])
            probs = Ring([s0(f"probs{i}", [P, HT, EXPERTS], F32)[:, :, :] for i in range(1)])
            small = Ring([s0(f"small{i}", [P, 8, HT], F32)[:, :, :] for i in range(2)])
            top = Ring([s0(f"top{i}", [P, HT, TOPK], F32)[:, :, :] for i in range(2)])
            picked = Ring([s0(f"picked{i}", [P, HT, EXPERTS], F32)[:, :, :] for i in range(1)])
            posf = Ring([s0("pos_f", [P, HT, EXPERTS], F32)[:, :, :]])
            posi = Ring([s0("pos_i", [P, 2, HT, EXPERTS], I32)[:, :, :, :]])

            m_w = {}

            def load_weights(*pairs):
                for name, t in pairs:
                    m_w[name] = dma.copy(t, D[name])

            load_weights(("wq", wq[:, :, :]), ("bq", bq[:, :]), ("bk", bk[:, :]))
            m = pool.do(G.memset, zeros[:, :, :], 0.0)
            m_zeros, m_sums = m, [[] for _ in sum_dram]
            ZERO_ROWS = (TILES + 1) // 3

            def clear_sums(n):
                sums_view = sum_dram[n // 3].rearrange("(p r) f -> p r f", p=P)
                sp.wait(m_zeros)
                m_sums[n // 3].append(dma.copy(
                    sums_view[:, ZERO_ROWS * (n % 3):ZERO_ROWS * (n % 3 + 1), :],
                    zeros[:, :, :].to_broadcast([P, ZERO_ROWS, DIM])))

            m_ones = pool.do(G.memset, ones[:, :], 1.0)
            m_before = pool.do(G.memset, before[:, :, :], 0.0)
            sum_ready = [m_before]
            m_z = pool.do(G.memset, k_raw.ap, 0.0)
            k_raw.free = [m_z]

            def clear_values(ring):
                for v in ring.slots:
                    a = [pool.do(G.memset, v.ap[:, 1, :, :], 0.0),
                         pool.do(G.memset, v.ap[:, 0, :, HD:32], 1.0)]
                    for j in range(4):
                        pool.wait(a)
                        a.append(pool.do(G.memset,
                            v.ap[32 * j:32 * j + REST, 1, j::4, HD:32], 1.0))
                    pool.wait(a)
                    v.free = a

            clear_values(vals_ring)

            misc = use(bank[6:8])
            s_banks = use(bank[0:5])
            o_bank = bank[5]
            keys_of, vals_of, stack_of, turned_of = {}, {}, {}, {}
            ctx_slot = Slot(ctx_t[:, :, :])

            def prepare_keys(b, ahead=4):
                sp.wait(ctx_slot.free)
                m_ctx = dma.copy(ctx_t[:, :, :], D["ctx_t"][b])
                coming = deque()

                def load_wk(n):
                    wk = wk_ring.take(sp)
                    wk.ready = [dma.copy(wk.ap, D["wk"][n])]
                    coming.append(wk)

                load_wk(0)
                load_wk(1)
                for _ in range(ahead):
                    yield
                pe.wait(m_ctx)
                dve.wait(k_raw.free, m_w["bk"])
                k_raw.free = None
                k_raw.ready = []
                for p in range(PAIRS):
                    if p % 2 == 0:
                        wk = coming.popleft()
                    pe.wait(wk.ready)
                    bk_slot = misc.take(pe)
                    for a in range(2):
                        for c in range(CD):
                            m = pe.do(T.matmul,
                                bk_slot.ap[0:STACK, a * KEYS:(a + 1) * KEYS], wk.ap[:, c, 2 * (p % 2) + a, :],
                                ctx_t[:, c, 0:KEYS], start=c == 0, stop=c == CD - 1,
                                signal=a == 1 and c == CD - 1)
                    if p % 2:
                        wk.free = [m]
                        if p // 2 + 2 < PAIRS // 2:
                            load_wk(p // 2 + 2)
                    view = bk_slot.ap[0:STACK, 0:2 * KEYS].rearrange("p (a k) -> p a k", a=2)
                    bias = bk[:, 2 * p:2 * p + 2].unsqueeze(2)
                    s = p % 2
                    dve.wait(m)
                    k_raw.ready.append(dve.do(V.tensor_tensor,
                        k_raw.ap[:, 2 * p:2 * p + 2, :], view[:, :, 0:P],
                        bias.to_broadcast([STACK, 2, P]), ALU.add))
                    k_raw.ready.append(dve.do(V.tensor_tensor,
                        k_raw.ap[:, HEADS + p, :].rearrange("p (j k) -> p j k", k=32)[:, 2 * s:2 * s + 2, 0:REST],
                        view[:, :, P:KEYS], bias.to_broadcast([STACK, 2, REST]), ALU.add))
                    bk_slot.free = k_raw.ready[-1:]
                    yield
                k_stack = keys_ring.take(act, dve)
                yield from split_keys(k_raw, k_stack, STACK, 0.25)
                keys_of[b] = k_stack
                yield
                v_slot = misc.take(pe)
                values = vals_ring.take(dve)
                pe.wait(m_w["wv"])
                for part in range(2):
                    for c in range(CD):
                        m = pe.do(T.matmul,
                            v_slot.ap[:, part * DIM:(part + 1) * DIM],
                            ctx_t[:, c, 2 * part * P:(2 * part + 1) * P], wv[:, c, :],
                            start=c == 0, stop=c == CD - 1, signal=part == 1 and c == CD - 1)
                ctx_slot.free = [m]
                dve.wait(m, m_w["bv"])
                values.ready = [dve.do(V.tensor_tensor,
                    values.ap[:, 0, :, 0:HD], v_slot.ap[:, 0:DIM].rearrange("p (h d) -> p h d", d=HD),
                    bv[:, :].rearrange("p (h d) -> p h d", d=HD), ALU.add)]
                for j in range(4):
                    r = slice(32 * j, 32 * j + REST)
                    values.ready.append(dve.do(V.tensor_tensor,
                        values.ap[r, 1, j::4, 0:HD],
                        v_slot.ap[r, DIM:2 * DIM].rearrange("p (h d) -> p h d", d=HD)[:, j::4, :],
                        bv[r, :].rearrange("p (h d) -> p h d", d=HD)[:, j::4, :], ALU.add))
                v_slot.free = values.ready[-1:]
                vals_of[b] = values
                yield

            def prepare_queries(h):
                n = normed.take(dve)
                yield from layernorm(h, n.ap, n)
                pool.wait(n.ready[-1], m_batt)
                m = pool.do(G.tensor_tensor,
                    x[:, HT * h:HT * h + HT, :], x[:, HT * h:HT * h + HT, :],
                    b_att[:, :].unsqueeze(1).to_broadcast([P, HT, DIM]), ALU.add)
                x_ready[h] = [m]
                yield
                pe.wait(m_ident)
                f = feats.take(act)
                for c, b in enumerate(turn_half(n.ap, n.ready, misc)):
                    act.wait(b.ready)
                    m = act.do(A.activation, f.ap[:, c, :], b.ap, ACT.Copy)
                    f.ready.append(m)
                    b.free = [m]
                    n.free = list(b.ready)
                yield
                stage = q_stage.take(act, dve)
                for mo in range(CD):
                    b = misc.take(pe)
                    pe.wait(f.ready, m_w["wq"])
                    for c in range(CD):
                        m = pe.do(T.matmul,
                            b.ap, wq[:, c, mo * P:(mo + 1) * P], f.ap[:, c, :],
                            start=c == 0, stop=c == CD - 1, signal=c == CD - 1)
                    act.wait(m, m_w["bq"])
                    m1 = act.do(A.activation,
                        stage.ap[:, 0, mo, :], b.ap, ACT.Identity, bias=bq[:, mo:mo + 1])
                    dve.wait(m1)
                    m2 = dve.do(V.scalar_tensor_tensor,
                        stage.ap[:, 1, mo, :], b.ap, bq[:, mo:mo + 1],
                        stage.ap[:, 0, mo, :].bitcast(F32), ALU.add, ALU.subtract)
                    b.free = [m2]
                    stage.ready += [m1, m2]
                    yield
                f.free = [m]
                stack = q_stacks.take(sp)
                send_stack(stage, stack)
                stack_of[h] = stack
                yield

            def after_attention(h, turned):
                a = att.take(dve)
                for t in range(HT):
                    m, m3 = normalize_heads(t, turned, misc, sums, a.ap[:, t, :])
                    a.ready.append(m3)
                    yield
                turned.free = [m]
                f = feats.take(act)
                for c, b in enumerate(turn_half(a.ap, a.ready, misc)):
                    act.wait(b.ready)
                    m = act.do(A.activation, f.ap[:, c, :], b.ap, ACT.Copy)
                    f.ready.append(m)
                    b.free = [m]
                    a.free = list(b.ready)
                yield
                x_marks = []
                for two in range(HT // 2):
                    b = misc.take(pe)
                    pe.wait(f.ready, m_w["wo"])
                    for i in range(2):
                        for c in range(CD):
                            t = 2 * two + i
                            m = pe.do(T.matmul,
                                b.ap[:, i * DIM:(i + 1) * DIM], f.ap[:, c, t * P:(t + 1) * P],
                                wo[:, c, :], start=c == 0, stop=c == CD - 1,
                                signal=i == 1 and c == CD - 1)
                    dve.wait(m, x_ready[h])
                    xs = x[:, HT * h + 2 * two:HT * h + 2 * two + 2, :].rearrange("p i f -> p (i f)")
                    m2 = dve.do(V.scalar_tensor_tensor,
                        xs, b.ap, tg[:, 0:1], xs, ALU.mult, ALU.add)
                    b.free = [m2]
                    x_marks.append(m2)
                    yield
                f.free = [m]
                x_ready[h] = x_marks
                r = rows.take(dve)
                yield from layernorm(h, r.ap[:, :, 0:DIM], r)
                f = feats.take(act)
                for c, b in enumerate(turn_half(r.ap, r.ready, misc)):
                    act.wait(b.ready)
                    m = act.do(A.activation, f.ap[:, c, :], b.ap, ACT.Copy)
                    f.ready.append(m)
                    b.free = [m]
                    turned_rows = list(b.ready)
                yield
                sp.wait(f.ready)
                m_feats = dma.copy(feats_dram[h].rearrange("p (c n) -> p c n", c=CD), f.ap)
                NL = EXPERTS + 1
                b = misc.take(pe)
                pe.wait(f.ready, m_w["gate_w"])
                for t in range(HT):
                    for c in range(CD):
                        m = pe.do(T.matmul,
                            b.ap[:, t * NL:(t + 1) * NL], f.ap[:, c, t * P:(t + 1) * P],
                            gate_w[:, c, :], start=c == 0, stop=c == CD - 1,
                            signal=t == HT - 1 and c == CD - 1)
                f.free = [m, m_feats]
                logits = b.ap[:, 0:HT * NL].rearrange("p (t n) -> p t n", n=NL)
                pr, sm, tp, pk = probs.take(dve), small.take(dve), top.take(dve), picked.take(dve)
                dve.wait(m)
                m = dve.do(V.tensor_reduce, sm.ap[:, 0, :], logits[:, :, 0:EXPERTS], AX.X, ALU.max)
                dve.wait(m)
                m = dve.do(V.tensor_tensor, pr.ap, logits[:, :, 0:EXPERTS],
                           sm.ap[:, 0, :].unsqueeze(2).to_broadcast([P, HT, EXPERTS]), ALU.subtract)
                act.wait(m)
                m1 = act.do(A.activation, pr.ap, pr.ap, ACT.Exp)
                m2 = act.do(A.activation, sm.ap[:, 1, :], logits[:, :, EXPERTS], ACT.Exp, scale=-1.0)
                b.free = [m, m2]
                yield
                dve.wait(m1, m2)
                ma = dve.do(V.tensor_reduce, sm.ap[:, 2, :], pr.ap, AX.X, ALU.add)
                mb = dve.do(V.tensor_scalar, sm.ap[:, 3, :], sm.ap[:, 1, :], 1.0, 0.0, ALU.add, ALU.add)
                dve.wait(ma, mb)
                ma = dve.do(V.reciprocal, sm.ap[:, 4:6, :].rearrange("p a t -> p (a t)"),
                                                   sm.ap[:, 2:4, :].rearrange("p a t -> p (a t)"))
                dve.wait(ma)
                dve.do(V.tensor_scalar, sgate[:, HT * h:HT * h + HT], sm.ap[:, 5, :],
                                                        tg[:, 1:2], None, ALU.mult)
                m = dve.do(V.tensor_tensor, pr.ap, pr.ap,
                           sm.ap[:, 4, :].unsqueeze(2).to_broadcast([P, HT, EXPERTS]), ALU.mult)
                dve.wait(m)
                ms = [dve.do(V.max, tp.ap[:, t, :], pr.ap[:, t, :]) for t in range(HT)]
                yield
                for t in range(HT):
                    dve.wait(ms[t])
                    m = dve.do(V.match_replace, pk.ap[:, t, :], tp.ap[:, t, :],
                                                              pr.ap[:, t, :], -1.0)
                ma = dve.do(V.tensor_reduce, sm.ap[:, 6, :], tp.ap, AX.X, ALU.add)
                dve.wait(m, ma, mask_free)
                m_mask = dve.do(V.tensor_scalar, masks[:, :, :], pk.ap, 0.0, None, ALU.is_lt)
                ma = dve.do(V.reciprocal, sm.ap[:, 7, :], sm.ap[:, 6, :])
                dve.wait(ma)
                ma = dve.do(V.tensor_scalar, sm.ap[:, 7, :], sm.ap[:, 7, :], tg[:, 1:2], None, ALU.mult)
                dve.wait(ma)
                m = dve.do(V.tensor_tensor, r.ap[:, :, DIM:ROW], pr.ap,
                           sm.ap[:, 7, :].unsqueeze(2).to_broadcast([P, HT, EXPERTS]), ALU.mult)
                pr.free = sm.free = tp.free = pk.free = [m]
                sp.wait(m, r.ready)
                m_rows = dma.copy(rows_dram[HALF * h:HALF * (h + 1), :].rearrange("(t p) n -> p t n", p=P), r.ap)
                r.free = [m_rows] + turned_rows
                yield
                yield
                yield
                b = misc.take(pe)
                pe.wait(m_mask, m_w["upper"], m_ones)
                pe.wait(sum_ready)
                old, new = before[:, h % 2, :], before[:, (h + 1) % 2, :]
                for t in range(HT):
                    earlier = [old] + [masks[:, u, :] for u in range(t)]
                    here = b.ap[:, t * EXPERTS:(t + 1) * EXPERTS]
                    pe.do(T.matmul, here, upper[:, :], masks[:, t, :], start=True, stop=False,
                          signal=False)
                    for n, mask in enumerate(earlier):
                        m = pe.do(T.matmul, here, ones[:, :], mask, start=False, stop=n == t,
                                  signal=n == t and t == HT - 1)
                for t in range(HT):
                    dve.wait(sum_ready)
                    sum_ready[:] = [dve.do(V.tensor_tensor, new, old if t == 0 else new,
                                           masks[:, t, :], ALU.add)]
                counts = b.ap[:, 0:HT * EXPERTS].rearrange("p (t n) -> p t n", n=EXPERTS)
                pf, pi = posf.take(dve), posi.take(dve)
                FAR = 4096.0
                dve.wait(m)
                m = dve.do(V.scalar_tensor_tensor, pf.ap, masks[:, :, :], -FAR, counts, ALU.mult, ALU.add)
                mask_free[:] = [m]
                b.free = [m]
                dve.wait(m)
                m = dve.do(V.tensor_scalar, pf.ap, pf.ap, FAR, None, ALU.add)
                dve.wait(m)
                ma = dve.do(V.tensor_copy, pi.ap[:, 0, :, :], pf.ap)
                pf.free = [ma]
                dve.wait(ma)
                mb = dve.do(V.tensor_scalar, pi.ap[:, 1, :, :], pi.ap[:, 0, :, :], 4, None,
                                                      ALU.logical_shift_right)
                dve.wait(mb)
                mc = dve.do(V.tensor_scalar, pi.ap[:, 0, :, :], pi.ap[:, 0, :, :], NB - 1, None,
                                                      ALU.bitwise_and)
                dve.wait(mc)
                sl = slice(HT * h, HT * h + HT)
                md = dve.do(V.tensor_copy, pos_a[:, sl, :], pi.ap[:, 1, :, :])
                me = dve.do(V.tensor_copy, pos_b[:, sl, :], pi.ap[:, 0, :, :])
                pos_ready.extend([md, me])
                pi.free = [me]
                yield

            mask_free, pos_ready = [], []
            first = [Background(), Background()]
            first[0].add(prepare_keys(0, ahead=1))
            first[1].add(prepare_queries(0))
            first[0].step()
            first[0].step()
            load_weights(("wv", wv[:, :, :]), ("bv", bv[:, :]))
            m_batt = dma.copy(b_att[:, :], D["bo"])
            load_weights(("wo", wo[:, :, :]), ("gate_w", gate_w[:, :, :]), ("upper", upper[:, :]))
            pool.wait(m_tg, m_batt)
            m_batt = pool.do(G.tensor_tensor, b_att[:, :], b_att[:, :],
                             tg[:, 0:1].to_broadcast([P, DIM]), ALU.mult)
            load_x(1)
            while first[0].work or first[1].work:
                first[1].step()
                first[0].step()
                if len(m_x) < HALVES:
                    load_x(len(m_x))
            early, late = Background(), Background()
            later = {}
            units = [(h, g, j) for h in range(HALVES) for g in range(GROUPS) for j in range(5)]
            chunks_of, needed = {}, {}

            def start_scores(n):
                h, g, j = units[n]
                if (g, j) == (0, 0):
                    for work in needed.pop(h, []):
                        early.finish(work)
                    late.drain()
                    if 1 <= h <= 3 * SUMS:
                        clear_sums(h - 1)
                    turned_of[h] = turned_ring.take(act)
                    if h + 1 < HALVES:
                        needed.setdefault(h + 1, []).append(early.add(prepare_queries(h + 1)))
                    if h % 2 == 0 and h + 2 < HALVES:
                        needed[h + 2] = [early.add(prepare_keys(h // 2 + 1))]
                stack, keys = stack_of[h], keys_of[h // 2]
                b = s_banks.take(pe)
                key_scores(j, STACK, b, keys, stack, g)
                if (g, j) == (GROUPS - 1, 4):
                    stack.free = list(b.ready)
                    if h % 2 == 1:
                        keys.free = list(b.ready)
                return b

            def finish_weights(n, b, w):
                dve.wait(w.log)
                w.ready = [dve.do(V.scalar_tensor_tensor, w.ap, b.ap, 1.0, w.ap, ALU.add, ALU.max)]
                b.free = w.ready

            def weigh(n, part):
                h, g, _ = units[n]
                m = weigh_values(g, part, chunks_of[h, g], vals_of[h // 2], o_bank)
                if part == 0:
                    return
                keep_weighted(g, m, o_bank, turned_of[h])
                if g == GROUPS - 1:
                    if h % 2 == 1:
                        vals_of[h // 2].free = [m]
                    late.add(after_attention(h, turned_of[h]))

            b = start_scores(0)
            logs, maxes = deque(), deque()
            for n in range(len(units) + 4):
                live = None
                if logs:
                    live, m, w, sign = logs.popleft()
                    act.wait(m)
                    m_log = act.do(A.activation, w.ap, w.ap, ACT.Ln, bias=1.0, scale=sign)
                if n < len(units):
                    h, g, j = units[n]
                    w_new = weights.take(act, dve)
                    chunks_of.setdefault((h, g), []).append(w_new)
                    if j in ON_ACT:
                        act.wait(b.ready)
                        m = act.do(A.activation, w_new.ap, b.ap, ACT.Relu, scale=-1.0)
                    else:
                        dve.wait(b.ready)
                        m = dve.do(V.tensor_scalar, w_new.ap, b.ap, 0.0, None, ALU.min)
                    logs.append((b, m, w_new, 1.0 if j in ON_ACT else -1.0))
                    if j == 4:
                        later[n + 2], later[n + 3] = (n, 0), (n, 1)
                if live:
                    act.wait(m_log)
                    w.log = act.do(A.activation, w.ap, w.ap, ACT.Exp, scale=-1.0)
                    maxes.append((n + 1, live, w))
                if maxes and maxes[0][0] <= n:
                    finish_weights(*maxes.popleft())
                if n + 1 < len(units):
                    b = start_scores(n + 1)
                if n in later:
                    weigh(*later.pop(n))
                early.step()
                late.step()
            late.drain()

        def barrier():
            marks = [(l.sem, l.count) for l in lanes if l.count]
            marks += [m for d in (dma, gdma) for m in d.last if m]
            for l in lanes:
                l.wait(marks)

        barrier()

        w_up = sb("w_up_fused", [P, CD, HID], F32)
        hid_bias = sb("hidden_bias", [P, HB], F32)
        b_out = sb("bias_out", [P, DIM], F32)

        scope = ExitStack()
        with scope:
            s1 = lambda n, s, d: sb(n, s, d, scope)
            a_iota = s1("a_iota", [P, 4, NA, EG], BF16)
            b_iota = s1("b_iota", [P, NB, EXPERTS], BF16)
            lane_no = s1("lane_no", [P, 1], F32)
            spare_row = s1("spare_row", [P, 1], F32)
            diag = s1("diag", [P, NB, EG], F32)
            hot_a = Ring([s1(f"hot_a{i}", [P, 3, 4, NA, EG], BF16)[:, :, :, :, :] for i in range(3)])
            hot_b = Ring([s1(f"hot_b{i}", [P, NB, EXPERTS], BF16)[:, :, :] for i in range(3)])
            lists = s1("lists", [P, 4, NB, EG], F32)
            lists_b = s1("lists_b", [P, 4, NB], F32)
            by_expert = s1("by_expert", [EXPERTS, P], F32)
            tokens = s1("tokens", [P, EXPERTS], U32)
            sum_rows = s1("sum_rows", [P, EXPERTS], U32)
            listed = s1("listed", [P, 3, EXPERTS], F32)
            w_ring = Ring([s1(f"expert_w{i}", [P, 3, DIM], F32)[:, :, :] for i in range(8)])
            got_ring = Ring([s1(f"got{i}", [P, ROW], F32)[:, :] for i in range(6)])
            got_t = Ring([s1(f"got_t{i}", [P, CD, P], F32)[:, :, :] for i in range(3)])
            silu_ring = Ring([s1(f"silu{i}", [P, P], F32)[:, :] for i in range(2)])
            inner_ring = Ring([s1(f"inner{i}", [P, P], F32)[:, :] for i in range(3)])
            made_ring = Ring([s1(f"made{i}", [P, DIM], F32)[:, :] for i in range(4)])
            w_sgu = s1("w_shared_up", [P, 2, CD * 2 * SHARED], F32R)
            w_sd = s1("w_shared_down", [P, 2, SHARED // P * DIM], F32R)
            feats = Ring([s1("feats_m", [P, CD * HALF], F32)[:, :]])
            feat_parts = Ring([s1("feat_parts", [P, 2, CD * HALF], F32R)[:, :, :]])
            s_silu = Ring([s1(f"shared_silu{i}", [P, HALF], F32)[:, :] for i in range(3)])
            s_inner = Ring([s1("shared_inner", [P, 2, SHARED // P, HALF], F32R)[:, :, :, :]])
            bf_u = s1("butterfly_u", [P, HB, DIM + 1], F32)
            bf_v = s1("butterfly_v", [P, HB, DIM + 1], F32)
            swaps = s1("swaps", [P, INSIDE, P], F32)
            taps = s1("taps", [P, 4, STAGES, HB], F32)
            up_bias = s1("up_bias", [P, HB], F32)
            down_bias = s1("down_bias", [P, DIM], F32)
            stage_m = Ring([s1(f"stage_m{i}", [P, P], F32)[:, :] for i in range(4)])
            part_ring = Ring([s1(f"stage_p{i}", [P, P], F32)[:, :] for i in range(2)])

            staging = bf_v[:, :, :].rearrange("p a n -> p (a n)")

            m_c = {n: dma.copy(t, D[n]) for n, t in (
                ("a_iota", a_iota[:, :, :, :]), ("b_iota", b_iota[:, :, :]), ("lane_no", lane_no[:, :]),
                ("spare_row", spare_row[:, :]),
                ("w_sgu", staging[:, 0:CD * 2 * SHARED]), ("diag", diag[:, :, :]),
                ("w_exp", bf_u[:, :, :]), ("swaps", swaps[:, :, :]), ("taps", taps[:, :, :, :]),
                ("up_bias", up_bias[:, :]), ("b_con", b_out[:, :]), ("down_bias", down_bias[:, :]))}
            experts_w = {}

            def load_expert(e_):
                w = w_ring.take(sp)
                w.ready = [dma.copy(w.ap, D["expert_w"][e_])]
                experts_w[e_] = w

            for e_ in range(3):
                load_expert(e_)

            back = Background()
            s_ring = use(bank[6:8])

            sgu_ready, sd_ready = [], []

            def shared_expert(h):
                whole = feats.take(sp)
                m = dma.copy(whole.ap, feats_dram[h])
                if h == 0:
                    yield
                    for n in range(2):
                        part = slice(n * 2 * SHARED, (n + 1) * 2 * SHARED)
                        sgu_ready.extend(split_parts(w_sgu[:, :, part], staging[:, part], m_c["w_sgu"]))
                    sp.wait(sgu_ready)
                    m_sd = dma.copy(staging[:, 0:SHARED // P * DIM], D["w_sd"])
                yield
                f = feat_parts.take(act, dve)
                f.ready = whole.free = split_parts(f.ap, whole.ap, m)
                if h == 0:
                    sd_ready.extend(split_parts(w_sd[:, :, :], staging[:, 0:SHARED // P * DIM], m_sd))
                inner = s_inner.take(dve)
                yield
                w_up_at = lambda part, c, a: w_sgu[:, part, c * 2 * SHARED + a:c * 2 * SHARED + a + P]
                w_down_at = lambda part, k: w_sd[:, part, k * DIM:(k + 1) * DIM]
                for k in range(SHARED // P):
                    got = []
                    for half in range(2):
                        b = s_ring.take(pe)
                        pe.wait(f.ready, sgu_ready)
                        for n, (pw, pf) in enumerate(PRODUCTS):
                            for c in range(CD):
                                m = pe.do(T.matmul, b.ap, w_up_at(pw, c, half * SHARED + k * P),
                                          f.ap[:, pf, c * HALF:(c + 1) * HALF], start=n == 0 and c == 0,
                                          stop=n == 2 and c == CD - 1, signal=n == 2 and c == CD - 1)
                        got.append((b, m))
                    (bg, mg), (bu, mu) = got
                    sl = s_silu.take(act)
                    act.wait(mg)
                    m1 = act.do(A.activation, sl.ap, bg.ap, ACT.Silu)
                    bg.free = [m1]
                    dve.wait(m1, mu)
                    m2 = dve.do(V.tensor_tensor, sl.ap, sl.ap, bu.ap, ALU.mult)
                    bu.free = [m2]
                    yield
                    sl.free = split_parts(inner.ap[:, :, k, :], sl.ap, m2)
                    inner.ready += sl.free
                f.free = [mu]
                yield
                marks = []
                for two in range(HT // 2):
                    b = s_ring.take(pe)
                    pe.wait(inner.ready, sd_ready)
                    for i in range(2):
                        t = 2 * two + i
                        for k in range(SHARED // P):
                            for n, (pi, pw) in enumerate(PRODUCTS):
                                last = n == 2 and k == SHARED // P - 1
                                m = pe.do(T.matmul, b.ap[:, i * DIM:(i + 1) * DIM],
                                          inner.ap[:, pi, k, t * P:(t + 1) * P], w_down_at(pw, k),
                                          start=k == 0 and n == 0, stop=last, signal=i == 1 and last)
                    dve.wait(m, x_ready[h])
                    for i in range(2):
                        t = HT * h + 2 * two + i
                        marks.append(dve.do(V.scalar_tensor_tensor, x[:, t, :], b.ap[:, i * DIM:(i + 1) * DIM],
                                            sgate[:, t:t + 1], x[:, t, :], ALU.mult, ALU.add))
                    b.free = [marks[-1]]
                    yield
                inner.free = [m]
                x_ready[h] = marks

            f_ring = use(bank[4:6])

            def stage_matrix(which, s, k):
                mm, pp = stage_m.take(dve), part_ring.take(act)
                own, other = taps[:, 2 * which, s, k:k + 1], taps[:, 2 * which + 1, s, k:k + 1]
                act.wait(m_ident, m_c["taps"])
                ma = act.do(A.activation, pp.ap, ident[:, :], ACT.Copy, scale=own)
                dve.wait(ma, m_c["taps"], m_c["swaps"])
                mb = dve.do(V.scalar_tensor_tensor, mm.ap, swaps[:, s, :], other, pp.ap, ALU.mult, ALU.add)
                pp.free = [mb]
                mm.ready = [mb]
                return mm

            def inside(buf, width, ready, which, stages):
                order = [(s, k) for s in stages for k in range(HB)]
                made = deque(stage_matrix(which, s, k) for s, k in order[:2])
                for n, (s, k) in enumerate(order):
                    if n + 2 < len(order):
                        made.append(stage_matrix(which, *order[n + 2]))
                    mm = made.popleft()
                    b = f_ring.take(pe)
                    pe.wait(mm.ready, ready[k])
                    mc = pe.do(T.matmul, b.ap[:, 0:width], mm.ap, buf[:, k, 0:width], start=True, stop=True)
                    mm.free = [mc]
                    act.wait(mc)
                    md = act.do(A.activation, buf[:, k, 0:width], b.ap[:, 0:width], ACT.Copy)
                    b.free = ready[k] = [md]
                    yield

            def across(src, dst, width, ready, which, s):
                new = []
                act.wait(ready, sd_ready)
                for k in range(HB):
                    o = k ^ (1 << (s - INSIDE))
                    own = taps[:, 2 * which, s, k:k + 1]
                    other = taps[:, 2 * which + 1, s, (o if which else k):(o if which else k) + 1]
                    ma = act.do(A.activation, dst[:, k, 0:width], src[:, k, 0:width], ACT.Copy, scale=own)
                    dve.wait(ma)
                    mb = dve.do(V.scalar_tensor_tensor, dst[:, k, 0:width], src[:, o, 0:width], other,
                                dst[:, k, 0:width], ALU.mult, ALU.add)
                    new.append([mb])
                ready[:] = new

            def fuse():
                ready = [[m_c["w_exp"]] for _ in range(HB)]
                yield from inside(bf_u, DIM + 1, ready, 0, range(INSIDE))
                bufs = [bf_u, bf_v]
                for s in range(INSIDE, STAGES):
                    across(bufs[0], bufs[1], DIM + 1, ready, 0, s)
                    bufs.reverse()
                    yield
                last = bufs[0]
                marks = []
                for c in range(CD):
                    for q in range(HB // 4):
                        b = f_ring.take(pe)
                        for i in range(4):
                            pe.wait(ready[4 * q + i])
                            m = pe.do(T.transpose, b.ap[:, i * P:(i + 1) * P],
                                      last[:, 4 * q + i, c * P:(c + 1) * P], ident[:, :], signal=i == 3)
                        act.wait(m)
                        m2 = act.do(A.activation, w_up[:, c, 4 * q * P:4 * (q + 1) * P], b.ap, ACT.Copy)
                        b.free = [m2]
                        marks.append(m)
                        yield
                dve.wait(ready, m_c["up_bias"])
                m = dve.do(V.tensor_tensor, hid_bias[:, :], last[:, :, DIM], up_bias[:, :], ALU.add)
                sp.wait(marks, m)
                m = dma.copy(bf_u[:, :, 0:DIM], D["w_con"])
                for _ in range(5):
                    yield
                ready = [[m] for _ in range(HB)]
                bufs = [bf_u, w_con]
                for s in reversed(range(INSIDE, STAGES)):
                    across(bufs[0], bufs[1], DIM, ready, 1, s)
                    bufs.reverse()
                    yield
                yield from inside(w_con, DIM, ready, 1, range(INSIDE - 1, -1, -1))
                dve.wait(m_c["b_con"], m_c["down_bias"])
                m = dve.do(V.tensor_tensor, b_out[:, :], b_out[:, :], down_bias[:, :], ALU.add)
                dve.wait(m)
                dve.do(V.tensor_scalar, b_out[:, :], b_out[:, :], tg[:, 3:4], None, ALU.mult)
                yield

            for h in range(HALVES):
                back.add(shared_expert(h))
            fusing = Background()
            fusing.add(fuse())

            back.step()
            hot_banks = bank[0:4]

            def one_hots(i):
                ha, hb = hot_a.take(dve, act), hot_b.take(dve)
                dve.wait(m_c["a_iota"], m_c["b_iota"], pos_ready)
                m = dve.do(V.tensor_tensor, ha.ap[:, 0, :, :, :], a_iota[:, :, :, :],
                           pos_a[:, i, :].rearrange("p (g e) -> p g e", e=EG).unsqueeze(2).to_broadcast(
                               [P, 4, NA, EG]), ALU.is_equal)
                mb = dve.do(V.tensor_tensor, hb.ap, b_iota[:, :, :],
                            pos_b[:, i, :].unsqueeze(1).to_broadcast([P, NB, EXPERTS]), ALU.is_equal)
                act.wait(m, m_c["lane_no"])
                act.do(A.activation, ha.ap[:, 1, :, :, :], ha.ap[:, 0, :, :, :], ACT.Copy,
                       scale=lane_no[:, 0:1])
                ma = act.do(A.activation, ha.ap[:, 2, :, :, :], ha.ap[:, 0, :, :, :], ACT.Copy,
                            scale=float(P * i))
                ha.ready, hb.ready = [ma], [mb]
                return ha, hb

            hots = deque([one_hots(0)])
            for i in range(TILES):
                if i + 1 < TILES:
                    hots.append(one_hots(i + 1))
                ha, hb = hots.popleft()
                pe.wait(ha.ready, hb.ready)
                for g in range(4):
                    eg = slice(EG * g, EG * g + EG)
                    if i == 0:
                        pe.wait(hot_banks[g].free)
                    for part in (1, 2):
                        m = pe.do(T.matmul, hot_banks[g].ap[:, 0:NB * EG], ha.ap[:, part, g, :, :],
                                  hb.ap[:, :, eg], start=i == 0 and part == 1,
                                  stop=i == TILES - 1 and part == 2, signal=g == 3 and part == 2)
                ha.free = hb.free = [m]
                m_hot = m
                if i % 2 and i > 4:
                    back.step()
            dve.wait(m_hot, m_c["diag"], m_c["spare_row"])
            parts = []
            for g in range(4):
                parts.append(dve.do(V.tensor_tensor, lists[:, g, :, :],
                                    hot_banks[g].ap[:, 0:NB * EG].rearrange("p (b e) -> p b e", e=EG),
                                    diag[:, :, :], ALU.mult))
                hot_banks[g].free = [parts[-1]]
            dve.wait(parts)
            m = dve.do(V.tensor_reduce, lists_b[:, :, :], lists[:, :, :, :], AX.X, ALU.add)
            sp.wait(m)
            m = dma.copy(list_dram.rearrange("g p b -> p g b"), lists_b[:, :, :])
            sp.wait(m)
            ms = [dma.copy(by_expert[EG * g:EG * g + EG, :].rearrange("e (a b) -> e a b", a=NA),
                           list_dram[g].rearrange("(a e) b -> e a b", a=NA)) for g in range(4)]
            tok_bank = bank[4]
            back.step(3)
            pe.wait(ms, tok_bank.free)
            m = pe.do(T.transpose, tok_bank.ap[:, 0:EXPERTS], by_expert[:, :], ident[0:EXPERTS, 0:EXPERTS])
            dve.wait(m)
            m1 = dve.do(V.tensor_scalar, listed[:, 0, :], tok_bank.ap[:, 0:EXPERTS], -1.0, 0.0, ALU.add, ALU.max)
            m2 = dve.do(V.tensor_scalar, listed[:, 1, :], tok_bank.ap[:, 0:EXPERTS], 0.5, None, ALU.is_lt)
            dve.wait(m1, m2)
            m_tokens = [dve.do(V.tensor_copy, tokens[:, :], listed[:, 0, :])]
            m = dve.do(V.scalar_tensor_tensor, listed[:, 2, :], listed[:, 1, :], spare_row[:, 0:1],
                       listed[:, 0, :], ALU.mult, ALU.add)
            dve.wait(m)
            m_tokens.append(dve.do(V.tensor_copy, sum_rows[:, :], listed[:, 2, :]))
            tok_bank.free = [m2]

            t_banks, h_banks, d_banks = use(bank[0:2]), use(bank[2:3]), use(bank[3:4])
            flow = {}

            def gather(e_):
                got = got_ring.take(pool)
                pool.wait(m_tokens)
                got.ready = [gdma.start(G.indirect_dma_start, got.ap, None, rows_dram,
                                        bass.IndirectOffsetOnAxis(ap=tokens[:, e_:e_ + 1], axis=0),
                                        bounds_check=TOKENS - 1, oob_is_err=False)]
                flow[e_] = {"got": got}

            def turn(e_):
                d = flow[e_]
                b = t_banks.take(pe)
                pe.wait(d["got"].ready)
                for c in range(CD):
                    m = pe.do(T.transpose, b.ap[:, c * P:(c + 1) * P], d["got"].ap[:, c * P:(c + 1) * P],
                              ident[:, :], signal=c == CD - 1)
                d["turned"] = m
                d["t"] = t = got_t.take(act)
                act.wait(m)
                m = act.do(A.activation, t.ap.rearrange("p c n -> p (c n)"), b.ap[:, 0:CD * P], ACT.Copy)
                b.free = t.ready = [m]

            def gate_up(e_):
                d = flow[e_]
                b, w, t = h_banks.take(pe), experts_w[e_], d["t"]
                pe.wait(t.ready, w.ready)
                for part in range(2):
                    for c in range(CD):
                        m = pe.do(T.matmul, b.ap[:, part * P:(part + 1) * P],
                                  w.ap[:, c, part * INNER:(part + 1) * INNER], t.ap[:, c, :],
                                  start=c == 0, stop=c == CD - 1, signal=part == 1 and c == CD - 1)
                t.free = [m]
                sl, inner = silu_ring.take(act), inner_ring.take(dve)
                act.wait(m)
                m1 = act.do(A.activation, sl.ap, b.ap[:, 0:P], ACT.Silu)
                dve.wait(m1)
                m2 = dve.do(V.tensor_tensor, inner.ap, sl.ap, b.ap[:, P:2 * P], ALU.mult)
                b.free = sl.free = inner.ready = [m2]
                d["inner"] = inner

            def down(e_):
                d = flow.pop(e_)
                b, w, inner, got = d_banks.take(pe), experts_w.pop(e_), d["inner"], d["got"]
                pe.wait(inner.ready)
                m = pe.do(T.matmul, b.ap[:, 0:DIM], inner.ap, w.ap[:, 2, :], start=True, stop=True)
                inner.free = w.free = [m]
                made = made_ring.take(dve)
                dve.wait(m, got.ready)
                m = dve.do(V.tensor_scalar, made.ap, b.ap[:, 0:DIM], got.ap[:, DIM + e_:DIM + e_ + 1],
                           None, ALU.mult)
                b.free = [m]
                got.free = [m, d["turned"]]
                pool.wait(m, m_sums[e_ % SUMS])
                m_sums[e_ % SUMS] = gdma.start(
                    G.indirect_dma_start, sum_dram[e_ % SUMS],
                    bass.IndirectOffsetOnAxis(ap=sum_rows[:, e_:e_ + 1], axis=0), made.ap, None,
                    bounds_check=TOKENS + P - 1, oob_is_err=True, compute_op=ALU.add)
                made.free = [m_sums[e_ % SUMS]]

            LAGS = ((gather, 0), (turn, 3), (gate_up, 4), (down, 5))
            for n in range(EXPERTS + LAGS[-1][1]):
                for (work, lag), other in zip(reversed(LAGS), (fusing, back, fusing, None)):
                    if 0 <= n - lag < EXPERTS:
                        work(n - lag)
                    if other and (other is fusing or n % 8):
                        other.step()
                if n + 3 < EXPERTS:
                    load_expert(n + 3)
            back.drain()
            fusing.drain()
        barrier()

        ROWS1 = STACK + 4
        scope = ExitStack()
        with scope:
            s2 = lambda n, s, d: sb(n, s, d, scope)
            k_raw = Slot(s2("k1_raw", [ROWS1, NK, P], F32)[:, :, :])
            keys_ring = Ring([s2(f"k1_stack{i}", [P, NK, P], F32R)[:, :, :] for i in range(2)])
            vals_ring = Ring([s2(f"values1_{i}", [P, 2, HEADS, 32], F32)[:, :, :, :] for i in range(2)])
            q_stacks = Ring([s2(f"q1_stack{i}", [P, PAIRS, HALF], F32R)[:, :, :] for i in range(3)])
            q_stage = Ring([s2("q1_stage", [P, 2, CD, HALF], F32R)[:, :, :, :]])
            weights = Ring([s2(f"weights1_{i}", [P, HALF], F32)[:, :] for i in range(8)])
            turned_ring = Ring([s2("turned1_0", [P, GROUPS, HALF], F32)[:, :, :]])
            normed = Ring([s2("normed1", [P, HT, DIM], F32)[:, :, :]])
            att = Ring([s2("att1", [P, HT, DIM], F32)[:, :, :]])
            sums = Ring([s2(f"sums1_{i}", [P, HEADS], F32)[:, :] for i in range(2)])
            fetched = Ring([s2(f"fetched{i}", [P, SUMS, HT, DIM], F32)[:, :, :, :] for i in range(2)])
            peaks = Ring([s2(f"peaks{i}", [P, HT, HEADS], F32)[:, :, :] for i in range(2)])
            peak_t = Ring([s2(f"peak_t{i}", [HEADS, 2, HALF], F32R)[:, :, :] for i in range(2)])
            clear_values(vals_ring)
            s_banks, misc, o_bank = use(bank[0:3]), use(bank[6:8]), bank[5]
            peak_banks = use(bank[3:5])
            keys_of, vals_of, stack_of, fetched_of = {}, {}, {}, {}

            def fetch_experts(h):
                f = fetched.take(sp)
                sp.wait(m_sums)
                f.ready = [dma.copy(f.ap[:, i, :, :], sum_dram[i][HALF * h:HALF * (h + 1), :].rearrange(
                    "(t p) f -> p t f", p=P)) for i in range(SUMS)]
                fetched_of[h] = f

            def add_experts(h):
                f = fetched_of.pop(h)
                xs = x[:, HT * h:HT * (h + 1), :]
                for i in range(SUMS):
                    lane, add = (dve, V.tensor_tensor) if h == 0 else (pool, G.tensor_tensor)
                    lane.wait(f.ready[i], x_ready[h])
                    x_ready[h] = [lane.do(add, xs, xs, f.ap[:, i, :, :], ALU.add)]
                    yield
                f.free = x_ready[h]

            def load_keys1(b):
                sp.wait(k_raw.free)
                k_raw.ready, k_raw.free = [dma.copy(k_raw.ap, D["k1"][b])], None
                values = vals_ring.take(sp)
                src = D["ctx"][b]
                values.ready = [dma.copy(values.ap[:, 0, :, 0:HD], src[0:P].rearrange("k (h d) -> k h d", d=HD))]
                rest = src[P:KEYS].rearrange("k (g j d) -> k g j d", j=4, d=HD)
                for j in range(4):
                    values.ready.append(dma.copy(values.ap[32 * j:32 * j + REST, 1, j::4, 0:HD], rest[:, :, j, :]))
                vals_of[b] = values

            def prepare_keys1(b):
                k_stack = keys_ring.take(act, dve)
                yield from split_keys(k_raw, k_stack, ROWS1, 1.0)
                keys_of[b] = k_stack

            def prepare_queries1(h):
                n = normed.take(dve)
                yield from layernorm(h, n.ap, n)
                stage = q_stage.take(act, dve)
                for c, b in enumerate(turn_half(n.ap, n.ready, misc)):
                    act.wait(b.ready)
                    m1 = act.do(A.activation, stage.ap[:, 0, c, :], b.ap, ACT.Copy)
                    dve.wait(m1)
                    m2 = dve.do(V.tensor_tensor, stage.ap[:, 1, c, :], b.ap,
                                stage.ap[:, 0, c, :].bitcast(F32), ALU.subtract)
                    b.free = [m2]
                    stage.ready += [m1, m2]
                    n.free = list(b.ready)
                yield
                stack = q_stacks.take(sp)
                send_stack(stage, stack)
                stack_of[h] = stack
                yield

            def find_peaks(h):
                stack, keys = stack_of[h], keys_of[h // 2]
                peak = peaks.take(dve)
                for t in range(HT):
                    for two in range(PAIRS // 2):
                        pe.wait(keys.ready, stack.ready)
                        got = []
                        for i in range(2):
                            p = 2 * two + i
                            b = peak_banks.take(pe)
                            q = stack.ap[0:STACK, p, t * P:(t + 1) * P]
                            view = b.ap[:, 0:2 * KEYS].rearrange("p (a k) -> p a k", a=2)
                            pe.do(T.matmul, view[:, :, 0:P], q, keys.ap[0:STACK, 2 * p:2 * p + 2, :],
                                  start=True, stop=True, signal=False)
                            rest = keys.ap[0:STACK, HEADS + p, :].rearrange("p (j k) -> p j k", k=32)
                            got.append((p, b, view, pe.do(
                                T.matmul, view[:, :, P:KEYS], q, rest[:, 2 * i:2 * i + 2, 0:REST],
                                start=True, stop=True)))
                        for p, b, view, m in got:
                            dve.wait(m)
                            m = dve.do(V.tensor_reduce, peak.ap[:, t, 2 * p:2 * p + 2], view, AX.X, ALU.max)
                            b.free = [m]
                        yield
                b = misc.take(pe)
                pe.wait(m)
                for t in range(HT):
                    m = pe.do(T.transpose, b.ap[0:HEADS, t * P:(t + 1) * P], peak.ap[:, t, :], ident[:, :],
                              signal=t == HT - 1)
                peak.free = [m]
                pt = peak_t.take(act, dve)
                act.wait(m)
                m1 = act.do(A.activation, pt.ap[:, 0, :], b.ap[0:HEADS, :], ACT.Copy, scale=-1.0)
                dve.wait(m1)
                m2 = dve.do(V.scalar_tensor_tensor, pt.ap[:, 1, :], b.ap[0:HEADS, :], -1.0,
                            pt.ap[:, 0, :].bitcast(F32), ALU.mult, ALU.subtract)
                b.free = [m2]
                sp.wait(m2)
                m = dma.copy(max_dram[h].rearrange("r h n -> h r n"), pt.ap.bitcast(F32))
                pt.free = [m]
                sp.wait(m)
                for r in range(2):
                    row = STACK + 2 * r
                    stack.ready.append(dma.copy(stack.ap[row:row + 2, :, :].bitcast(F32),
                                                max_dram[h, r].rearrange("(p a) n -> a p n", a=2)))
                yield

            def after_attention1(h, turned):
                a = att.take(dve)
                for t in range(HT):
                    m, m3 = normalize_heads(t, turned, misc, sums, a.ap[:, t, :])
                    a.ready.append(m3)
                    yield
                turned.free = [m]
                marks = []
                for t in range(HT):
                    xs = x[:, HT * h + t, :]
                    dve.wait(a.ready[t], x_ready[h])
                    marks.append(dve.do(V.scalar_tensor_tensor, xs, a.ap[:, t, :], tg[:, 2:3], xs,
                                        ALU.mult, ALU.add))
                a.free = marks[-1:]
                x_ready[h] = marks
                yield

            needed = {}
            early, peaking, late = Background(), Background(), Background()
            fetch_experts(0)
            load_keys1(0)
            early.add(prepare_keys1(0))
            fetch_experts(1)
            peaking.add(add_experts(0))
            peaking.add(prepare_queries1(0))
            peaking.step(4)
            while early.work or peaking.work:
                peaking.step()
                early.step()
            load_keys1(1)
            peaking.add(find_peaks(0))
            early.add(add_experts(1))
            early.add(prepare_queries1(1))
            while peaking.work:
                peaking.step(2)
                early.step()
            early.drain()
            needed[1] = [early.add(prepare_keys1(1))]
            turned_of, chunks_of, later = {}, {}, {}

            def start_scores(n):
                h, g, j = units[n]
                if (g, j) == (0, 0):
                    peaking.drain()
                    for work in needed.pop(h, []):
                        early.finish(work)
                    if h + 1 < HALVES:
                        peaking.add(find_peaks(h + 1))
                    if h + 2 < HALVES:
                        fetch_experts(h + 2)
                        early.add(add_experts(h + 2))
                        needed.setdefault(h + 1, []).append(early.add(prepare_queries1(h + 2)))
                    if h % 2 == 0 and 2 <= h < HALVES - 2:
                        needed[h + 1].append(early.add(prepare_keys1(h // 2 + 1)))
                stack, keys = stack_of[h], keys_of[h // 2]
                b = s_banks.take(pe)
                key_scores(j, ROWS1, b, keys, stack, g)
                if (g, j) == (GROUPS - 1, 4):
                    stack.free = list(b.ready)
                    if h % 2 == 1:
                        keys.free = list(b.ready)
                return b

            def weigh(n, part):
                h, g, _ = units[n]
                m = weigh_values(g, part, chunks_of[h, g], vals_of[h // 2], o_bank)
                if part == 0:
                    return
                if g == 0:
                    turned_of[h] = turned_ring.take(act)
                keep_weighted(g, m, o_bank, turned_of[h])
                if g == GROUPS - 1:
                    if h % 2 == 1:
                        vals_of[h // 2].free = [m]
                    late.add(after_attention1(h, turned_of[h]))

            b = start_scores(0)
            for n in range(len(units) + 2):
                if n < len(units):
                    h, g, j = units[n]
                    w = weights.take(act)
                    act.wait(b.ready)
                    w.ready = [act.do(A.activation, w.ap, b.ap, ACT.Exp)]
                    b.free = list(w.ready)
                    chunks_of.setdefault((h, g), []).append(w)
                    if j == 4:
                        later[n], later[n + 1] = (n, 0), (n, 1)
                if n + 1 < len(units):
                    b = start_scores(n + 1)
                if n in later:
                    weigh(*later.pop(n))
                if n % 40 == 3 and 40 <= n < len(units) - 40:
                    load_keys1(n // 40 + 1)
                early.step()
                peaking.step(PEAK_STEPS[n % len(PEAK_STEPS)])
                late.step()
            late.drain()
        barrier()

        scope = ExitStack()
        with scope:
            s3 = lambda n, s, d: sb(n, s, d, scope)
            normed = Ring([s3(f"normed2_{i}", [P, HT, DIM], F32)[:, :, :] for i in range(2)])
            feats = Ring([s3(f"feats3_{i}", [P, 2, CD, HALF], F32R)[:, :, :, :] for i in range(2)])
            hidden = Ring([s3(f"hidden{i}", [P, 2, HB, HALF], F32R)[:, :, :, :] for i in range(2)])
            whole = Ring([s3(f"hidden_whole{i}", [P, HALF], F32)[:, :] for i in range(3)])
            up_parts = s3("w_up_parts", [P, 2, CD, HID], F32R)
            con_parts = s3("w_con_parts", [P, 2, HB, DIM], F32R)
            up_banks, down_banks, misc = use(bank[0:4]), use(bank[4:6]), use(bank[6:8])
            feats_of, up_ready, con_ready = {}, [[] for _ in range(HB)], []

            def prepare_weights():
                for q in range(0, HB, 2):
                    cols = slice(q * P, (q + 2) * P)
                    m = act.do(A.activation, up_parts[:, 0, :, cols], w_up[:, :, cols], ACT.Copy)
                    dve.wait(m)
                    m2 = dve.do(V.tensor_tensor, up_parts[:, 1, :, cols], w_up[:, :, cols],
                                up_parts[:, 0, :, cols].bitcast(F32), ALU.subtract)
                    up_ready[q] = up_ready[q + 1] = [m, m2]
                    yield
                for q in range(0, HB, 4):
                    rows_ = slice(q, q + 4)
                    m = act.do(A.activation, con_parts[:, 0, rows_, :], w_con[:, rows_, :], ACT.Copy)
                    dve.wait(m)
                    con_ready.extend([m, dve.do(V.tensor_tensor, con_parts[:, 1, rows_, :],
                                                w_con[:, rows_, :],
                                                con_parts[:, 0, rows_, :].bitcast(F32), ALU.subtract)])
                    yield

            def prepare_ffn(h):
                n = normed.take(dve)
                yield from layernorm(h, n.ap, n)
                pool.wait(n.ready[-1])
                x_ready[h] = [pool.do(G.tensor_tensor, x[:, HT * h:HT * h + HT, :],
                                      x[:, HT * h:HT * h + HT, :],
                                      b_out[:, :].unsqueeze(1).to_broadcast([P, HT, DIM]), ALU.add)]
                f = feats.take(act, dve)
                for c, b in enumerate(turn_half(n.ap, n.ready, misc)):
                    act.wait(b.ready)
                    m = act.do(A.activation, f.ap[:, 0, c, :], b.ap, ACT.Copy)
                    dve.wait(m)
                    m2 = dve.do(V.tensor_tensor, f.ap[:, 1, c, :], b.ap, f.ap[:, 0, c, :].bitcast(F32),
                                ALU.subtract)
                    f.ready += [m, m2]
                    b.free = [m2]
                    n.free = list(b.ready)
                feats_of[h] = f
                yield

            def up(h, k, hid):
                f = feats_of[h]
                b = up_banks.take(pe)
                pe.wait(f.ready, up_ready[k])
                for i, (pw, pf) in enumerate(PRODUCTS):
                    for c in range(CD):
                        m = pe.do(T.matmul, b.ap, up_parts[:, pw, c, k * P:(k + 1) * P],
                                  f.ap[:, pf, c, :], start=i == 0 and c == 0,
                                  stop=i == 2 and c == CD - 1, signal=i == 2 and c == CD - 1)
                if k == HB - 1:
                    f.free = [m]
                wh = whole.take(act)
                act.wait(m)
                m = act.do(A.activation, wh.ap, b.ap, ACT.Gelu, bias=hid_bias[:, k:k + 1])
                b.free = [m]
                dve.wait(m)
                m1 = dve.do(V.tensor_copy, hid.ap[:, 0, k, :], wh.ap)
                dve.wait(m1)
                m2 = dve.do(V.tensor_tensor, hid.ap[:, 1, k, :], wh.ap, hid.ap[:, 0, k, :].bitcast(F32),
                            ALU.subtract)
                wh.free = [m2]
                hid.ready.append(m2)

            def down(h, two, hid):
                b = down_banks.take(pe)
                for i in range(2):
                    t = 2 * two + i
                    for k in range(HB):
                        pe.wait(hid.ready[k], con_ready)
                        for n, (ph, pw) in enumerate(PRODUCTS):
                            m = pe.do(T.matmul, b.ap[:, i * DIM:(i + 1) * DIM],
                                      hid.ap[:, ph, k, t * P:(t + 1) * P], con_parts[:, pw, k, :],
                                      start=k == 0 and n == 0, stop=k == HB - 1 and n == 2,
                                      signal=i == 1 and k == HB - 1 and n == 2)
                dve.wait(m, x_ready[h])
                tiles = slice(HT * h + 2 * two, HT * h + 2 * two + 2)
                xs = x[:, tiles, :].rearrange("p i f -> p (i f)")
                m2 = dve.do(V.scalar_tensor_tensor, xs, b.ap, tg[:, 3:4], xs, ALU.mult, ALU.add)
                b.free = [m2]
                sp.wait(m2)
                dma.copy(out_view[:, tiles, :], x[:, tiles, :])
                return m

            early = Background()
            early.add(prepare_weights())
            early.step()
            late = Background()
            late.add(prepare_ffn(0))
            late.drain()
            early.drain()
            before = None
            for h in range(HALVES):
                hid = hidden.take(dve)
                if h + 1 < HALVES:
                    early.add(prepare_ffn(h + 1))
                for k in range(HB):
                    up(h, k, hid)
                    early.step()
                    if before and k in (2, 5):
                        m = down(h - 1, k // 3, before)
                        if k == 5:
                            before.free = [m]
                early.drain()
                before = hid
            for two in range(HT // 2):
                down(HALVES - 1, two, before)

        barrier()
        block = ctx.enter_context(nc.Block())

        @block.tensor
        def _(_):
            pe.run()

        @block.scalar
        def _(_):
            act.run()

        @block.vector
        def _(_):
            dve.run()

        @block.gpsimd
        def _(_):
            pool.run()

        @block.sync
        def _(_):
            sp.run()


def constants():
    bf = mybir.dt.np(BF16)
    rows, cols = np.arange(P)[:, None], np.arange(P)[None, :]
    return {
        "ident": np.eye(P, dtype=np.float32),
        "upper": (rows < cols).astype(bf),
        "a_iota": np.broadcast_to(np.arange(NA)[:, None], (P, 4, NA, EG)).astype(bf),
        "b_iota": np.broadcast_to(np.arange(NB)[:, None], (P, NB, EXPERTS)).astype(bf),
        "lane_no": np.arange(1, P + 1, dtype=np.float32)[:, None].copy(),
        "spare_row": np.arange(TOKENS, TOKENS + P, dtype=np.float32)[:, None].copy(),
        "diag": np.broadcast_to((np.arange(P)[:, None] % EG == np.arange(EG)[None, :])[:, None, :],
                                (P, NB, EG)).astype(np.float32),
        "swaps": np.stack([rows ^ (1 << s) == cols for s in range(INSIDE)], 1).astype(np.float32),
    }


def feature_rows(w):
    return np.ascontiguousarray(w.reshape(-1, P, w.shape[1]).transpose(1, 0, 2))


def on_all(v):
    return np.ascontiguousarray(np.broadcast_to(v, (P, v.shape[0])))


def stacked(by_head, rows_aug):
    n = by_head.shape[1]
    s = np.zeros((STACK + rows_aug, HEADS, n), by_head.dtype)
    for h in range(HEADS):
        for block in range(3):
            r = 32 * block + HD * (h % 2)
            s[r:r + HD, h] = by_head[HD * h:HD * (h + 1)]
    return s


def key_stacks(keys):
    s = stacked(keys.T, 4)
    for h in range(HEADS):
        s[STACK + h % 2, h] = s[STACK + 2 + h % 2, h] = 1.0
    out = np.zeros((STACK + 4, NK, P), keys.dtype)
    out[:, :HEADS] = s[:, :, :P]
    for h in range(HEADS):
        out[:, HEADS + h // 2, 32 * (h % 4):32 * (h % 4) + REST] = s[:, h, P:]
    return out


def tap_rows(w):
    own, other = np.empty((STAGES, HID), w.dtype), np.empty((STAGES, HID), w.dtype)
    for s in range(STAGES):
        st = 1 << s
        v = w[s].reshape(HID // (2 * st), st, 2, 2)
        o, p = own[s].reshape(-1, 2, st), other[s].reshape(-1, 2, st)
        for r in range(2):
            o[:, r], p[:, r] = v[:, :, r, r], v[:, :, r, 1 - r]
    return own, other


def laid_out(i):
    ctx = i["ctx_1024"]
    d = constants()
    d["x"] = i["x"].reshape(TOKENS, DIM)
    d["gates"] = np.ascontiguousarray(np.broadcast_to(
        np.stack([i["g_xattn"][0], i["g_ffn"][0], i["g_xattn"][1], i["g_ffn"][1]]), (P, 4)))
    for n in "qvo":
        d[f"w{n}"] = feature_rows(i[f"L0_xattn_W{n}"].T)
    d["wk"] = stacked(i["L0_xattn_Wk"], 0).reshape(STACK, GROUPS, 4, CD, P).transpose(1, 4, 3, 2, 0)
    d["bk"] = np.ascontiguousarray(stacked(i["L0_xattn_bk"][:, None], 0)[:, :, 0])
    d["bq"] = np.ascontiguousarray(i["L0_xattn_bq"].reshape(CD, P).T)
    d["bv"], d["bo"] = on_all(i["L0_xattn_bv"]), on_all(i["L0_xattn_bo"])
    d["gate_w"] = feature_rows(np.concatenate([i["L0_ffn_gate_w"], i["L0_ffn_shared_gate_w"]], 1))
    keys = np.zeros((BATCH, DIM, 3 * P), ctx.dtype)
    keys[:, :, :KEYS] = ctx.transpose(0, 2, 1)
    for j in range(4):
        keys[:, :, 2 * P + 32 * j:2 * P + 32 * j + REST] = ctx[:, P:].transpose(0, 2, 1)
    d["ctx_t"] = np.stack([feature_rows(k) for k in keys])
    d["ctx"] = ctx
    d["k1"] = np.stack([key_stacks(ctx[b]) for b in range(BATCH)])
    gu, dn = i["L0_ffn_expert_gate_up_w"], i["L0_ffn_expert_down_w"]
    d["expert_w"] = np.ascontiguousarray(np.concatenate(
        [gu.reshape(EXPERTS, CD, P, 2 * INNER).transpose(0, 2, 1, 3), dn[:, :, None, :]], 2))
    d["w_sgu"] = feature_rows(i["L0_ffn_shared_gate_up_w"]).reshape(P, -1)
    d["w_sd"] = feature_rows(i["L0_ffn_shared_down_w"]).reshape(P, -1)
    d["w_exp"] = feature_rows(np.concatenate([i["L1_ffn_W_exp"].T, i["L1_ffn_b_exp"][:, None]], 1))
    d["w_con"] = feature_rows(i["L1_ffn_W_con"])
    taps = np.empty((4, STAGES, HID), i["L1_ffn_up_weights"].dtype)
    taps[0], taps[1] = tap_rows(i["L1_ffn_up_weights"])
    taps[2], taps[3] = tap_rows(i["L1_ffn_down_weights"])
    at = np.arange(HID)
    for s in range(INSIDE):
        taps[1, s] = taps[1, s][at ^ (1 << s)]
    d["taps"] = np.ascontiguousarray(taps.reshape(4, STAGES, HB, P).transpose(3, 0, 1, 2))
    d["up_bias"] = np.ascontiguousarray(i["L1_ffn_up_bias"].reshape(HB, P).T)
    d["b_con"], d["down_bias"] = on_all(i["L1_ffn_b_con"]), on_all(i["L1_ffn_down_bias"])
    return d


def kernel(**inputs):
    import concourse.bacc as bacc
    from concourse.bass_utils import run_bass_kernel_spmd

    nc = bacc.Bacc("TRN2", target_bir_lowering=False, num_devices=1)
    host = {n: np.asarray(a) for n, a in inputs.items()}
    arrays, aps = {}, {}
    for name, a in laid_out(host).items():
        arrays[f"in_{name}"] = np.ascontiguousarray(a)
        aps[name] = nc.dram_tensor(f"in_{name}", a.shape, mybir.dt.from_np(a.dtype), kind="ExternalInput").ap()
    out = nc.dram_tensor("out", (TOKENS, DIM), F32, kind="ExternalOutput").ap()
    build(nc, aps, out)
    result = run_bass_kernel_spmd(nc, [arrays], core_ids=[0])
    return result.results[0]["out"].reshape(BATCH, SEQ, DIM)
```
